# Optimizing a Trainium2 kernel written in Bass

```python
import numpy as np
import jax
import jax.numpy as jnp

def _softmax(x, axis=-1):
    return jax.nn.softmax(x, axis=axis)

def _gelu(x):
    return jax.nn.gelu(x, approximate=True)

def _silu(x):
    return jax.nn.silu(x)

def _sigmoid(x):
    return jax.nn.sigmoid(x)

def _layernorm(x, axis=-1, eps=1e-05):
    m = jnp.mean(x, axis=axis, keepdims=True)
    v = jnp.var(x, axis=axis, keepdims=True)
    return (x - m) / jnp.sqrt(v + eps)

def _scatter_add(tgt, idx, src, axis=0):
    return tgt.at[idx].add(src)

def _segment_sum(src, seg, n):
    return jax.ops.segment_sum(src, seg, n)
kernel_name = 'mk_flamingo_gated_d1_seqx_r4_47a221'

def setup_inputs(seed: int=0):
    np.random.seed(seed)
    _w = jnp.asarray

    def _rec_inputs():
        import jax
        import jax.numpy as jnp
        _rk = jax.random.key(seed)
        x = -0.0002928 + 1 * jax.random.normal(jax.random.fold_in(_rk, 1), (8, 512, 256), jnp.float32)
        _lenS = 512 - jax.random.randint(jax.random.fold_in(_rk, 7), (8,), 0, max(1, 512 // 4) + 1, jnp.int32)
        _lenS2 = 512 - jax.random.randint(jax.random.fold_in(_rk, 8), (8,), 0, max(1, 512 // 4) + 1, jnp.int32)
        _ctx_1024P = jax.random.normal(jax.random.fold_in(_rk, 11), (8, 16, 256), jnp.float32)
        _ctx_1024c = jax.random.dirichlet(jax.random.fold_in(_rk, 511), 0.3 * jnp.ones((16,), jnp.float32), (8, 512))
        _ctx_1024t = jnp.einsum('bsk,bkd->bsd', _ctx_1024c, _ctx_1024P)
        _ctx_1024t = _ctx_1024t * jax.lax.rsqrt(jnp.mean(jnp.square(_ctx_1024t)) + 1e-12) * 0.953939
        ctx_1024 = 4.13588e-05 + 0.999923 * (_ctx_1024t + 0.3 * jax.random.normal(jax.random.fold_in(_rk, 611), (8, 512, 256), jnp.float32))
        _validS = jnp.arange(512)[None, :] < _lenS[:, None]
        _validS2 = jnp.arange(512)[None, :] < _lenS2[:, None]
        _causal = jnp.tril(jnp.ones((512, 512), dtype=bool))
        mask_Bx1x1xS2_ff0 = jnp.where(jnp.ones((8, 1, 1, 512), dtype=bool), 0.0, -1000000000.0).astype(jnp.float32)
        _g = jax.random.normal(jax.random.fold_in(_rk, 9001), (2, 1), jnp.float32)
        _g = jnp.sign(_g) * jnp.maximum(jnp.abs(_g), 1.0) + (_g == 0) * 1.0
        g_xattn = _g[0]
        g_ffn = _g[1]
        return (x, ctx_1024, mask_Bx1x1xS2_ff0, g_xattn, g_ffn)
    x, ctx_1024, mask_Bx1x1xS2_ff0, g_xattn, g_ffn = _rec_inputs()

    def _L0_xattn_setup():
        import jax, jax.numpy as jnp
        import numpy as np
        H = 16
        D = 256
        F = 1024
        LN_EPS = 1e-05

        def _glorot(key, shape):
            fan_in, fan_out = (shape[0], shape[1])
            lim = np.sqrt(6.0 / (fan_in + fan_out))
            return jax.random.uniform(key, shape, jnp.float32, -lim, lim)

        def _split_heads(x):
            b, l, _ = x.shape
            return x.reshape(b, l, H, D // H)

        def _mha(x, ctx, mask, qw, qb, kw, kb, vw, vb):
            q = _split_heads(x @ qw + qb)
            k = _split_heads(ctx @ kw + kb)
            v = _split_heads(ctx @ vw + vb)
            scores = jnp.einsum('bqhd,bkhd->bhqk', q, k) / np.sqrt(D // H).astype(np.float32)
            if mask is not None:
                scores = scores + mask
            probs = jax.nn.softmax(scores, axis=-1)
            out = jnp.einsum('bhqk,bkhd->bqhd', probs, v)
            return out.reshape(x.shape[0], x.shape[1], D)

        def _self_output(h, residual, w, b, g, be):
            h = h @ w + b
            h = h + residual
            mu = jnp.mean(h, axis=-1, keepdims=True)
            var = jnp.mean(jnp.square(h - mu), axis=-1, keepdims=True)
            return (h - mu) * jax.lax.rsqrt(var + LN_EPS) * g + be
        key = jax.random.key(seed)
        ks = jax.random.split(key, 16)
        inp = {'input_tensor': jax.random.normal(ks[0], (4, 256, D), jnp.float32), 'ctx_tensor': jax.random.normal(ks[1], (4, 512, D), jnp.float32), 'ctx_attn_mask': jnp.zeros((4, 1, 1, 512), jnp.float32), 'cq_w': _glorot(ks[2], (D, D)), 'cq_b': jnp.zeros((D,)), 'ck_w': _glorot(ks[3], (D, D)), 'ck_b': jnp.zeros((D,)), 'cv_w': _glorot(ks[4], (D, D)), 'cv_b': jnp.zeros((D,)), 'co_w': _glorot(ks[5], (D, D)), 'co_b': jnp.zeros((D,)), 'co_g': jnp.ones((D,)), 'co_be': jnp.zeros((D,)), 'sq_w': _glorot(ks[6], (D, D)), 'sq_b': jnp.zeros((D,)), 'sk_w': _glorot(ks[7], (D, D)), 'sk_b': jnp.zeros((D,)), 'sv_w': _glorot(ks[8], (D, D)), 'sv_b': jnp.zeros((D,)), 'so_w': _glorot(ks[9], (D, D)), 'so_b': jnp.zeros((D,)), 'so_g': jnp.ones((D,)), 'so_be': jnp.zeros((D,)), 'fi_w': _glorot(ks[10], (D, F)), 'fi_b': jnp.zeros((F,)), 'fo_w': _glorot(ks[11], (F, D)), 'fo_b': jnp.zeros((D,)), 'fo_g': jnp.ones((D,)), 'fo_be': jnp.zeros((D,))}
        return inp
    _L0_xattn_all = _L0_xattn_setup()
    _L0_xattn_in = {k: v for k, v in _L0_xattn_all.items() if k in ('cq_w', 'cq_b', 'ck_w', 'ck_b', 'cv_w', 'cv_b', 'co_w', 'co_b', 'co_g', 'co_be', 'sq_w', 'sq_b', 'sk_w', 'sk_b', 'sv_w', 'sv_b', 'so_w', 'so_b', 'so_g', 'so_be', 'fi_w', 'fi_b', 'fo_w', 'fo_b', 'fo_g', 'fo_be')}
    del _L0_xattn_all

    def _L0_ffn_setup():
        import jax, jax.numpy as jnp
        import numpy as np
        EPS = 1e-06
        TOP_K = 2
        key = jax.random.key(seed)
        k0, k1, k2, k3, k4 = jax.random.split(key, 5)
        B, S, H, I, E = (1, 512, 256, 896, 8)
        return {'hidden_states': jax.random.normal(k0, (B, S, H), jnp.float32), 'rms_weight': jnp.ones((H,), jnp.float32), 'gate_w': jax.random.normal(k1, (E, H), jnp.float32) * H ** (-0.5), 'w1': jax.random.normal(k2, (E, I, H), jnp.float32) * H ** (-0.5), 'w2': jax.random.normal(k3, (E, H, I), jnp.float32) * I ** (-0.5), 'w3': jax.random.normal(k4, (E, I, H), jnp.float32) * H ** (-0.5)}
    _L0_ffn_all = _L0_ffn_setup()
    _L0_ffn_in = {k: v for k, v in _L0_ffn_all.items() if k in ('rms_weight', 'gate_w', 'w1', 'w2', 'w3')}
    del _L0_ffn_all
    return {'x': x, 'ctx_1024': ctx_1024, 'mask_Bx1x1xS2_ff0': mask_Bx1x1xS2_ff0, 'g_xattn': g_xattn, 'g_ffn': g_ffn, 'L0_xattn_cq_w': _L0_xattn_in['cq_w'], 'L0_xattn_cq_b': _L0_xattn_in['cq_b'], 'L0_xattn_ck_w': _L0_xattn_in['ck_w'], 'L0_xattn_ck_b': _L0_xattn_in['ck_b'], 'L0_xattn_cv_w': _L0_xattn_in['cv_w'], 'L0_xattn_cv_b': _L0_xattn_in['cv_b'], 'L0_xattn_co_w': _L0_xattn_in['co_w'], 'L0_xattn_co_b': _L0_xattn_in['co_b'], 'L0_xattn_co_g': _L0_xattn_in['co_g'], 'L0_xattn_co_be': _L0_xattn_in['co_be'], 'L0_xattn_sq_w': _L0_xattn_in['sq_w'], 'L0_xattn_sq_b': _L0_xattn_in['sq_b'], 'L0_xattn_sk_w': _L0_xattn_in['sk_w'], 'L0_xattn_sk_b': _L0_xattn_in['sk_b'], 'L0_xattn_sv_w': _L0_xattn_in['sv_w'], 'L0_xattn_sv_b': _L0_xattn_in['sv_b'], 'L0_xattn_so_w': _L0_xattn_in['so_w'], 'L0_xattn_so_b': _L0_xattn_in['so_b'], 'L0_xattn_so_g': _L0_xattn_in['so_g'], 'L0_xattn_so_be': _L0_xattn_in['so_be'], 'L0_xattn_fi_w': _L0_xattn_in['fi_w'], 'L0_xattn_fi_b': _L0_xattn_in['fi_b'], 'L0_xattn_fo_w': _L0_xattn_in['fo_w'], 'L0_xattn_fo_b': _L0_xattn_in['fo_b'], 'L0_xattn_fo_g': _L0_xattn_in['fo_g'], 'L0_xattn_fo_be': _L0_xattn_in['fo_be'], 'L0_ffn_rms_weight': _L0_ffn_in['rms_weight'], 'L0_ffn_gate_w': _L0_ffn_in['gate_w'], 'L0_ffn_w1': _L0_ffn_in['w1'], 'L0_ffn_w2': _L0_ffn_in['w2'], 'L0_ffn_w3': _L0_ffn_in['w3']}

def reference(x, ctx_1024, mask_Bx1x1xS2_ff0, g_xattn, g_ffn, L0_xattn_cq_w, L0_xattn_cq_b, L0_xattn_ck_w, L0_xattn_ck_b, L0_xattn_cv_w, L0_xattn_cv_b, L0_xattn_co_w, L0_xattn_co_b, L0_xattn_co_g, L0_xattn_co_be, L0_xattn_sq_w, L0_xattn_sq_b, L0_xattn_sk_w, L0_xattn_sk_b, L0_xattn_sv_w, L0_xattn_sv_b, L0_xattn_so_w, L0_xattn_so_b, L0_xattn_so_g, L0_xattn_so_be, L0_xattn_fi_w, L0_xattn_fi_b, L0_xattn_fo_w, L0_xattn_fo_b, L0_xattn_fo_g, L0_xattn_fo_be, L0_ffn_rms_weight, L0_ffn_gate_w, L0_ffn_w1, L0_ffn_w2, L0_ffn_w3):
    import jax
    import jax.numpy as jnp

    def _L0_xattn_ref(input_tensor, ctx_tensor, ctx_attn_mask, cq_w, cq_b, ck_w, ck_b, cv_w, cv_b, co_w, co_b, co_g, co_be, sq_w, sq_b, sk_w, sk_b, sv_w, sv_b, so_w, so_b, so_g, so_be, fi_w, fi_b, fo_w, fo_b, fo_g, fo_be):
        import jax, jax.numpy as jnp
        import numpy as np
        H = 16
        D = 256
        F = 1024
        LN_EPS = 1e-05

        def _glorot(key, shape):
            fan_in, fan_out = (shape[0], shape[1])
            lim = np.sqrt(6.0 / (fan_in + fan_out))
            return jax.random.uniform(key, shape, jnp.float32, -lim, lim)

        def _split_heads(x):
            b, l, _ = x.shape
            return x.reshape(b, l, H, D // H)

        def _mha(x, ctx, mask, qw, qb, kw, kb, vw, vb):
            q = _split_heads(x @ qw + qb)
            k = _split_heads(ctx @ kw + kb)
            v = _split_heads(ctx @ vw + vb)
            scores = jnp.einsum('bqhd,bkhd->bhqk', q, k) / np.sqrt(D // H).astype(np.float32)
            if mask is not None:
                scores = scores + mask
            probs = jax.nn.softmax(scores, axis=-1)
            out = jnp.einsum('bhqk,bkhd->bqhd', probs, v)
            return out.reshape(x.shape[0], x.shape[1], D)

        def _self_output(h, residual, w, b, g, be):
            h = h @ w + b
            h = h + residual
            mu = jnp.mean(h, axis=-1, keepdims=True)
            var = jnp.mean(jnp.square(h - mu), axis=-1, keepdims=True)
            return (h - mu) * jax.lax.rsqrt(var + LN_EPS) * g + be
        ca = _mha(input_tensor, ctx_tensor, ctx_attn_mask, cq_w, cq_b, ck_w, ck_b, cv_w, cv_b)
        x = _self_output(ca, input_tensor, co_w, co_b, co_g, co_be)
        sa = _mha(x, x, None, sq_w, sq_b, sk_w, sk_b, sv_w, sv_b)
        x = _self_output(sa, x, so_w, so_b, so_g, so_be)
        inter = jax.nn.gelu(x @ fi_w + fi_b, approximate=False)
        x = _self_output(inter, x, fo_w, fo_b, fo_g, fo_be)
        return x

    def _L0_ffn_ref(hidden_states, rms_weight, gate_w, w1, w2, w3):
        import jax, jax.numpy as jnp
        import numpy as np
        EPS = 1e-06
        TOP_K = 2
        B, S, H = hidden_states.shape
        E = gate_w.shape[0]
        x = hidden_states.astype(jnp.float32)
        var = jnp.mean(x * x, axis=-1, keepdims=True)
        h = rms_weight * (x * jax.lax.rsqrt(var + EPS))
        logits = jnp.einsum('bsh,eh->bse', h, gate_w)
        scores = jax.nn.softmax(logits.astype(jnp.float32), axis=-1)
        top_w, top_i = jax.lax.top_k(scores, TOP_K)
        top_w = top_w / jnp.sum(top_w, axis=-1, keepdims=True)
        top_w = top_w.astype(h.dtype)
        hf = h.reshape(-1, H)
        oh = jax.nn.one_hot(top_i.reshape(-1, TOP_K), E, dtype=h.dtype)
        cw = jnp.einsum('tke,tk->te', oh, top_w.reshape(-1, TOP_K))
        a = jnp.einsum('th,eih->eti', hf, w1)
        g = jnp.einsum('th,eih->eti', hf, w3)
        eo = jnp.einsum('eti,ehi->eth', jax.nn.silu(a) * g, w2)
        out = jnp.einsum('eth,te->th', eo, cw)
        return hidden_states + out.reshape(B, S, H)
    x = x + jnp.tanh(g_xattn[0]) * _L0_xattn_ref(_layernorm(x, axis=-1), ctx_1024, mask_Bx1x1xS2_ff0, L0_xattn_cq_w, L0_xattn_cq_b, L0_xattn_ck_w, L0_xattn_ck_b, L0_xattn_cv_w, L0_xattn_cv_b, L0_xattn_co_w, L0_xattn_co_b, L0_xattn_co_g, L0_xattn_co_be, L0_xattn_sq_w, L0_xattn_sq_b, L0_xattn_sk_w, L0_xattn_sk_b, L0_xattn_sv_w, L0_xattn_sv_b, L0_xattn_so_w, L0_xattn_so_b, L0_xattn_so_g, L0_xattn_so_be, L0_xattn_fi_w, L0_xattn_fi_b, L0_xattn_fo_w, L0_xattn_fo_b, L0_xattn_fo_g, L0_xattn_fo_be)
    x = x + jnp.tanh(g_ffn[0]) * _L0_ffn_ref(_layernorm(x, axis=-1), L0_ffn_rms_weight, L0_ffn_gate_w, L0_ffn_w1, L0_ffn_w2, L0_ffn_w3)
    return x

_drawn_inputs = setup_inputs


def setup_inputs(seed=0):
    import zlib

    import numpy as np

    out = dict(_drawn_inputs(seed))
    spreads = {'L0_xattn_cq_b': (0.0, 0.1),
     'L0_xattn_ck_b': (0.0, 0.8),
     'L0_xattn_cv_b': (0.0, 0.1),
     'L0_xattn_co_b': (0.0, 0.1),
     'L0_xattn_co_g': (1.0, 0.2),
     'L0_xattn_co_be': (0.0, 0.1),
     'L0_xattn_sq_b': (0.0, 0.302),
     'L0_xattn_sk_b': (0.0, 0.8),
     'L0_xattn_sv_b': (0.0, 0.1),
     'L0_xattn_so_b': (0.0, 0.1),
     'L0_xattn_so_g': (1.0, 0.2),
     'L0_xattn_so_be': (0.0, 0.1),
     'L0_xattn_fi_b': (0.0, 0.1),
     'L0_xattn_fo_b': (0.0, 0.1),
     'L0_xattn_fo_g': (1.0, 0.2),
     'L0_xattn_fo_be': (0.0, 0.1),
     'L0_ffn_rms_weight': (1.0, 0.2)}
    factors = {}
    for name, (base, spread) in spreads.items():
        noise = np.random.default_rng([zlib.crc32(name.encode()), seed]).standard_normal(out[name].shape)
        drawn = base * np.exp(spread * noise) if base else spread * noise
        out[name] = jnp.asarray(drawn.astype(out[name].dtype))
    for name, factor in factors.items():
        out[name] = (out[name] * factor).astype(out[name].dtype)
    return out
```

```python
import concourse.bass as bass
from concourse import mybir
from contextlib import ExitStack

F32 = mybir.dt.float32
F32R = mybir.dt.float32r
BF16 = mybir.dt.bfloat16
U32 = mybir.dt.uint32
I32 = mybir.dt.int32
ALU = mybir.AluOpType
ACT = mybir.ActivationFunctionType
AX = mybir.AxisListType

P = 128
B, S, D = 8, 512, 256
H, DH = 16, 16
F = 1024
I = 896
NE = 8
QT = S // P
KD = D // P
KF = F // P
NP_ = H // 2
G = 4
NG = H // G
HALF = P // 2
SCALE = 1.0 / 4.0
LN_EPS = 1e-5
RMS_EPS = 1e-6
KI = I // P
GT = 3
GR = GT * P
T = B * S
STEPS = (2 * T + NE * (GR - 1)) // GR
STEPS += STEPS % 2
CAP = T + GR
ROW_MASK, ROW_MAX = 3 * DH, 3 * DH + 2


def split_products(hi_l, lo_l, hi_r, lo_r):
    return [(hi_l, hi_r), (hi_l, lo_r), (lo_l, hi_r)]


def mixer_phase(nc, ctx, A, scratch):
    sb = lambda name, shape, dt=F32: ctx.enter_context(nc.sbuf_tensor(name, shape, dt))
    sem_list = []

    def sem(name):
        s = ctx.enter_context(nc.semaphore(name))
        sem_list.append(s)
        return s

    ident, topv, slots, tanh_g = A["ident"], A["topv"], A["slots"], A["tanh_g"]
    experts, running = A["experts"], A["running"]
    w_hi = sb("w_hi", [P, 8, KD, D], F32R)
    w_lo = sb("w_lo", [P, 8, KD, D], F32R)
    fi_hi = sb("fi_hi", [P, KD, F], F32R)
    fi_lo = sb("fi_lo", [P, KD, F], F32R)
    fo_hi = sb("fo_hi", [P, KF, D], F32R)
    fo_lo = sb("fo_lo", [P, KF, D], F32R)
    gate_hi = sb("gate_hi", [P, KD, NE], F32R)
    gate_lo = sb("gate_lo", [P, KD, NE], F32R)
    rows = {n: sb("row_" + n, [P, D]) for n in ROW_NAMES}
    cols = sb("cols", [P, 4 * KD + KF])
    neg_half = sb("neg_half", [P, QT])
    Q, K, V, O = 0, 1, 2, 3
    first_row = A["first_row"]
    before = sb("before", [P, P], BF16)
    ones_sq = sb("ones_sq", [P, P], BF16)
    col_of = lambda l, which, mt: cols[:, 4 * l + 2 * which + mt:4 * l + 2 * which + mt + 1]
    fi_col = lambda mt: cols[:, 4 * KD + mt:4 * KD + mt + 1]

    with nc.sbuf_tensor("w_raw", [P, 8, KD, D], F32) as w_raw, \
            nc.sbuf_tensor("fi_raw", [P, KD, F], F32) as fi_raw, \
            nc.sbuf_tensor("fo_raw", [P, KF, D], F32) as fo_raw, \
            nc.sbuf_tensor("gate_raw", [P, KD, NE], F32) as gate_raw, \
            nc.sbuf_tensor("g_raw", [P, 2], F32) as g_raw, \
            nc.semaphore("weights_in") as weights_in, \
            nc.semaphore("hi_made") as hi_made, \
            nc.semaphore("lo_made") as lo_made, \
            nc.semaphore("ident_zero") as ident_zero, \
            nc.semaphore("ident_made") as ident_made, \
            nc.semaphore("iota_made") as iota_made, \
            nc.semaphore("tanh_made") as tanh_made, \
            nc.Block() as block:
        raws = [(w_raw[:, j], w_hi[:, j], w_lo[:, j]) for j in range(8)]
        raws += [(fi_raw[:, :, :], fi_hi[:, :, :], fi_lo[:, :, :]),
                 (fo_raw[:, :, :], fo_hi[:, :, :], fo_lo[:, :, :]),
                 (gate_raw[:, :, :], gate_hi[:, :, :], gate_lo[:, :, :])]

        @block.sync
        def _(sp):
            sp.dma_start(w_raw[:, :, :, :], A["attn_w"]).then_inc(weights_in, 16)
            sp.dma_start(fi_raw[:, :, :], A["fi_w"]).then_inc(weights_in, 16)
            sp.dma_start(fo_raw[:, :, :], A["fo_w"]).then_inc(weights_in, 16)
            sp.dma_start(gate_raw[:, :, :], A["gate_w"]).then_inc(weights_in, 16)
            sp.dma_start(cols[:, :], A["cols"]).then_inc(weights_in, 16)
            for n in ROW_NAMES:
                sp.dma_start(rows[n][:, :], A[n].partition_broadcast(P)).then_inc(weights_in, 16)
            sp.dma_start(g_raw[:, 0:1], A["g_xattn"].partition_broadcast(P)).then_inc(weights_in, 16)
            sp.dma_start(g_raw[:, 1:2], A["g_ffn"].partition_broadcast(P)).then_inc(weights_in, 16)

        n_loads = 5 + len(ROW_NAMES) + 2

        @block.scalar
        def _(act):
            act.wait_ge(weights_in, 16 * n_loads)
            act.activation(tanh_g[:, :], g_raw[:, :], ACT.Tanh).then_inc(tanh_made, 1)

        @block.vector
        def _(dve):
            dve.memset(running[:, :, :], 0.0)
            dve.memset(neg_half[:, :], -0.5).then_inc(hi_made, 1)
            dve.wait_ge(weights_in, 16 * n_loads)
            for n, (raw, hi, lo) in enumerate(raws):
                dve.tensor_copy(hi, raw).then_inc(hi_made, 1)
            for n, (raw, hi, lo) in enumerate(raws):
                dve.wait_ge(hi_made, n + 2)
                dve.tensor_tensor(lo, raw, hi.bitcast(F32), ALU.subtract).then_inc(lo_made, 1)

        @block.gpsimd
        def _(pool):
            pool.memset(ident[:, :], 0.0).then_inc(ident_zero, 1)
            pool.wait_ge(ident_zero, 1)
            pool.affine_select(out=ident[:, :], in_=ident[:, :], compare_op=ALU.not_equal, fill=1.0,
                               base=0, pattern=[[-1, P]], channel_multiplier=1).then_inc(ident_made, 1)
            pool.memset(ones_sq[:, :], 1.0).then_inc(ident_zero, 1)
            pool.memset(before[:, :], 1.0).then_inc(ident_zero, 1)
            pool.wait_ge(ident_zero, 3)
            pool.affine_select(out=before[:, :], in_=before[:, :], compare_op=ALU.is_gt, fill=0.0,
                               base=0, pattern=[[1, P]], channel_multiplier=-1)
            pool.iota(experts[:, :], pattern=[[1, NE]], base=0, channel_multiplier=0,
                      allow_small_or_imprecise_dtypes=True).then_inc(iota_made, 1)
            pool.wait_ge(iota_made, 1)
            pool.tensor_scalar(first_row[:, :], experts[:, :], float(CAP), 0.0, ALU.mult, ALU.add)

    kz = sb("kz", [P, NP_, 2, S], F32R)
    work = sb("work", [P, 2 * KF * S], F32R)
    qst = work[:, 0:NP_ * S].rearrange("p (r n) -> p r n", r=NP_)
    qk = work[:, NP_ * S:2 * NP_ * S].rearrange("p (w m n) -> p w m n", w=4, m=KD)
    q_hi, q_lo, k_hi, k_lo = (qk[:, n] for n in range(4))
    in_hi = work[:, 0:KF * S].rearrange("p (m n) -> p m n", m=KF)
    in_lo = work[:, KF * S:2 * KF * S].rearrange("p (m n) -> p m n", m=KF)
    a_hi = sb("a_hi", [P, KD, S], F32R)
    a_lo = sb("a_lo", [P, KD, S], F32R)
    c_hi = sb("c_hi", [P, KD, S], F32R)
    c_lo = sb("c_lo", [P, KD, S], F32R)
    x_tok = sb("x_tok", [P, QT, D])
    n_tok = sb("n_tok", [P, QT, D])
    h_tok = sb("h_tok", [P, QT, D])
    vaug = sb("vaug", [P, QT, H, 2 * DH])
    probs = sb("probs", [P, 4, 2, S])
    ev = sb("ev", [P, NG, S])
    nmf = ev[0:G, NG - 1]
    negmax = sb("negmax", [P, NG, QT, G])
    nm_hi = sb("nm_hi", [G, S], F32R)
    nm_lo = sb("nm_lo", [G, S], F32R)
    words = lambda ap: ap.bitcast(F32)
    mask_row, mask_hi, mask_lo = ev[0:1, NG - 1], nm_hi[0:1, :], nm_lo[0:1, :]
    ones_row = kz[ROW_MAX:ROW_MAX + 1, 0, 0, :]
    zero_row = kz[HALF:HALF + 1, 0, 0, :]
    stats = sb("stats", [P, QT, 6])
    mv = sb("mv", [P, QT, 2])
    var_eps = sb("var_eps", [P, QT])
    rstd = sb("rstd", [P, QT])
    sumsq = sb("sumsq", [P, QT])
    rden = sb("rden", [P, QT, H])
    logits = sb("logits", [P, QT, NE])
    max8 = sb("max8", [P, QT, 8])
    idx8 = sb("idx8", [P, QT, 8], U32)
    small = lambda at, n: probs[:, 0, 0, at:at + n]
    onehot = small(0, 64).rearrange("p (s q e) -> p s q e", s=2, q=QT)
    weighed = small(64, 64).rearrange("p (s q e) -> p s q e", s=2, q=QT)
    place = small(128, 32).rearrange("p (q e) -> p q e", q=QT)
    chosen_f = small(160, 2 * QT).rearrange("p (q s) -> p q s", q=QT)
    slot_f = small(168, 2 * QT)
    picks = sb("picks", [P, QT, NE], BF16)
    slot_now = sb("slot_now", [P, 2 * QT], U32)
    ps = ctx.enter_context(nc.psum_tensor("ps", [P, 8, S], F32))

    ones_r = nm_hi[0:1, :]
    with nc.semaphore("cleared") as cleared, nc.semaphore("ones_placed") as ones_placed, \
            nc.Block() as block:
        @block.vector
        def _(dve):
            dve.memset(kz[:, :, :, :].bitcast(F32), 0.0).then_inc(cleared, 1)
            dve.memset(work[:, :].bitcast(F32), 0.0).then_inc(cleared, 1)
            dve.memset(vaug[:, :, :, :], 0.0).then_inc(cleared, 1)
            dve.memset(ones_r.bitcast(F32), 1.0).then_inc(cleared, 1)
            dve.wait_ge(cleared, 3)
            dve.memset(vaug[:, :, :, DH:DH + 1], 1.0)

        @block.sync
        def _(sp):
            sp.wait_ge(cleared, 4)
            for half in range(2):
                for t in range(2):
                    sp.dma_start(words(kz[HALF * half + ROW_MAX + t:HALF * half + ROW_MAX + t + 1, :, half, :]),
                                 words(ones_r).unsqueeze(1).to_broadcast([1, NP_, S])).then_inc(ones_placed, 16)
            sp.wait_ge(ones_placed, 64)

    scattered = ctx.enter_context(nc.semaphore("scattered"))
    x_in = sem("x_in")
    ctx_in = sem("ctx_in")
    mask_in = sem("mask_in")
    mask_made = sem("mask_made")
    var_made = sem("var_made")
    rstd_made = sem("rstd_made")
    normed = sem("normed")
    affine_mul = sem("affine_mul")
    res_made = sem("res_made")
    tr_ctx = sem("tr_ctx")
    tr_in = sem("tr_in")
    c_hi_made = sem("c_hi_made")
    c_lo_made = sem("c_lo_made")
    a_hi_made = sem("a_hi_made")
    a_lo_made = sem("a_lo_made")
    qk_mm = sem("qk_mm")
    qk_hi_made = sem("qk_hi_made")
    qk_lo_made = sem("qk_lo_made")
    v_mm = sem("v_mm")
    v_made = sem("v_made")
    k_filled = sem("k_filled")
    q_filled = sem("q_filled")
    max_mm = sem("max_mm")
    max_made = sem("max_made")
    nm_tr = sem("nm_tr")
    nm_copied = sem("nm_copied")
    nm_hi_made = sem("nm_hi_made")
    nm_lo_made = sem("nm_lo_made")
    nm_filled = sem("nm_filled")
    score_mm = sem("score_mm")
    exp_made = sem("exp_made")
    pv_mm = sem("pv_mm")
    ev_made = sem("ev_made")
    at_tr = sem("at_tr")
    at_norm = sem("at_norm")
    o_mm = sem("o_mm")
    h_made = sem("h_made")
    fi_mm = sem("fi_mm")
    gelu_made = sem("gelu_made")
    in_hi_made = sem("in_hi_made")
    in_lo_made = sem("in_lo_made")
    sq_made = sem("sq_made")
    out_made = sem("out_made")
    stored = sem("stored")
    lg_mm = sem("lg_mm")
    picks_made = sem("picks_made")
    rank_mm = sem("rank_mm")
    slots_made = sem("slots_made")
    dve_chain = sem("dve_chain")
    pool_chain = sem("pool_chain")

    N_FILL = 3 * H
    N_NM = 2 * G * 16
    scope = {}
    with nc.Fori(0, B) as b:
        with nc.Block() as block:

            @block.sync
            def _(sp):
                sp.dma_start(h_tok[:, :, :], A["ctx"][b]).then_inc(ctx_in, 16)
                sp.dma_start(x_tok[:, :, :], A["x"][b]).then_inc(x_in, 16)
                sp.dma_start(mask_row, A["mask"][b]).then_inc(mask_in, 16)
                for l in range(2):
                    if l == 0:
                        sp.wait_ge(mask_made, 3)
                    else:
                        sp.wait_ge(exp_made, 32)
                    for half in range(2):
                        for t in range(2):
                            src = ((mask_hi, mask_lo)[t] if l == 0 else zero_row)
                            sp.dma_start(words(kz[HALF * half + ROW_MASK + t:HALF * half + ROW_MASK + t + 1, :, half, :]),
                                         words(src).unsqueeze(1).to_broadcast([1, NP_, S])).then_inc(k_filled, 16)
                        for t in range(4):
                            src = ones_row if t < 2 else zero_row
                            sp.dma_start(words(qst[HALF * half + ROW_MASK + t:HALF * half + ROW_MASK + t + 1, :, :]),
                                         words(src).unsqueeze(1).to_broadcast([1, NP_, S])).then_inc(q_filled, 16)
                    for what in range(2):
                        for mt in range(KD):
                            n = 4 * l + 2 * what + mt + 1
                            sp.wait_ge(qk_hi_made, n)
                            sp.wait_ge(qk_lo_made, n)
                            parts = ((k_hi, k_lo, k_hi), (q_hi, q_hi, q_lo))[what]
                            for i in range(H // KD):
                                pair, half = (H // KD * mt + i) // 2, i % 2
                                for t in range(3):
                                    at = slice(HALF * half + DH * t, HALF * half + DH * t + DH)
                                    dst = qst[at, pair, :] if what else kz[at, pair, half, :]
                                    sp.dma_start(words(dst), words(parts[t][DH * i:DH * i + DH, mt])) \
                                        .then_inc((k_filled, q_filled)[what], 16)
                    for g in range(NG):
                        sp.wait_ge(nm_lo_made, NG * l + g + 1)
                        for j in range(G):
                            for t in range(2):
                                at = HALF * (j % 2) + ROW_MAX + t
                                sp.dma_start(words(qst[at:at + 1, 2 * g + j // 2, :]),
                                             words((nm_hi, nm_lo)[t][j:j + 1, :])) \
                                    .then_inc(nm_filled, 16)
                sp.wait_ge(out_made, QT)
                sp.dma_start(scratch["res"][b], x_tok[:, :, :]).then_inc(stored, 16)
                sp.wait_ge(stored, 16)

            @block.gpsimd
            def _(pool):
                chain = [0]

                def link(ins):
                    chain[0] += 1
                    ins.then_inc(pool_chain, 1)
                    pool.wait_ge(pool_chain, chain[0])

                def root(n):
                    pool.wait_ge(var_made, n + 1)
                    pool.tensor_tensor(rstd[:, :], var_eps[:, :], neg_half[:, :], ALU.pow) \
                        .then_inc(rstd_made, 1)

                def add_beta(n, name):
                    for qt in range(QT):
                        pool.wait_ge(affine_mul, QT * n + qt + 1)
                        pool.tensor_tensor(n_tok[:, qt], h_tok[:, qt], rows[name][:, :], ALU.add) \
                            .then_inc(normed, 1)

                def residual(n, name):
                    pool.wait_ge(tr_in, KD * (n + 1))
                    for qt in range(QT):
                        pool.tensor_tensor(n_tok[:, qt], n_tok[:, qt], rows[name][:, :], ALU.add) \
                            .then_inc(res_made, 1)

                pool.wait_ge(mask_in, 16)
                pool.tensor_scalar(mask_row, mask_row, 1.0 / SCALE, 0.0, ALU.mult, ALU.add) \
                    .then_inc(mask_made, 1)
                pool.wait_ge(mask_made, 1)
                pool.tensor_copy(mask_hi, mask_row).then_inc(mask_made, 1)
                pool.wait_ge(mask_made, 2)
                pool.tensor_tensor(mask_lo, mask_row, mask_hi.bitcast(F32),
                                   ALU.subtract).then_inc(mask_made, 1)
                root(0)
                for l in range(2):
                    residual(l, ("co_b", "so_b")[l])
                    for g in range(NG):
                        n = NG * l + g
                        pool.wait_ge(nm_copied, n + 1)
                        if n:
                            pool.wait_ge(nm_filled, N_NM * n)
                        pool.tensor_copy(nm_hi[:, :], nmf).then_inc(nm_hi_made, 1)
                        pool.wait_ge(nm_hi_made, n + 1)
                        pool.tensor_tensor(nm_lo[:, :], nmf, nm_hi[:, :].bitcast(F32),
                                           ALU.subtract).then_inc(nm_lo_made, 1)
                    root(1 + l)
                    add_beta(l, ("co_be", "so_be")[l])
                residual(2, "fo_b")
                for mt in range(KF):
                    pool.wait_ge(in_hi_made, mt + 1)
                    pool.tensor_tensor(in_lo[:, mt], ev[:, mt % NG], in_hi[:, mt].bitcast(F32),
                                       ALU.subtract).then_inc(in_lo_made, 1)
                root(3)
                add_beta(2, "fo_be")
                root(4)
                root(5)
                pool.wait_ge(slots_made, 1)
                for s in range(2):
                    for qt in range(QT):
                        n = QT * s + qt
                        pool.indirect_dma_start(
                            out=scratch["xs"], in_=n_tok[:, qt], in_offset=None,
                            out_offset=bass.IndirectOffsetOnAxis(ap=slot_now[:, n:n + 1], axis=0)) \
                            .then_inc(scattered, 16)
                pool.wait_ge(scattered, b * (16 * 2 * QT) + 16 * 2 * QT)

            @block.scalar
            def _(act):
                def hi_of_ctx(n, bank):
                    for mt in range(KD):
                        act.wait_ge(tr_ctx, KD * n + mt + 1)
                        act.activation(c_hi[:, mt], ps[:, bank + mt], ACT.Copy).then_inc(c_hi_made, 1)

                def hi_of_in(n, bank):
                    for mt in range(KD):
                        act.wait_ge(tr_in, KD * n + mt + 1)
                        act.activation(a_hi[:, mt], ps[:, bank + mt], ACT.Copy).then_inc(a_hi_made, 1)

                hi_of_ctx(0, 0)
                hi_of_in(0, 6)
                for l in range(2):
                    if l == 1:
                        hi_of_in(1, 6)
                    for what in range(2):
                        for mt in range(KD):
                            n = 4 * l + 2 * what + mt
                            act.wait_ge(qk_mm, n + 1)
                            if l == 1 and what == 0 and mt == 0:
                                act.wait_ge(k_filled, 16 * (4 + N_FILL))
                                act.wait_ge(q_filled, 16 * (8 + N_FILL))
                            act.activation((k_hi, q_hi)[what][:, mt], ps[:, (2, 0)[what] + mt],
                                           ACT.Identity, bias=col_of(l, what, mt)) \
                                .then_inc(qk_hi_made, 1)

                    def copy_max(g):
                        n = NG * l + g
                        act.wait_ge(nm_tr, n + 1)
                        if n:
                            act.wait_ge(nm_lo_made, n)
                        act.activation(nmf, ps[0:G, 7], ACT.Copy).then_inc(nm_copied, 1)

                    copy_max(0)
                    for g in range(NG):
                        for s in range(8):
                            n = 8 * NG * l + 8 * g + s
                            act.wait_ge(score_mm, n + 1)
                            if n >= 4:
                                act.wait_ge(pv_mm, (n - 4) // 2 + 1)
                            act.activation(probs[:, s % 4], ps[:, 2 * (s % 2):2 * (s % 2) + 2],
                                           ACT.Exp, scale=SCALE).then_inc(exp_made, 1)
                            if s == 1 and g > 0:
                                act.wait_ge(pv_mm, 4 * (NG * l + g))
                                act.activation(ev[:, g - 1], ps[:, 6], ACT.Copy).then_inc(ev_made, 1)
                        if g + 1 < NG:
                            copy_max(g + 1)
                    act.wait_ge(pv_mm, 4 * NG * (l + 1))
                    act.activation(ev[:, NG - 1], ps[:, 6], ACT.Copy).then_inc(ev_made, 1)
                    hi_of_ctx(1 + l, 4)
                hi_of_in(2, 6)
                for mt in range(KF):
                    act.wait_ge(fi_mm, mt + 1)
                    if mt >= NG:
                        act.wait_ge(in_lo_made, mt - NG + 1)
                    act.activation(ev[:, mt % NG], ps[:, mt % 6], ACT.Gelu, bias=fi_col(mt)) \
                        .then_inc(gelu_made, 1)
                for qt in range(QT):
                    act.wait_ge(normed, 4 * QT + qt + 1)
                    act.activation(ev[:, qt, 0:D], h_tok[:, qt], ACT.Square,
                                   accum_out=sumsq[:, qt:qt + 1]).then_inc(sq_made, 1)
                hi_of_in(3, 2)

            @block.vector
            def _(dve):
                chain = [0]

                def link(ins):
                    chain[0] += 1
                    ins.then_inc(dve_chain, 1)
                    return chain[0]

                def settle():
                    dve.wait_ge(dve_chain, chain[0])

                def statistics(src):
                    for qt in range(QT):
                        link(dve.bn_stats(stats[:, qt], src[:, qt]))
                    settle()
                    for qt in range(QT):
                        link(dve.bn_aggr(mv[:, qt], stats[:, qt]))
                    settle()
                    dve.tensor_scalar(var_eps[:, :], mv[:, :, 1], LN_EPS, None, ALU.add) \
                        .then_inc(var_made, 1)

                def normalise(dst, src, n):
                    dve.wait_ge(rstd_made, n + 1)
                    for qt in range(QT):
                        yield qt, dve.tensor_scalar(dst[:, qt], src[:, qt], mv[:, qt, 0:1],
                                                    rstd[:, qt:qt + 1], ALU.subtract, ALU.mult)

                def lo_of_ctx(n, bank):
                    for mt in range(KD):
                        dve.wait_ge(c_hi_made, KD * n + mt + 1)
                        dve.tensor_tensor(c_lo[:, mt], ps[:, bank + mt], c_hi[:, mt].bitcast(F32),
                                          ALU.subtract).then_inc(c_lo_made, 1)

                def lo_of_in(n, bank):
                    for mt in range(KD):
                        dve.wait_ge(a_hi_made, KD * n + mt + 1)
                        dve.tensor_tensor(a_lo[:, mt], ps[:, bank + mt], a_hi[:, mt].bitcast(F32),
                                          ALU.subtract).then_inc(a_lo_made, 1)

                def close(n, gamma):
                    for qt in range(QT):
                        dve.wait_ge(o_mm, QT * n + qt + 1)
                        dve.wait_ge(res_made, QT * n + qt + 1)
                        dve.tensor_tensor(h_tok[:, qt], ps[:, o_bank(n, qt), 0:D], n_tok[:, qt],
                                          ALU.add).then_inc(h_made, 1)
                    dve.wait_ge(h_made, QT * (n + 1))
                    statistics(h_tok)
                    for qt, ins in normalise(h_tok, h_tok, n + 1):
                        link(ins)
                    settle()
                    for qt in range(QT):
                        dve.tensor_tensor(h_tok[:, qt], h_tok[:, qt], rows[gamma][:, :],
                                          ALU.mult).then_inc(affine_mul, 1)

                dve.wait_ge(x_in, 16)
                statistics(x_tok)
                lo_of_ctx(0, 0)
                for qt, ins in normalise(n_tok, x_tok, 0):
                    ins.then_inc(normed, 1)
                lo_of_in(0, 6)
                for l in range(2):
                    if l == 1:
                        lo_of_in(1, 6)
                    for what in range(2):
                        for mt in range(KD):
                            n = 4 * l + 2 * what + mt
                            dve.wait_ge(qk_hi_made, n + 1)
                            dve.scalar_tensor_tensor(
                                (k_lo, q_lo)[what][:, mt], ps[:, (2, 0)[what] + mt],
                                col_of(l, what, mt), (k_hi, q_hi)[what][:, mt].bitcast(F32),
                                ALU.add, ALU.subtract).then_inc(qk_lo_made, 1)
                    for kt in range(QT):
                        dve.wait_ge(v_mm, QT * l + kt + 1)
                        half = kt % 2
                        dve.tensor_tensor(
                            vaug[:, kt, :, 0:DH],
                            ps[:, V_BANK[kt], 0:D].rearrange("p (h d) -> p h d", d=DH),
                            rows[("cv_b", "sv_b")[l]][:, :].rearrange("p (h d) -> p h d", d=DH),
                            ALU.add).then_inc(v_made, 1)
                    for n in range(16 * NG):
                        i = 16 * NG * l + n
                        g, j, qt = n // 16, (n // 4) % 4, n % 4
                        dve.wait_ge(max_mm, i + 1)
                        dve.tensor_reduce(negmax[:, g, qt, j:j + 1], ps[:, 4 + n % 2], AX.X,
                                          ALU.max, negate=True).then_inc(max_made, 1)
                    for qt in range(QT):
                        dve.wait_ge(at_tr, QT * l + qt + 1)
                        src = ps[:, qt].rearrange("p (h d) -> p h d", d=2 * DH)
                        link(dve.reciprocal(rden[:, qt], src[:, :, DH]))
                        settle()
                        dve.tensor_tensor(h_tok[:, qt].rearrange("p (h d) -> p h d", d=DH),
                                          src[:, :, 0:DH],
                                          rden[:, qt].unsqueeze(2).to_broadcast([P, H, DH]),
                                          ALU.mult).then_inc(at_norm, 1)
                    lo_of_ctx(1 + l, 4)
                    close(l, ("co_g", "so_g")[l])
                lo_of_in(2, 6)
                for mt in range(KF):
                    dve.wait_ge(gelu_made, mt + 1)
                    dve.tensor_copy(in_hi[:, mt], ev[:, mt % NG]).then_inc(in_hi_made, 1)
                close(2, "fo_g")
                for qt in range(QT):
                    dve.wait_ge(normed, 3 * QT + qt + 1)
                    link(dve.scalar_tensor_tensor(x_tok[:, qt], n_tok[:, qt], tanh_g[:, 0:1],
                                                  x_tok[:, qt], ALU.mult, ALU.add))
                settle()
                statistics(x_tok)
                for qt, ins in normalise(h_tok, x_tok, 4):
                    ins.then_inc(normed, 1)
                dve.wait_ge(normed, 5 * QT)
                for qt in range(QT):
                    dve.scalar_tensor_tensor(x_tok[:, qt], h_tok[:, qt], tanh_g[:, 1:2],
                                             x_tok[:, qt], ALU.mult, ALU.add).then_inc(out_made, 1)
                dve.wait_ge(sq_made, QT)
                dve.tensor_scalar(var_eps[:, :], sumsq[:, :], 1.0 / D, RMS_EPS, ALU.mult,
                                  ALU.add).then_inc(var_made, 1)
                dve.wait_ge(rstd_made, 6)
                for qt in range(QT):
                    dve.scalar_tensor_tensor(n_tok[:, qt], h_tok[:, qt], rstd[:, qt:qt + 1],
                                             rows["rms"][:, :], ALU.mult, ALU.mult) \
                        .then_inc(normed, 1)
                lo_of_in(3, 2)
                dve.wait_ge(lg_mm, 1)
                link(dve.tensor_copy(logits[:, :, :],
                                     ps[:, 4, 0:QT * NE].rearrange("p (q e) -> p q e", q=QT)))
                settle()
                for qt in range(QT):
                    link(dve.max(max8[:, qt], logits[:, qt]))
                settle()
                for qt in range(QT):
                    link(dve.max_index(idx8[:, qt], max8[:, qt], logits[:, qt]))
                settle()
                link(dve.tensor_copy(topv[:, bass.ds(b * QT, QT), :], max8[:, :, 0:2]))
                link(dve.tensor_copy(chosen_f, idx8[:, :, 0:2]))
                link(dve.tensor_copy(running[:, 0], running[:, QT]))
                settle()
                for s in range(2):
                    link(dve.tensor_tensor(
                        onehot[:, s], experts[:, :].unsqueeze(1).to_broadcast([P, QT, NE]),
                        chosen_f[:, :, s].unsqueeze(2).to_broadcast([P, QT, NE]), ALU.is_equal))
                settle()
                dve.tensor_tensor(picks[:, :, :], onehot[:, 0], onehot[:, 1], ALU.add) \
                    .then_inc(picks_made, 1)
                dve.wait_ge(rank_mm, 1)
                for qt in range(QT):
                    link(dve.tensor_tensor(running[:, qt + 1], ps[:, 5, (QT + qt) * NE:(QT + qt + 1) * NE],
                                           running[:, qt], ALU.add))
                    settle()
                link(dve.tensor_tensor(place,
                                       ps[:, 5, 0:QT * NE].rearrange("p (q e) -> p q e", q=QT),
                                       running[:, 0:QT], ALU.add))
                settle()
                link(dve.tensor_tensor(place, place,
                                       first_row[:, :].unsqueeze(1).to_broadcast([P, QT, NE]),
                                       ALU.add))
                settle()
                for s in range(2):
                    link(dve.tensor_tensor(weighed[:, s], onehot[:, s], place, ALU.mult))
                settle()
                link(dve.tensor_reduce(slot_f, small(64, 64).rearrange("p (n e) -> p n e", e=NE),
                                       AX.X, ALU.add))
                settle()
                link(dve.tensor_copy(slots[:, bass.ds(b * 2 * QT, 2 * QT)], slot_f))
                dve.tensor_copy(slot_now[:, :], slot_f).then_inc(slots_made, 1)
                settle()

            @block.tensor
            def _(pe):
                def turn(src, bank, ready, base, done):
                    for mt in range(KD):
                        for qt in range(QT):
                            if mt == 0:
                                pe.wait_ge(ready, base + qt + 1)
                            ins = pe.transpose(ps[:, bank + mt, qt * P:(qt + 1) * P],
                                               src[:, qt, mt * P:(mt + 1) * P], ident[:, :])
                        ins.then_inc(done, 1)

                def product(out, left, right):
                    terms = [(l_, r_) for ls, rs in zip(left, right)
                             for l_, r_ in split_products(*ls, *rs)]
                    for n, (l_, r_) in enumerate(terms):
                        ins = pe.matmul(out, l_, r_, start=n == 0, stop=n == len(terms) - 1)
                    return ins

                pe.wait_ge(ctx_in, 16)
                for mt in range(KD):
                    for qt in range(QT):
                        ins = pe.transpose(ps[:, mt, qt * P:(qt + 1) * P],
                                           h_tok[:, qt, mt * P:(mt + 1) * P], ident[:, :])
                    ins.then_inc(tr_ctx, 1)
                turn(n_tok, 6, normed, 0, tr_in)
                for l in range(2):
                    if l == 0:
                        src_hi, src_lo = c_hi, c_lo
                        pe.wait_ge(c_lo_made, KD)
                    else:
                        src_hi, src_lo = a_hi, a_lo
                        turn(n_tok, 6, normed, QT, tr_in)
                        pe.wait_ge(a_lo_made, 2 * KD)
                    w = lambda which, part, kt, c: part[:, 4 * l + which, kt, c]
                    for mt in range(KD):
                        c = slice(mt * P, (mt + 1) * P)
                        product(ps[:, 2 + mt], [(w(K, w_hi, kt, c), w(K, w_lo, kt, c)) for kt in range(KD)],
                                [(src_hi[:, kt], src_lo[:, kt]) for kt in range(KD)]) \
                            .then_inc(qk_mm, 1)
                    if l == 0:
                        pe.wait_ge(a_lo_made, KD)
                    for mt in range(KD):
                        c = slice(mt * P, (mt + 1) * P)
                        product(ps[:, mt], [(w(Q, w_hi, kt, c), w(Q, w_lo, kt, c)) for kt in range(KD)],
                                [(a_hi[:, kt], a_lo[:, kt]) for kt in range(KD)]).then_inc(qk_mm, 1)
                    for kt in range(QT):
                        c = slice(kt * P, (kt + 1) * P)
                        if kt == 2:
                            pe.wait_ge(a_lo_made, KD * (l + 1))
                        product(ps[:, V_BANK[kt], 0:D],
                                [(src_hi[:, k, c], src_lo[:, k, c]) for k in range(KD)],
                                [(w(V, w_hi, k, slice(0, D)), w(V, w_lo, k, slice(0, D)))
                                 for k in range(KD)]).then_inc(v_mm, 1)

                    def maxima(g, j, qt):
                        n = 16 * NG * l + 16 * g + 4 * j + qt
                        half, pair = j % 2, 2 * g + j // 2
                        if g == 0 and j == 0 and qt < 2:
                            pe.wait_ge(v_made, QT * (l + 1))
                        elif n % (16 * NG) >= 2:
                            pe.wait_ge(max_made, n - 1)
                        pe.matmul(ps[:, 4 + n % 2], qst[:, pair, qt * P:(qt + 1) * P],
                                  kz[:, pair, half, :], start=True, stop=True).then_inc(max_mm, 1)

                    def turn_maxima(g):
                        n = NG * l + g
                        pe.wait_ge(max_made, 16 * (n + 1))
                        if n:
                            pe.wait_ge(nm_copied, n)
                        for qt in range(QT):
                            ins = pe.transpose(ps[0:G, 7, qt * P:(qt + 1) * P], negmax[:, g, qt],
                                               ident[:, :])
                        ins.then_inc(nm_tr, 1)

                    def values(g, kt):
                        n = 4 * (NG * l + g) + kt
                        pe.wait_ge(exp_made, 2 * n + 2)
                        if kt == 0 and g > 0:
                            pe.wait_ge(ev_made, NG * l + g)
                        for j in range(G):
                            half, i = j % 2, j // 2
                            ins = pe.matmul(ps[32 * j:32 * j + 32, 6], vaug[:, kt, G * g + j],
                                            probs[:, (2 * kt + i) % 4, half], start=kt == 0,
                                            stop=kt == QT - 1, tile_position=(0, 32 * j))
                        ins.then_inc(pv_mm, 1)

                    pe.wait_ge(k_filled, 16 * (4 + N_FILL) * (l + 1))
                    pe.wait_ge(q_filled, 16 * (8 + N_FILL) * (l + 1))
                    for j in range(G):
                        for qt in range(QT):
                            maxima(0, j, qt)
                    turn_maxima(0)
                    for g in range(NG):
                        pe.wait_ge(nm_filled, N_NM * (NG * l + g + 1))
                        for s in range(8):
                            n = 8 * (NG * l + g) + s
                            kt, i = s // 2, s % 2
                            if n % 32 >= 2:
                                pe.wait_ge(exp_made, n - 1)
                            for half in range(2):
                                ins = pe.matmul(ps[:, 2 * i + half],
                                                kz[:, 2 * g + i, half, kt * P:(kt + 1) * P],
                                                qst[:, 2 * g + i, :], start=True, stop=True)
                            ins.then_inc(score_mm, 1)
                            if g + 1 < NG:
                                maxima(g + 1, s // 2, 2 * (s % 2))
                                maxima(g + 1, s // 2, 2 * (s % 2) + 1)
                            if s % 2 and s > 1:
                                values(g, s // 2 - 1)
                        if g + 1 < NG:
                            turn_maxima(g + 1)
                        values(g, QT - 1)
                    pe.wait_ge(ev_made, NG * (l + 1))
                    pe.wait_ge(exp_made, 32 * (l + 1))
                    for qt in range(QT):
                        for g in range(NG):
                            ins = pe.transpose(ps[:, qt, g * P:(g + 1) * P],
                                               ev[:, g, qt * P:(qt + 1) * P], ident[:, :])
                        ins.then_inc(at_tr, 1)
                    turn(h_tok, 4, at_norm, QT * l, tr_ctx)
                    pe.wait_ge(c_lo_made, KD * (2 + l))
                    for qt in range(QT):
                        c = slice(qt * P, (qt + 1) * P)
                        product(ps[:, o_bank(l, qt), 0:D],
                                [(c_hi[:, k, c], c_lo[:, k, c]) for k in range(KD)],
                                [(w(O, w_hi, k, slice(0, D)), w(O, w_lo, k, slice(0, D)))
                                 for k in range(KD)]).then_inc(o_mm, 1)
                turn(n_tok, 6, normed, 2 * QT, tr_in)
                pe.wait_ge(a_lo_made, 3 * KD)
                for mt in range(KF):
                    c = slice(mt * P, (mt + 1) * P)
                    if mt >= 6:
                        pe.wait_ge(gelu_made, mt - 5)
                    product(ps[:, mt % 6], [(fi_hi[:, k, c], fi_lo[:, k, c]) for k in range(KD)],
                            [(a_hi[:, k], a_lo[:, k]) for k in range(KD)]).then_inc(fi_mm, 1)
                pe.wait_ge(in_lo_made, KF)
                for qt in range(QT):
                    c = slice(qt * P, (qt + 1) * P)
                    product(ps[:, o_bank(2, qt), 0:D],
                            [(in_hi[:, k, c], in_lo[:, k, c]) for k in range(KF)],
                            [(fo_hi[:, k], fo_lo[:, k]) for k in range(KF)]).then_inc(o_mm, 1)
                turn(n_tok, 2, normed, 5 * QT, tr_in)
                pe.wait_ge(a_lo_made, 4 * KD)
                for qt in range(QT):
                    c = slice(qt * P, (qt + 1) * P)
                    ins = product(ps[:, 4, qt * NE:(qt + 1) * NE],
                                  [(a_hi[:, k, c], a_lo[:, k, c]) for k in range(KD)],
                                  [(gate_hi[:, k], gate_lo[:, k]) for k in range(KD)])
                ins.then_inc(lg_mm, 1)
                pe.wait_ge(picks_made, 1)
                flat = picks[:, :, :].rearrange("p q e -> p (q e)")
                pe.matmul(ps[:, 5, 0:QT * NE], before[:, :], flat, start=True, stop=True)
                pe.matmul(ps[:, 5, QT * NE:2 * QT * NE], ones_sq[:, :], flat, start=True, stop=True) \
                    .then_inc(rank_mm, 1)

        nc.all_engine_barrier(sems_to_clear=range(sem_list[0].num, sem_list[-1].num + 1))


ROW_NAMES = ["cv_b", "co_b", "co_g", "co_be", "sv_b", "so_b", "so_g", "so_be", "fo_b", "fo_g",
             "fo_be", "rms"]
V_BANK = (4, 5, 6, 7)


def o_bank(n, qt):
    return qt if n < 2 else (6, 7, 0, 1)[qt]


def expert_phase(nc, ctx, A, scratch):
    sb = lambda name, shape, dt=F32: ctx.enter_context(nc.sbuf_tensor(name, shape, dt))
    sem = lambda name: ctx.enter_context(nc.semaphore(name))
    ident, experts, running = A["ident"], A["experts"], A["running"]

    table = sb("table", [P, 2, STEPS], I32)
    counts_i = sb("counts_i", [P, NE], I32)
    zeros = sb("zeros", [P, GT, D])
    ps = ctx.enter_context(nc.psum_tensor("ps_e", [P, 8, 512], F32))

    with nc.sbuf_tensor("steps_f", [P, STEPS], F32) as steps_f, \
            nc.sbuf_tensor("firsts", [P, NE], F32) as firsts, \
            nc.sbuf_tensor("need", [P, NE], F32) as need, \
            nc.sbuf_tensor("upto", [P, 4, NE], F32) as upto, \
            nc.sbuf_tensor("past", [P, NE, STEPS], F32) as past, \
            nc.sbuf_tensor("above", [P, 2 * B * QT, NE], F32) as above, \
            nc.sbuf_tensor("shift", [P, NE], F32) as shift, \
            nc.sbuf_tensor("moved", [P, 2 * B * QT], F32) as moved, \
            nc.sbuf_tensor("found", [P, 6, STEPS], F32) as found, \
            nc.semaphore("iota_s") as iota_s, nc.semaphore("chain") as chain_sem, \
            nc.semaphore("counts_made") as counts_made, nc.semaphore("padded") as padded, \
            nc.Block() as block:
        @block.gpsimd
        def _(pool):
            pool.iota(steps_f[:, :], pattern=[[1, STEPS]], base=0, channel_multiplier=0,
                      allow_small_or_imprecise_dtypes=True).then_inc(iota_s, 1)

        @block.vector
        def _(dve):
            n = [0]

            def step(ins):
                n[0] += 1
                ins.then_inc(chain_sem, 1)
                dve.wait_ge(chain_sem, n[0])

            count = running[:, QT]
            step(dve.tensor_copy(counts_i[:, :], count))
            dve.memset(zeros[:, :, :], 0.0).then_inc(counts_made, 1)
            dve.wait_ge(iota_s, 1)
            over = past[:, :, 0:T // GR + 1]
            j = steps_f[:, 0:T // GR + 1]
            step(dve.tensor_scalar(found[:, 0, 0:T // GR + 1], j, float(GR), None, ALU.mult))
            step(dve.tensor_tensor(over, count.unsqueeze(2).to_broadcast([P, NE, T // GR + 1]),
                                   found[:, 0, 0:T // GR + 1].unsqueeze(1)
                                   .to_broadcast([P, NE, T // GR + 1]), ALU.is_gt))
            step(dve.tensor_reduce(need[:, :], over, AX.X, ALU.add))
            step(dve.tensor_copy(upto[:, 0], need[:, :]))
            for r, reach in enumerate((1, 2, 4)):
                step(dve.tensor_copy(upto[:, r + 1, 0:reach], upto[:, r, 0:reach]))
                step(dve.tensor_tensor(upto[:, r + 1, reach:], upto[:, r, reach:],
                                       upto[:, r, 0:NE - reach], ALU.add))
            step(dve.tensor_tensor(past[:, :, :],
                                   steps_f[:, :].unsqueeze(1).to_broadcast([P, NE, STEPS]),
                                   upto[:, 3].unsqueeze(2).to_broadcast([P, NE, STEPS]), ALU.is_ge))
            by_step = past[:, :, :].rearrange("p e n -> p n e")
            expert, begun, spare, inside, row = (found[:, m] for m in range(5))
            step(dve.tensor_reduce(expert, by_step, AX.X, ALU.add))
            step(dve.tensor_scalar(spare, expert, float(NE), None, ALU.is_ge))
            step(dve.tensor_scalar(expert, expert, float(NE - 1), None, ALU.min))
            step(dve.tensor_tensor(past[:, :, :], past[:, :, :],
                                   need[:, :].unsqueeze(2).to_broadcast([P, NE, STEPS]), ALU.mult))
            step(dve.tensor_reduce(begun, by_step, AX.X, ALU.add))
            step(dve.tensor_tensor(inside, steps_f[:, :], begun, ALU.subtract))
            step(dve.tensor_scalar(found[:, 5], spare, -1.0, 1.0, ALU.mult, ALU.add))
            step(dve.tensor_tensor(inside, inside, found[:, 5], ALU.mult))
            step(dve.tensor_scalar(inside, inside, float(GR), None, ALU.mult))
            step(dve.scalar_tensor_tensor(row, expert, float(CAP), inside, ALU.mult, ALU.add))
            step(dve.tensor_copy(table[:, 0], expert))
            step(dve.tensor_copy(table[:, 1], row))
            slots = A["slots"][:, :]
            n_slots = 2 * B * QT
            step(dve.tensor_tensor(above[:, :, :], slots.unsqueeze(2).to_broadcast([P, n_slots, NE]),
                                   A["first_row"][:, :].unsqueeze(1).to_broadcast([P, n_slots, NE]),
                                   ALU.is_ge))
            step(dve.tensor_scalar(shift[:, 1:NE], need[:, 0:NE - 1], float(GR), float(-CAP),
                                   ALU.mult, ALU.add))
            step(dve.memset(shift[:, 0:1], 0.0))
            step(dve.tensor_tensor(above[:, :, :], above[:, :, :],
                                   shift[:, :].unsqueeze(1).to_broadcast([P, n_slots, NE]), ALU.mult))
            step(dve.tensor_reduce(moved[:, :], above[:, :, :], AX.X, ALU.add))
            step(dve.tensor_tensor(A["picks"][:, :], slots, moved[:, :], ALU.add))

        @block.sync
        def _(sp):
            sp.wait_ge(counts_made, 1)
            for e in range(NE):
                at = sp.value_load(counts_i[0:1, e:e + 1], min_val=0, max_val=T)
                sp.dma_start(scratch["xs"][bass.ds(at + e * CAP, GR), :]
                             .rearrange("(t p) d -> p t d", p=P), zeros[:, :, :]).then_inc(padded, 16)
            sp.wait_ge(padded, 16 * NE)

    w_raw = sb("we_raw", [P, 3, KD * I])
    w_hi = sb("we_hi", [P, 2, 3, KD * I], F32R)
    w_lo = sb("we_lo", [P, 2, 3, KD * I], F32R)
    x_raw = sb("x_raw", [P, 2, GT, D])
    x_hi = sb("x_hi", [P, 2, KD, GR], F32R)
    x_lo = sb("x_lo", [P, 2, KD, GR], F32R)
    silu = sb("silu", [P, 2, GR])
    u_f = sb("u_f", [P, 2, GR])
    u_hi = sb("u_hi", [P, KI, GR], F32R)
    u_lo = sb("u_lo", [P, KI, GR], F32R)
    eo = sb("eo_sb", [P, GT, D])
    raw_in = [sem(f"raw_in{c}") for c in range(3)]
    x_in = [sem("x_in0"), sem("x_in1")]
    whi_made = sem("whi_made")
    wlo_made = sem("wlo_made")
    xt_mm = sem("xt_mm")
    xhi_made = sem("xhi_made")
    xlo_made = sem("xlo_made")
    up_mm = sem("up_mm")
    silu_made = sem("silu_made")
    u_made = sem("u_made")
    uhi_made = sem("uhi_made")
    ulo_made = sem("ulo_made")
    down_kt = sem("down_kt")
    eo_made = sem("eo_made")
    eo_out = sem("eo_out")

    def wait(eng, s, value):
        if not isinstance(value, int) or value > 0:
            eng.wait_ge(s, value)

    def over_steps(eng, body, prologue=None):
        for k in range(2):
            body(0, k, False)
        with eng.Fori(1, STEPS // 2 - 1) as i:
            for k in range(2):
                body(i, k, False)
        for k in range(2):
            body(STEPS // 2 - 1, k, k == 1)

    with nc.Block() as block:
        @block.sync
        def _(sp):
            def body(i, k, last):
                n = i * 2 + k
                e = sp.value_load(table[0:1, 0, bass.ds(n, 1)], min_val=0, max_val=NE - 1)
                r = sp.value_load(table[0:1, 1, bass.ds(n, 1)], min_val=0, max_val=NE * CAP - GR)
                wait(sp, xt_mm, n * 2 - 2)
                sp.dma_start(x_raw[:, k], scratch["xs"][bass.ds(r, GR), :]
                             .rearrange("(t p) d -> p t d", p=P)).then_inc(x_in[k], 16)
                for c in range(3):
                    wait(sp, wlo_made, n * 3 - 2 + c)
                    sp.dma_start(w_raw[:, c], A["experts_w"][bass.ds(e, 1), c]
                                 .rearrange("o p n -> (o p) n")).then_inc(raw_in[c], 16)

            over_steps(sp, body)

        @block.vector
        def _(dve):
            def split(n, k, c):
                wait(dve, raw_in[c], n * 16 + 16)
                if c == 2:
                    wait(dve, down_kt, n * KI - KI)
                dve.tensor_copy(w_hi[:, k, c], w_raw[:, c]).then_inc(whi_made, 1)
                wait(dve, whi_made, n * 3 + c + 1)
                dve.tensor_tensor(w_lo[:, k, c], w_raw[:, c], w_hi[:, k, c].bitcast(F32),
                                  ALU.subtract).then_inc(wlo_made, 1)

            def lo_of_x(n, k, mt):
                wait(dve, xhi_made, n * 2 + mt + 1)
                dve.tensor_tensor(x_lo[:, k, mt], ps[:, 7, 0:GR], x_hi[:, k, mt].bitcast(F32),
                                  ALU.subtract).then_inc(xlo_made, 1)

            lo_of_x(0, 0, 0)
            lo_of_x(0, 0, 1)
            for c in range(3):
                split(0, 0, c)

            def body(i, k, last):
                n = i * 2 + k
                for it in range(KI):
                    slot = (k + it) % 2
                    wait(dve, silu_made, n * KI + it + 1)
                    wait(dve, up_mm, n * (2 * KI) + 2 * it + 2)
                    wait(dve, ulo_made, n * KI + it - 1)
                    dve.tensor_tensor(u_f[:, slot], ps[:, 2 * slot + 1, 0:GR], silu[:, slot],
                                      ALU.mult).then_inc(u_made, 1)
                    if last:
                        continue
                    if it % 2 and it < 6:
                        split(n + 1, 1 - k, it // 2)
                    if it in (3, 5):
                        lo_of_x(n + 1, 1 - k, (it - 3) // 2)

            over_steps(dve, body)

        @block.gpsimd
        def _(pool):
            def body(i, k, last):
                n = i * 2 + k
                for it in range(KI):
                    slot = (k + it) % 2
                    wait(pool, uhi_made, n * KI + it + 1)
                    pool.tensor_tensor(u_lo[:, it], u_f[:, slot], u_hi[:, it].bitcast(F32),
                                       ALU.subtract).then_inc(ulo_made, 1)

            over_steps(pool, body)

        @block.scalar
        def _(act):
            def hi_of_x(n, k, mt):
                wait(act, xt_mm, n * 2 + mt + 1)
                act.activation(x_hi[:, k, mt], ps[:, 7, 0:GR], ACT.Copy).then_inc(xhi_made, 1)

            def hi_of_u(n, k, it):
                wait(act, u_made, n * KI + it + 1)
                wait(act, down_kt, n * KI + it + 1 - KI)
                act.activation(u_hi[:, it], u_f[:, (k + it) % 2], ACT.Copy).then_inc(uhi_made, 1)

            def put_out(n):
                wait(act, down_kt, n * KI + KI)
                wait(act, eo_out, n * 16)
                act.activation(eo[:, :, :], ps[:, 4:4 + GT, 0:D], ACT.Copy).then_inc(eo_made, 1)
                wait(act, eo_made, n + 1)
                act.dma_start(scratch["eo"][bass.ds(n * GR, GR), :].rearrange("(t p) d -> p t d", p=P),
                              eo[:, :, :]).then_inc(eo_out, 16)

            hi_of_x(0, 0, 0)
            hi_of_x(0, 0, 1)

            def body(i, k, last):
                n = i * 2 + k
                for it in range(KI):
                    slot = (k + it) % 2
                    wait(act, up_mm, n * (2 * KI) + 2 * it + 1)
                    wait(act, u_made, n * KI + it - 1)
                    act.activation(silu[:, slot], ps[:, 2 * slot, 0:GR], ACT.Silu) \
                        .then_inc(silu_made, 1)
                    if it:
                        hi_of_u(n, k, it - 1)
                    if it == 1 and not (isinstance(n, int) and n == 0):
                        put_out(n - 1)
                    if it in (3, 5) and not last:
                        hi_of_x(n + 1, 1 - k, (it - 3) // 2)
                hi_of_u(n, k, KI - 1)

            over_steps(act, body)
            put_out(STEPS - 1)
            act.wait_ge(eo_out, 16 * STEPS)

        @block.tensor
        def _(pe):
            def turn_rows(i, n, k, mt):
                if mt == 0:
                    wait(pe, x_in[k], i * 16 + 16)
                wait(pe, xlo_made, n * 2 + mt)
                for t in range(GT):
                    ins = pe.transpose(ps[:, 7, t * P:(t + 1) * P],
                                       x_raw[:, k, t, mt * P:(mt + 1) * P], ident[:, :])
                ins.then_inc(xt_mm, 1)

            def up(n, k, it):
                slot = (k + it) % 2
                wait(pe, u_made, n * KI + it - 1)
                for c in range(2):
                    if it == 0:
                        wait(pe, wlo_made, n * 3 + c + 1)
                    cut = lambda part, kt: part[:, k, c, kt * I + it * P:kt * I + (it + 1) * P]
                    terms = [t for kt in range(KD)
                             for t in split_products(cut(w_hi, kt), cut(w_lo, kt),
                                                     x_hi[:, k, kt], x_lo[:, k, kt])]
                    for m, (left, right) in enumerate(terms):
                        ins = pe.matmul(ps[:, 2 * slot + c, 0:GR], left, right, start=m == 0,
                                        stop=m == len(terms) - 1)
                    ins.then_inc(up_mm, 1)

            def down(n, k, it):
                if it == 0:
                    wait(pe, wlo_made, n * 3 + 3)
                    wait(pe, eo_made, n)
                wait(pe, ulo_made, n * KI + it + 1)
                w2 = slice(it * D, (it + 1) * D)
                for t in range(GT):
                    rows = slice(t * P, (t + 1) * P)
                    terms = split_products(u_hi[:, it, rows], u_lo[:, it, rows],
                                           w_hi[:, k, 2, w2], w_lo[:, k, 2, w2])
                    for m, (left, right) in enumerate(terms):
                        ins = pe.matmul(ps[:, 4 + t, 0:D], left, right, start=it == 0 and m == 0,
                                        stop=it == KI - 1 and m == len(terms) - 1)
                ins.then_inc(down_kt, 1)

            turn_rows(0, 0, 0, 0)
            turn_rows(0, 0, 0, 1)

            def body(i, k, last):
                n = i * 2 + k
                wait(pe, xlo_made, n * 2 + 2)
                for it in range(KI):
                    up(n, k, it)
                    if it >= 2:
                        down(n, k, it - 2)
                    if it in (2, 4) and not last:
                        turn_rows(i + k, n + 1, 1 - k, (it - 2) // 2)
                down(n, k, KI - 2)
                down(n, k, KI - 1)

            over_steps(pe, body)


def combine_phase(nc, ctx, A, scratch, out):
    sb = lambda name, shape, dt=F32: ctx.enter_context(nc.sbuf_tensor(name, shape, dt))
    sem = lambda name: ctx.enter_context(nc.semaphore(name))
    topv, slots, tanh_g = A["topv"], A["picks"], A["tanh_g"]
    share = sb("share", [P, 4, B * QT])
    tmp = sb("share_tmp", [P, 2, B * QT])
    picked = sb("picked", [P, 2, 2, QT, D])
    res = sb("res_sb", [P, 2, QT, D])
    picked_in = [sem("picked_in0"), sem("picked_in1")]
    res_in = [sem("res_in0"), sem("res_in1")]
    gap_made, exp_made, share_made, sum_made, out_sent = (
        sem(n) for n in ("gap_made", "share_exp", "share_made", "sum_made", "out_sent"))

    with nc.Block() as block:
        @block.sync
        def _(sp):
            for b in range(B):
                if b >= 2:
                    sp.wait_ge(out_sent, 16 * (b - 1))
                sp.dma_start(res[:, b % 2], scratch["res"][b]).then_inc(res_in[b % 2], 16)
                if b:
                    sp.wait_ge(sum_made, 2 * QT * b)
                    sp.dma_start(out[b - 1], res[:, (b - 1) % 2]).then_inc(out_sent, 16)
            sp.wait_ge(sum_made, 2 * QT * B)
            sp.dma_start(out[B - 1], res[:, (B - 1) % 2]).then_inc(out_sent, 16)
            sp.wait_ge(out_sent, 16 * B)

        @block.gpsimd
        def _(pool):
            for b in range(B):
                if b >= 2:
                    pool.wait_ge(sum_made, 2 * QT * (b - 1))
                for m in range(2 * QT):
                    n = 2 * QT * b + m
                    pool.indirect_dma_start(
                        out=picked[:, b % 2, m // QT, m % QT], out_offset=None, in_=scratch["eo"],
                        in_offset=bass.IndirectOffsetOnAxis(ap=slots[:, n:n + 1], axis=0)) \
                        .then_inc(picked_in[b % 2], 16)

        @block.scalar
        def _(act):
            act.wait_ge(gap_made, 1)
            act.activation(tmp[:, 1], tmp[:, 0], ACT.Exp).then_inc(exp_made, 1)

        @block.vector
        def _(dve):
            dve.tensor_tensor(tmp[:, 0], topv[:, :, 1], topv[:, :, 0], ALU.subtract) \
                .then_inc(gap_made, 1)
            dve.wait_ge(exp_made, 1)
            dve.tensor_scalar(share[:, 0], tmp[:, 1], 1.0, None, ALU.add).then_inc(share_made, 1)
            dve.wait_ge(share_made, 1)
            dve.reciprocal(share[:, 1], share[:, 0]).then_inc(share_made, 1)
            dve.wait_ge(share_made, 2)
            dve.tensor_scalar(share[:, 2], share[:, 1], tanh_g[:, 1:2], None, ALU.mult) \
                .then_inc(share_made, 1)
            dve.wait_ge(share_made, 3)
            dve.tensor_tensor(share[:, 3], share[:, 2], tmp[:, 1], ALU.mult).then_inc(share_made, 1)
            dve.wait_ge(share_made, 4)
            for b in range(B):
                k = b % 2
                dve.wait_ge(res_in[k], 16 * (b // 2 + 1))
                dve.wait_ge(picked_in[k], 16 * 2 * QT * (b // 2 + 1))
                for s in range(2):
                    if s:
                        dve.wait_ge(sum_made, QT * (2 * b + 1))
                    for qt in range(QT):
                        n = QT * b + qt
                        dve.scalar_tensor_tensor(res[:, k, qt], picked[:, k, s, qt],
                                                 share[:, 2 + s, n:n + 1], res[:, k, qt],
                                                 ALU.mult, ALU.add).then_inc(sum_made, 1)


def build(nc, A, out):
    with ExitStack() as ctx:
        sb = lambda name, shape, dt=F32: ctx.enter_context(nc.sbuf_tensor(name, shape, dt))
        A["ident"] = sb("ident", [P, P])
        A["tanh_g"] = sb("tanh_g", [P, 2])
        A["topv"] = sb("topv", [P, B * QT, 2])
        A["slots"] = sb("slots", [P, B * 2 * QT])
        A["picks"] = sb("picks_at", [P, B * 2 * QT], U32)
        A["experts"] = sb("experts", [P, NE])
        A["first_row"] = sb("first_row", [P, NE])
        A["running"] = sb("running", [P, QT + 1, NE])
        xs = nc.dram_tensor("xs", [NE * CAP, D], F32).ap()
        eo = nc.dram_tensor("eo", [STEPS * GR, D], F32).ap()
        res = nc.dram_tensor("res", [B, P, QT, D], F32).ap()
        scratch = {"xs": xs, "eo": eo, "res": res}
        with ExitStack() as phase:
            mixer_phase(nc, phase, A, scratch)
        with ExitStack() as phase:
            expert_phase(nc, phase, A, scratch)
        with ExitStack() as phase:
            combine_phase(nc, phase, A, scratch, out)


def kernel(**inputs):
    import numpy as np
    import concourse.bacc as bacc
    from concourse.bass_utils import run_bass_kernel_spmd

    nc = bacc.Bacc("TRN2", target_bir_lowering=False, num_devices=1)
    arrays, A = {}, {}

    def give(name, a):
        a = np.ascontiguousarray(a)
        arrays["in_" + name] = a
        A[name] = nc.dram_tensor("in_" + name, a.shape, mybir.dt.from_np(a.dtype),
                                 kind="ExternalInput").ap()

    def stack(w):
        return w.reshape(-1, P, w.shape[1]).transpose(1, 0, 2)

    X = {k[len("L0_xattn_"):]: np.asarray(v) for k, v in inputs.items() if k.startswith("L0_xattn_")}
    tokens = lambda a: np.asarray(a).reshape(B, QT, P, D).transpose(0, 2, 1, 3)
    give("x", tokens(inputs["x"]))
    give("ctx", tokens(inputs["ctx_1024"]))
    give("mask", np.asarray(inputs["mask_Bx1x1xS2_ff0"]).reshape(B, 1, S))
    give("attn_w", np.stack([stack(X[a + n + "_w"])
                             for a in "cs" for n in "qkvo"], axis=1))
    E1, E2, E3 = (np.asarray(inputs["L0_ffn_w" + n]) for n in "123")
    lay = lambda w: w.reshape(NE, -1, P, w.shape[2]).transpose(0, 2, 1, 3).reshape(NE, P, -1)
    give("experts_w", np.stack([lay(E1.transpose(0, 2, 1)), lay(E3.transpose(0, 2, 1)),
                                lay(E2.transpose(0, 2, 1))], axis=1))
    give("fi_w", stack(X["fi_w"]))
    give("fo_w", stack(X["fo_w"]))
    give("gate_w", stack(np.asarray(inputs["L0_ffn_gate_w"]).T))
    give("cols", np.concatenate([X[a + n + "_b"].reshape(KD, P)
                                 for a in "cs" for n in "kq"] + [X["fi_b"].reshape(KF, P)]).T)
    for n in ROW_NAMES:
        give(n, X[n] if n != "rms" else inputs["L0_ffn_rms_weight"])
    give("g_xattn", inputs["g_xattn"])
    give("g_ffn", inputs["g_ffn"])
    out = nc.dram_tensor("out", [B, P, QT, D], F32, kind="ExternalOutput").ap()
    build(nc, A, out)
    r = run_bass_kernel_spmd(nc, [arrays], core_ids=[0])
    return r.results[0]["out"].transpose(0, 2, 1, 3).reshape(B, S, D)
```

```python
import concourse.bass as bass
from concourse import mybir
from contextlib import ExitStack

F32 = mybir.dt.float32
F32R = mybir.dt.float32r
BF16 = mybir.dt.bfloat16
U32 = mybir.dt.uint32
I32 = mybir.dt.int32
ALU = mybir.AluOpType
ACT = mybir.ActivationFunctionType
AX = mybir.AxisListType

P = 128
B, S, D = 8, 512, 256
H, DH = 16, 16
F = 1024
I = 896
NE = 8
QT = S // P
KD = D // P
KF = F // P
NP_ = H // 2
G = 4
NG = H // G
HALF = P // 2
SCALE = 1.0 / 4.0
LN_EPS = 1e-5
RMS_EPS = 1e-6
KI = I // P
GT = 3
GR = GT * P
T = B * S
STEPS = (2 * T + NE * (GR - 1)) // GR
STEPS += STEPS % 2
CAP = T + GR
ROW_MASK = 2 * 3 * DH
ROW_MAX = ROW_MASK + 2
SLOTS = NG * 2 * QT
LEAD = 18
ATTN_ROWS = ["cv_b", "co_b", "co_g", "co_be", "sv_b", "so_b", "so_g", "so_be"]
GELU_ROWS = ["fo_b", "fo_g", "fo_be", "rms"]
LN_STEPS = ("stats", "aggr", "var", "root", "normed")
PERIOD_ITEMS = [["stk3"], ["stq3"], [">ctx0"], ["<at3"], ["stk4"], ["stq4"], [">ctx1"],
                ["<tb1", "nm1"], ["stk5"], ["stq5"], ["<o0"], ["<o1", "at0"], ["stk6"],
                ["stq6", ">in0"], [">in1"], ["nm2"], ["stk7", ">k0"], ["stq7", ">q0"], [">k1"],
                ["at1"], [">stk0"], [">stq0"], [">q1"], ["tb0", "nm3"], [">stk1"], [">stq1"],
                [">v0"], ["at2"], [">stk2"], [">stq2"], [">v1"], [">nm0"]]
START_ITEMS = ["ctx0", "ctx1", "in0", "in1", "k0", "q0", "k1", "q1", "v0", "stk0", "stq0", "stk1",
               "stq1", "stk2", "stq2", "v1", "nm0"]
START_MAXIMA = {"stq1": range(0, 8), "v1": range(8, LEAD)}
END_ITEMS = ["at3", "tb1", "o0", "o1"]
LATE_ITEMS = ("ctx", "in", "tb", "k", "q", "nm")
MISC_BANKS = (6, 7)


def period_banks(before, after):
    n, slots = 0, []
    for names in PERIOD_ITEMS:
        slots.append([])
        for name in names:
            if name[0] == "<" and not before or name[0] == ">" and not after:
                continue
            if name.startswith(">ctx") and not after[0]:
                continue
            slots[-1].append((name, MISC_BANKS[n % 2]))
            n += 1
    return slots


def start_banks(cross):
    names = START_ITEMS if cross else START_ITEMS[2:]
    return [(name, MISC_BANKS[(n + 1) % 2]) for n, name in enumerate(names)]


def end_banks():
    return [(name, MISC_BANKS[(n + 1) % 2]) for n, name in enumerate(END_ITEMS)]


def split_products(hi_l, lo_l, hi_r, lo_r):
    return [(hi_l, hi_r), (hi_l, lo_r), (lo_l, hi_r)]




def attention_phase(nc, ctx, A, scratch):
    sb = lambda name, shape, dt=F32: ctx.enter_context(nc.sbuf_tensor(name, shape, dt))
    sem = lambda name: ctx.enter_context(nc.semaphore(name))
    ident = A["ident"]
    w_hi = sb("w_hi", [P, 8, KD, D], F32R)
    w_lo = sb("w_lo", [P, 8, KD, D], F32R)
    rows = {n: sb("row_" + n, [P, D]) for n in ATTN_ROWS}
    cols = sb("cols", [P, 4 * KD])
    col_of = lambda l, what, mt: cols[:, 4 * l + 2 * what + mt:4 * l + 2 * what + mt + 1]
    choose = sb("choose", [P, 4, 2, 2, P], F32R)
    choose_mask = sb("choose_mask", [P, P], F32R)
    stack_cols = sb("stack_cols", [P, 7])
    keep = lambda half: stack_cols[:, half:half + 1]
    k_ones = lambda j: stack_cols[:, 2 + j:3 + j]
    q_ones = stack_cols[:, 6:7]
    K, V, O = 1, 2, 3
    neg_half = sb("neg_half", [P, QT])

    with nc.sbuf_tensor("w_raw", [P, 8, KD, D], F32) as w_raw, \
            nc.sbuf_tensor("choose_raw", [P, 4, 2, 2, P], F32) as choose_raw, \
            nc.sbuf_tensor("choose_mask_raw", [P, P], F32) as choose_mask_raw, \
            nc.semaphore("weights_in") as weights_in, nc.semaphore("hi_made") as hi_made, \
            nc.Block() as block:
        @block.sync
        def _(sp):
            sp.dma_start(w_raw[:, :, :, :], A["attn_w"]).then_inc(weights_in, 16)
            sp.dma_start(cols[:, :], A["cols"]).then_inc(weights_in, 16)
            sp.dma_start(choose_raw[:, :, :, :, :], A["choose"]).then_inc(weights_in, 16)
            sp.dma_start(choose_mask_raw[:, :], A["choose_mask"]).then_inc(weights_in, 16)
            sp.dma_start(stack_cols[:, :], A["stack_cols"]).then_inc(weights_in, 16)
            for n in ATTN_ROWS:
                sp.dma_start(rows[n][:, :], A[n].partition_broadcast(P)).then_inc(weights_in, 16)
            sp.wait_ge(weights_in, 16 * (5 + len(ATTN_ROWS)))

        @block.vector
        def _(dve):
            dve.memset(neg_half[:, :], -0.5)
            dve.wait_ge(weights_in, 16 * (5 + len(ATTN_ROWS)))
            dve.tensor_copy(choose[:, :, :, :, :], choose_raw[:, :, :, :, :])
            dve.tensor_copy(choose_mask[:, :], choose_mask_raw[:, :])
            for j in range(8):
                dve.tensor_copy(w_hi[:, j], w_raw[:, j]).then_inc(hi_made, 1)
            for j in range(0, 8, 2):
                dve.wait_ge(hi_made, j + 1)
                dve.tensor_tensor(w_lo[:, j], w_raw[:, j], w_hi[:, j].bitcast(F32), ALU.subtract)

        @block.gpsimd
        def _(pool):
            for j in range(1, 8, 2):
                pool.wait_ge(hi_made, j + 1)
                pool.tensor_tensor(w_lo[:, j], w_raw[:, j], w_hi[:, j].bitcast(F32), ALU.subtract)

    kz = sb("kz", [P, NP_, 2, S], F32R)
    qst = sb("qst", [P, NP_, S], F32R)
    parts = sb("parts", [P, 4, KD, S], F32R)
    k_hi, k_lo, q_hi, q_lo = (parts[:, n] for n in range(4))
    probs = sb("probs", [P, 8, S])
    vaug = sb("vaug", [P, 2, QT, H, 2 * DH])
    mask_raw = sb("mask_raw", [HALF, S])
    mask_z = sb("mask_z", [P, S], F32R)
    a_hi = sb("a_hi", [P, KD, S], F32R)
    a_lo = sb("a_lo", [P, KD, S], F32R)
    ctx_hi = sb("ctx_hi", [P, KD, S], F32R)
    ctx_lo = sb("ctx_lo", [P, KD, S], F32R)
    c_hi = sb("c_hi", [P, KD, S], F32R)
    c_lo = sb("c_lo", [P, KD, S], F32R)
    x_tok = sb("x_tok", [P, QT, D])
    ctx_tok = sb("ctx_tok", [P, QT, D])
    x1_tok = sb("x1_tok", [P, QT, D])
    resid = sb("resid", [P, 2, QT, D])
    at_tok = sb("at_tok", [P, QT, D])
    sum_tok = sb("sum_tok", [P, QT, D])
    ev = sb("ev", [P, S])
    nraw = sb("nraw", [P, 2, QT, G])
    nz = sb("nz", [P, 2, QT, 32], F32R)
    stats = sb("stats", [P, 2, QT, 6])
    mv = sb("mv", [P, 2, QT, 2])
    var_eps = sb("var_eps", [P, 2, QT])
    rstd = sb("rstd", [P, 2, QT])
    settled = sb("settled", [P, 1])
    rden = sb("rden", [P, QT, G])
    ps = ctx.enter_context(nc.psum_tensor("ps", [P, 8, S], F32))
    SCORE, MAXIMA, OUT, MISC = 0, 3, 5, 6

    with nc.semaphore("cleared") as cleared, nc.Block() as block:
        @block.vector
        def _(dve):
            dve.memset(mask_z[:, :].bitcast(F32), 0.0)
            dve.memset(mask_raw[:, :], 0.0)
            dve.memset(nz[:, :, :, :].bitcast(F32), 0.0)
            dve.memset(vaug[:, :, :, :, :], 0.0).then_inc(cleared, 1)
            dve.wait_ge(cleared, 1)
            dve.memset(vaug[:, :, :, :, DH:DH + 1], 1.0)

    x_in, ctx_in, mask_in = sem("x_in"), sem("ctx_in"), sem("mask_in")
    mask_made = sem("mask_made")
    x_stats, x_aggr, x_var, x_root, x_normed = (sem("x_" + n) for n in LN_STEPS)
    tr_ctx, ctx_hi_made, ctx_lo_made = sem("tr_ctx"), sem("ctx_hi_made"), sem("ctx_lo_made")
    stored = sem("stored")
    tr_in, in_hi_made, in_lo_made = sem("tr_in"), sem("in_hi_made"), sem("in_lo_made")
    qk_mm, qk_hi_made, qk_lo_made = sem("qk_mm"), sem("qk_hi_made"), sem("qk_lo_made")
    v_mm, v_made = sem("v_mm"), sem("v_made")
    sel_mm = sem("sel_mm")
    kz_made = sem("kz_made")
    qst_made = sem("qst_made")
    max_mm, max_made = sem("max_mm"), sem("max_made")
    nm_hi_made, nm_lo_made, nm_tr = sem("nm_hi_made"), sem("nm_lo_made"), sem("nm_tr")
    nm_even, nm_odd = sem("nm_even"), sem("nm_odd")
    score_mm, exp_made = sem("score_mm"), sem("exp_made")
    pv_mm = sem("pv_mm")
    ev_made, at_tr, rden_made, at_norm = (sem(n) for n in
                                          ("ev_made", "at_tr", "rden_made", "at_norm"))
    tb_mm, c_hi_made, c_lo_made = sem("tb_mm"), sem("c_hi_made"), sem("c_lo_made")
    o_mm, sum_made = sem("o_mm"), sem("sum_made")
    res_made, gain_made, shift_made = sem("res_made"), sem("gain_made"), sem("shift_made")
    t_stats, t_aggr, t_var, t_root, t_normed = (sem("t_" + n) for n in LN_STEPS)

    def wait(eng, s, value):
        if not isinstance(value, int) or value > 0:
            eng.wait_ge(s, value)

    def run(eng, start, period, end):
        cross, own = True, False
        start(0, cross, 0)
        period(0, 0, (cross, 0), None, (cross, 1))
        period(1, 1, (cross, 1), (cross, 0), None)
        start(2, own, 0)
        with eng.Fori(1, B - 1) as i:
            period(i * 2, 0, (own, i - 1), (cross, i), (cross, i + 1))
            period(i * 2 + 1, 1, (cross, i + 1), (own, i - 1), (own, i))
        period(2 * B - 2, 0, (own, B - 2), (cross, B - 1), None)
        start(2 * B - 1, own, B - 1)
        period(2 * B - 1, 1, (own, B - 1), (own, B - 2), None)
        end(2 * B - 1, own, B - 1)

    def unit_of(cross, b):
        if not cross:
            return b * 2 + 2
        return 0 if isinstance(b, int) and b == 0 else b * 2 - 1

    def whose(name, u, now, before, after):
        step = {"<": -1, ">": 1}.get(name[0], 0)
        return (u + step if step else u, *(now, after, before)[step])

    with nc.Block() as block:

        @block.sync
        def _(sp):
            sp.sem_inc(stored, 1)

            def load(u, cross, b):
                if not cross:
                    return
                if not (isinstance(b, int) and b == 0):
                    wait(sp, res_made, unit_of(True, b - 1) + 1)
                sp.dma_start(x_tok[:, :, :], A["x"][b]).then_inc(x_in, 16)
                wait(sp, tr_ctx, b * KD)
                sp.dma_start(ctx_tok[:, :, :], A["ctx"][b]).then_inc(ctx_in, 16)
                for row in (0, 32):
                    wait(sp, mask_made, b * 2)
                    sp.dma_start(mask_raw[row:row + 1, :], A["mask"][b]).then_inc(mask_in, 16)

            def store(u, cross, b):
                if not cross:
                    wait(sp, shift_made, u + 1)
                    sp.dma_start(scratch["x2"][b], sum_tok[:, :, :]).then_inc(stored, 16)

            def period(u, par, now, before, after):
                if after:
                    load(u + 1, *after)
                if before:
                    store(u - 1, *before)

            run(sp, load, period, store)
            sp.wait_ge(stored, 16 * B + 1)

        @block.gpsimd
        def _(pool):
            def root(n, var, done, count):
                wait(pool, var, count)
                pool.tensor_tensor(rstd[:, n], var_eps[:, n], neg_half[:, :], ALU.pow) \
                    .then_inc(done, 1)

            def row(name):
                return rows[name][:, :].unsqueeze(1).to_broadcast([P, QT, D])

            def start_early(u, cross, b):
                if not cross:
                    return
                root(0, x_var, x_root, b + 1)
                wait(pool, x_root, b + 1)
                wait(pool, mask_made, b * 2 + 1)
                pool.tensor_tensor(mask_z[32:33, :], mask_raw[32:33, :],
                                   mask_z[32:33, :].bitcast(F32), ALU.subtract) \
                    .then_inc(mask_made, 1)
                wait(pool, mask_made, b * 2 + 2)

            def residual(u, cross, b, par):
                wait(pool, tr_in, u * KD + KD)
                wait(pool, sum_made, u * 2 - 2)
                pool.tensor_tensor(resid[:, par], (x_tok if cross else x1_tok)[:, :, :],
                                   row("co_b" if cross else "so_b"), ALU.add).then_inc(res_made, 1)

            def finish(u, cross, b):
                wait(pool, t_normed, u * QT + QT)
                pool.tensor_tensor(sum_tok[:, :, :], sum_tok[:, :, :], row("co_g" if cross else "so_g"),
                                   ALU.mult).then_inc(gain_made, 1)
                wait(pool, gain_made, u + 1)
                if cross:
                    if not (isinstance(u, int) and u == 0):
                        wait(pool, tr_in, u * KD + 2 * KD)
                    pool.tensor_tensor(x1_tok[:, :, :], sum_tok[:, :, :], row("co_be"), ALU.add) \
                        .then_inc(shift_made, 1)
                else:
                    pool.tensor_tensor(sum_tok[:, :, :], sum_tok[:, :, :], row("so_be"), ALU.add) \
                        .then_inc(shift_made, 1)

            def start(u, cross, b):
                start_early(u, cross, b)
                residual(u, cross, b, u % 2)

            def end(u, cross, b):
                root(1, t_var, t_root, u + 1)
                finish(u, cross, b)

            def period(u, par, now, before, after):
                if after:
                    start_early(u + 1, *after)
                if before:
                    root(1, t_var, t_root, u)
                if after:
                    residual(u + 1, *after, 1 - par)
                if before:
                    finish(u - 1, *before)

            run(pool, start, period, end)

        @block.scalar
        def _(act):
            def high(dst, done, src_bank, ready, count, bias=None):
                wait(act, ready, count)
                if bias is None:
                    act.activation(dst, ps[:, src_bank], ACT.Copy).then_inc(done, 1)
                else:
                    act.activation(dst, ps[:, src_bank], ACT.Identity, bias=bias).then_inc(done, 1)

            def item(name, bank, u, cross, b):
                kind, n = name[:-1], int(name[-1])
                if kind == "ctx":
                    high(ctx_hi[:, n], ctx_hi_made, bank, tr_ctx, b * KD + n + 1)
                elif kind == "in":
                    high(a_hi[:, n], in_hi_made, bank, tr_in, u * KD + n + 1)
                elif kind == "tb":
                    high(c_hi[:, n], c_hi_made, bank, tb_mm, u * KD + n + 1)
                elif kind in ("k", "q"):
                    what = "kq".index(kind)
                    high((k_hi, q_hi)[what][:, n], qk_hi_made, bank, qk_mm, u * 4 + 2 * n + what + 1,
                         col_of(0 if cross else 1, what, n))
                elif kind == "nm":
                    wait(act, nm_tr, u * NG + n + 1)
                    act.activation(qst[96:P, 2 * n], ps[96:P, bank], ACT.Identity,
                                   bias=q_ones[96:P, :]).then_inc(nm_even, 1)
                elif kind == "stk":
                    wait(act, sel_mm, u * (2 * NP_) + 2 * n + 1)
                    for half in range(2):
                        act.activation(kz[:, n, half], ps[:, bank], ACT.Identity,
                                       bias=k_ones(2 * (n % 2) + half), scale=keep(half)) \
                            .then_inc(kz_made, 1)

            def split_mask(b):
                wait(act, mask_in, b * 32 + 32)
                if not (isinstance(b, int) and b == 0):
                    wait(act, sel_mm, unit_of(True, b - 1) * (2 * NP_) + 2 * NP_)
                act.activation(mask_z[0:33, :], mask_raw[0:33, :], ACT.Copy).then_inc(mask_made, 1)

            def start(u, cross, b):
                if cross:
                    split_mask(b)
                for name, bank in start_banks(cross):
                    item(name, bank, u, cross, b)

            def outputs(u, g):
                wait(act, pv_mm, u * (NG * QT) + QT * g + QT)
                act.activation(ev[:, :], ps[:, OUT], ACT.Copy).then_inc(ev_made, 1)

            def end(u, cross, b):
                outputs(u, NG - 1)
                for name, bank in end_banks():
                    item(name, bank, u, cross, b)

            def period(u, par, now, before, after):
                banks = period_banks(before, after)
                for s in range(SLOTS):
                    for half in range(2):
                        e = 2 * s + half
                        wait(act, score_mm, u * 64 + e + 1)
                        wait(act, pv_mm, u * (NG * QT) + (e - 8) // 4 + 1)
                        act.activation(probs[:, e % 8], ps[:, SCORE + e % 3], ACT.Exp,
                                       scale=SCALE).then_inc(exp_made, 1)
                    if s == (4 if before else 18) and after and after[0]:
                        split_mask(after[1])
                    if s % 8 == 1 and (s > 8 or before):
                        outputs(u if s > 8 else u - 1, (s // 8 - 1) % NG)
                    for name, bank in banks[s]:
                        item(name.strip("<>"), bank, *whose(name, u, now, before, after))

            run(act, start, period, end)

        @block.vector
        def _(dve):
            def low(dst, done, bank, high, ready, count, bias=None):
                wait(dve, ready, count)
                if bias is None:
                    dve.tensor_tensor(dst, ps[:, bank], high.bitcast(F32), ALU.subtract) \
                        .then_inc(done, 1)
                else:
                    dve.scalar_tensor_tensor(dst, ps[:, bank], bias, high.bitcast(F32), ALU.add,
                                             ALU.subtract).then_inc(done, 1)

            def item(name, bank, u, cross, b, par):
                kind, n = name[:-1], int(name[-1])
                if kind == "ctx":
                    low(ctx_lo[:, n], ctx_lo_made, bank, ctx_hi[:, n], ctx_hi_made, b * KD + n + 1)
                elif kind == "in":
                    low(a_lo[:, n], in_lo_made, bank, a_hi[:, n], in_hi_made, u * KD + n + 1)
                elif kind == "tb":
                    low(c_lo[:, n], c_lo_made, bank, c_hi[:, n], c_hi_made, u * KD + n + 1)
                elif kind in ("k", "q"):
                    what = "kq".index(kind)
                    low((k_lo, q_lo)[what][:, n], qk_lo_made, bank, (k_hi, q_hi)[what][:, n],
                        qk_hi_made, u * 4 + 2 * n + what + 1, col_of(0 if cross else 1, what, n))
                elif kind == "nm":
                    wait(dve, nm_even, u * NG + n + 1)
                    dve.tensor_scalar(qst[96:P, 2 * n + 1], ps[96:P, bank], q_ones[96:P, :], None,
                                      ALU.add).then_inc(nm_odd, 1)
                elif kind == "stq":
                    wait(dve, sel_mm, u * (2 * NP_) + 2 * n + 2)
                    dve.tensor_scalar(qst[:, n], ps[:, bank], q_ones, None, ALU.add) \
                        .then_inc(qst_made, 1)
                elif kind == "v":
                    wait(dve, v_mm, u * 2 + n + 1)
                    dve.tensor_tensor(
                        vaug[:, par, 2 * n:2 * n + 2, :, 0:DH],
                        ps[:, bank].rearrange("p (t h d) -> p t h d", t=2, d=DH),
                        rows["cv_b" if cross else "sv_b"][:, :].rearrange("p (h d) -> p h d", d=DH)
                        .unsqueeze(1).to_broadcast([P, 2, H, DH]), ALU.add).then_inc(v_made, 1)
                elif kind == "at":
                    wait(dve, at_tr, u * NG + n + 1)
                    src = ps[:, bank].rearrange("p (q j d) -> p q j d", q=QT, j=G)
                    wait(dve, at_norm, u * NG + n)
                    dve.reciprocal(rden[:, :, :], src[:, :, :, DH]).then_inc(rden_made, 1)
                    wait(dve, rden_made, u * NG + n + 1)
                    dve.tensor_tensor(
                        at_tok[:, :, G * DH * n:G * DH * (n + 1)].rearrange("p q (j d) -> p q j d", j=G),
                        src[:, :, :, 0:DH], rden[:, :, :].unsqueeze(3).to_broadcast([P, QT, G, DH]),
                        ALU.mult).then_inc(at_norm, 1)
                elif kind == "o":
                    wait(dve, o_mm, u * 2 + n + 1)
                    if n == 0:
                        wait(dve, res_made, u + 1)
                        wait(dve, shift_made, u)
                        if cross:
                            wait(dve, stored, b * 16 - 16 + 1)
                        elif isinstance(b, int) and b == B - 1:
                            wait(dve, stored, 16 * (B - 1) + 1)
                    dve.tensor_tensor(sum_tok[:, 2 * n:2 * n + 2],
                                      ps[:, bank].rearrange("p (t d) -> p t d", t=2),
                                      resid[:, par, 2 * n:2 * n + 2], ALU.add).then_inc(sum_made, 1)

            def moments(n, src, s_stats, s_aggr, s_var, count):
                for qt in range(QT):
                    dve.bn_stats(stats[:, n, qt], src[:, qt]).then_inc(s_stats, 1)
                wait(dve, s_stats, count * QT + QT)
                dve.tensor_copy(settled[:, :], stats[:, n, 0, 0:1])
                for qt in range(QT):
                    dve.bn_aggr(mv[:, n, qt], stats[:, n, qt]).then_inc(s_aggr, 1)
                wait(dve, s_aggr, count * QT + QT)
                dve.tensor_scalar(var_eps[:, n], mv[:, n, :, 1], LN_EPS, None, ALU.add) \
                    .then_inc(s_var, 1)

            def normalise(n, tok, s_root, s_normed, count):
                wait(dve, s_root, count + 1)
                for qt in range(QT):
                    dve.tensor_scalar(tok[:, qt], tok[:, qt], mv[:, n, qt, 0:1],
                                      rstd[:, n, qt:qt + 1], ALU.subtract, ALU.mult) \
                        .then_inc(s_normed, 1)

            def x_moments(b):
                wait(dve, x_in, b * 16 + 16)
                moments(0, x_tok, x_stats, x_aggr, x_var, b)

            def sum_moments(u):
                wait(dve, sum_made, u * 2 + 2)
                moments(1, sum_tok, t_stats, t_aggr, t_var, u)

            def reduce_max(u, m):
                wait(dve, max_mm, u * 64 + m + 1)
                g, j, qt = m // 16, m // 4 % 4, m % 4
                dve.tensor_reduce(nraw[:, g % 2, qt, j:j + 1], ps[:, MAXIMA + m % 2], AX.X, ALU.max,
                                  negate=True).then_inc(max_made, 1)

            def split_max(u, g):
                wait(dve, max_made, u * 64 + 16 * g + 16)
                dve.tensor_copy(nz[:, g % 2, :, 2:2 + G], nraw[:, g % 2]).then_inc(nm_hi_made, 1)
                wait(dve, nm_hi_made, u * NG + g + 1)
                dve.tensor_tensor(nz[:, g % 2, :, 2 + G:2 + 2 * G], nraw[:, g % 2],
                                  nz[:, g % 2, :, 2:2 + G].bitcast(F32), ALU.subtract) \
                    .then_inc(nm_lo_made, 1)

            def start(u, cross, b):
                if cross:
                    x_moments(b)
                    normalise(0, x_tok, x_root, x_normed, b)
                for name, bank in start_banks(cross):
                    if name == "nm0":
                        split_max(u, 0)
                    item(name, bank, u, cross, b, u % 2)
                    for m in START_MAXIMA.get(name, ()):
                        reduce_max(u, m)

            def end(u, cross, b):
                for name, bank in end_banks():
                    item(name, bank, u, cross, b, u % 2)
                sum_moments(u)
                normalise(1, sum_tok, t_root, t_normed, u)

            def period(u, par, now, before, after):
                banks = period_banks(before, after)
                late = []
                for s in range(SLOTS):
                    for name, bank in late:
                        item(name.strip("<>"), bank, *whose(name, u, now, before, after),
                             par if name[0] not in "<>" else 1 - par)
                    late = [n for n in banks[s] if n[0].strip("<>")[:-1] in LATE_ITEMS]
                    for m in (2 * s + LEAD, 2 * s + LEAD + 1):
                        if m < 64:
                            reduce_max(u, m)
                        elif after:
                            reduce_max(u + 1, m - 64)
                    if s % 8 == 6:
                        if s < 24:
                            split_max(u, s // 8 + 1)
                        elif after:
                            split_max(u + 1, 0)
                    for name, bank in banks[s]:
                        if (name, bank) not in late:
                            item(name.strip("<>"), bank, *whose(name, u, now, before, after),
                                 par if name[0] not in "<>" else 1 - par)
                    if after and after[0]:
                        if s == 1:
                            x_moments(after[1])
                        if s == 5:
                            normalise(0, x_tok, x_root, x_normed, after[1])
                    if before:
                        if s == 12:
                            sum_moments(u - 1)
                        if s == 14:
                            normalise(1, sum_tok, t_root, t_normed, u - 1)
                for name, bank in late:
                    item(name.strip("<>"), bank, *whose(name, u, now, before, after), 1 - par)

            run(dve, start, period, end)

        @block.tensor
        def _(pe):
            taken = {6: [], 7: []}

            def frees(name, u, b=None):
                kind, n = name[:-1], int(name[-1])
                return {"ctx": lambda: [(ctx_lo_made, b * KD + n + 1)],
                        "in": lambda: [(in_lo_made, u * KD + n + 1)],
                        "tb": lambda: [(c_lo_made, u * KD + n + 1)],
                        "k": lambda: [(qk_lo_made, u * 4 + 2 * n + 1)],
                        "q": lambda: [(qk_lo_made, u * 4 + 2 * n + 2)],
                        "v": lambda: [(v_made, u * 2 + n + 1)],
                        "stk": lambda: [(kz_made, u * (2 * NP_) + 2 * n + 2)],
                        "stq": lambda: [(qst_made, u * NP_ + n + 1)],
                        "nm": lambda: [(nm_even, u * NG + n + 1), (nm_odd, u * NG + n + 1)],
                        "at": lambda: [(at_norm, u * NG + n + 1)],
                        "o": lambda: [(sum_made, u * 2 + n + 1)]}[kind]()

            def turn(bank, src, mt):
                for qt in range(QT):
                    ins = pe.transpose(ps[:, bank, qt * P:(qt + 1) * P],
                                       src[:, qt, mt * P:(mt + 1) * P], ident[:, :])
                return ins

            def product(out, left, right):
                terms = [t for ls, rs in zip(left, right) for t in split_products(*ls, *rs)]
                for n, (l_, r_) in enumerate(terms):
                    ins = pe.matmul(out, l_, r_, start=n == 0, stop=n == len(terms) - 1)
                return ins

            def item(name, bank, u, cross, b):
                for s, count in taken[bank]:
                    wait(pe, s, count)
                taken[bank] = frees(name, u, b)
                kind, n = name[:-1], int(name[-1])
                l = 0 if cross else 1
                w = lambda which, k, c: (w_hi[:, 4 * l + which, k, c], w_lo[:, 4 * l + which, k, c])
                key_side = (ctx_hi, ctx_lo) if cross else (a_hi, a_lo)
                if kind == "ctx":
                    wait(pe, ctx_in, b * 16 + 16)
                    turn(bank, ctx_tok, n).then_inc(tr_ctx, 1)
                elif kind == "in":
                    if cross:
                        wait(pe, x_normed, b * QT + QT)
                    else:
                        wait(pe, shift_made, unit_of(True, b) + 1)
                    turn(bank, x_tok if cross else x1_tok, n).then_inc(tr_in, 1)
                elif kind in ("k", "q"):
                    side = key_side if kind == "k" else (a_hi, a_lo)
                    if n == 0:
                        wait(pe, in_lo_made, u * KD + KD)
                        if cross:
                            wait(pe, ctx_lo_made, b * KD + KD)
                    c = slice(n * P, (n + 1) * P)
                    product(ps[:, bank], [w("qk".index(kind), k, c) for k in range(KD)],
                            [(side[0][:, k], side[1][:, k]) for k in range(KD)]).then_inc(qk_mm, 1)
                elif kind == "v":
                    for t in range(2):
                        c = slice((2 * n + t) * P, (2 * n + t + 1) * P)
                        ins = product(ps[:, bank, t * D:(t + 1) * D],
                                      [(key_side[0][:, k, c], key_side[1][:, k, c]) for k in range(KD)],
                                      [w(V, k, slice(0, D)) for k in range(KD)])
                    ins.then_inc(v_mm, 1)
                elif kind in ("stk", "stq"):
                    what = "kq".index(kind[2])
                    hi_lo = ((k_hi, k_lo), (q_hi, q_lo))[what]
                    wait(pe, qk_lo_made, u * 4 + 2 * (n // 4) + what + 1)
                    masked = what == 0 and cross
                    if masked:
                        if n == 0:
                            wait(pe, mask_made, b * 2 + 2)
                        pe.matmul(ps[:, bank], choose_mask[:, :], mask_z[:, :], start=True, stop=False)
                    for t in range(2):
                        ins = pe.matmul(ps[:, bank], choose[:, n % 4, what, t], hi_lo[t][:, n // 4],
                                        start=t == 0 and not masked, stop=t == 1)
                    ins.then_inc(sel_mm, 1)
                elif kind == "nm":
                    wait(pe, nm_lo_made, u * NG + n + 1)
                    for qt in range(QT):
                        ins = pe.matmul(ps[96:P, bank, qt * P:(qt + 1) * P],
                                        nz[:, n % 2, qt].bitcast(F32), ident[:, :], start=True,
                                        stop=True, tile_position=(0, 96))
                    ins.then_inc(nm_tr, 1)
                elif kind == "at":
                    wait(pe, ev_made, u * NG + n + 1)
                    for qt in range(QT):
                        ins = pe.transpose(ps[:, bank, qt * P:(qt + 1) * P],
                                           ev[:, qt * P:(qt + 1) * P], ident[:, :])
                    ins.then_inc(at_tr, 1)
                elif kind == "tb":
                    wait(pe, at_norm, u * NG + 2 * n + 2)
                    turn(bank, at_tok, n).then_inc(tb_mm, 1)
                elif kind == "o":
                    if n == 0:
                        wait(pe, c_lo_made, u * KD + KD)
                    for t in range(2):
                        c = slice((2 * n + t) * P, (2 * n + t + 1) * P)
                        ins = product(ps[:, bank, t * D:(t + 1) * D],
                                      [(c_hi[:, k, c], c_lo[:, k, c]) for k in range(KD)],
                                      [w(O, k, slice(0, D)) for k in range(KD)])
                    ins.then_inc(o_mm, 1)

            def maximum(u, m):
                g, j, qt = m // 16, m // 4 % 4, m % 4
                pair, half = 2 * g + j // 2, j % 2
                if j % 2 == 0 and qt == 0:
                    wait(pe, kz_made, u * (2 * NP_) + 2 * pair + 2)
                    wait(pe, qst_made, u * NP_ + pair + 1)
                wait(pe, max_made, u * 64 + m - 1)
                pe.matmul(ps[:, MAXIMA + m % 2], qst[:, pair, qt * P:(qt + 1) * P],
                          kz[:, pair, half, :], start=True, stop=True).then_inc(max_mm, 1)

            def values(u, g, kt, par):
                wait(pe, exp_made, u * 64 + 16 * g + 4 * kt + 4)
                if kt == 0:
                    wait(pe, ev_made, u * NG + g)
                    if g == 0:
                        wait(pe, v_made, u * 2 + 2)
                for j in range(G):
                    ins = pe.matmul(ps[32 * j:32 * j + 32, OUT], vaug[:, par, kt, G * g + j],
                                    probs[:, (4 * kt + j) % 8], start=kt == 0, stop=kt == QT - 1,
                                    tile_position=(0, 32 * j))
                ins.then_inc(pv_mm, 1)

            def start(u, cross, b):
                for name, bank in start_banks(cross):
                    item(name, bank, u, cross, b)
                    for m in START_MAXIMA.get(name, ()):
                        maximum(u, m)

            def end(u, cross, b):
                values(u, NG - 1, QT - 1, u % 2)
                for name, bank in end_banks():
                    item(name, bank, u, cross, b)

            def period(u, par, now, before, after):
                taken[MISC], taken[MISC + 1] = frees("v1", u), frees("nm0", u)
                banks = period_banks(before, after)
                for s in range(SLOTS):
                    g, kt, i = s // 8, s // 2 % 4, s % 2
                    if s % 8 < 2:
                        wait(pe, (nm_even, nm_odd)[s % 8], u * NG + g + 1)
                    for half in range(2):
                        e = 2 * s + half
                        wait(pe, exp_made, u * 64 + e - 2)
                        pe.matmul(ps[:, SCORE + e % 3], kz[:, 2 * g + i, half, kt * P:(kt + 1) * P],
                                  qst[:, 2 * g + i, :], start=True, stop=True).then_inc(score_mm, 1)
                    for m in (2 * s + LEAD, 2 * s + LEAD + 1):
                        if m < 64:
                            maximum(u, m)
                        elif after:
                            maximum(u + 1, m - 64)
                    if s % 2:
                        if s >= 3:
                            values(u, (s - 3) // 8, (s - 3) // 2 % 4, par)
                        elif before:
                            values(u - 1, NG - 1, QT - 1, 1 - par)
                    for name, bank in banks[s]:
                        item(name.strip("<>"), bank, *whose(name, u, now, before, after))

            run(pe, start, period, end)


def gelu_phase(nc, ctx, A, scratch):
    sb = lambda name, shape, dt=F32: ctx.enter_context(nc.sbuf_tensor(name, shape, dt))
    sem_list = []

    def sem(name):
        s = ctx.enter_context(nc.semaphore(name))
        sem_list.append(s)
        return s

    ident, topv, slots, tanh_g = A["ident"], A["topv"], A["slots"], A["tanh_g"]
    experts, running, first_row = A["experts"], A["running"], A["first_row"]
    fi_hi = sb("fi_hi", [P, KD, F], F32R)
    fi_lo = sb("fi_lo", [P, KD, F], F32R)
    fo_hi = sb("fo_hi", [P, KF, D], F32R)
    fo_lo = sb("fo_lo", [P, KF, D], F32R)
    gate_hi = sb("gate_hi", [P, KD, NE], F32R)
    gate_lo = sb("gate_lo", [P, KD, NE], F32R)
    rows = {n: sb("row_" + n, [P, D]) for n in GELU_ROWS}
    fi_b = sb("fi_b", [P, KF])
    neg_half = sb("neg_half2", [P, QT])
    before = sb("before", [P, P], BF16)
    ones_sq = sb("ones_sq", [P, P], BF16)
    fi_col = lambda mt: fi_b[:, mt:mt + 1]
    with nc.sbuf_tensor("fi_raw", [P, KD, F], F32) as fi_raw, \
            nc.sbuf_tensor("fo_raw", [P, KF, D], F32) as fo_raw, \
            nc.sbuf_tensor("gate_raw", [P, KD, NE], F32) as gate_raw, \
            nc.sbuf_tensor("g_raw", [P, 2], F32) as g_raw, \
            nc.semaphore("weights_in") as weights_in, \
            nc.semaphore("hi_made") as hi_made, \
            nc.semaphore("lo_made") as lo_made, \
            nc.semaphore("ones_made") as ones_made, \
            nc.semaphore("iota_made") as iota_made, \
            nc.semaphore("tanh_made") as tanh_made, \
            nc.Block() as block:
        raws = [(fi_raw[:, :, :], fi_hi[:, :, :], fi_lo[:, :, :]),
                (fo_raw[:, :, :], fo_hi[:, :, :], fo_lo[:, :, :]),
                (gate_raw[:, :, :], gate_hi[:, :, :], gate_lo[:, :, :])]

        @block.sync
        def _(sp):
            sp.dma_start(fi_raw[:, :, :], A["fi_w"]).then_inc(weights_in, 16)
            sp.dma_start(fo_raw[:, :, :], A["fo_w"]).then_inc(weights_in, 16)
            sp.dma_start(gate_raw[:, :, :], A["gate_w"]).then_inc(weights_in, 16)
            sp.dma_start(fi_b[:, :], A["fi_b"]).then_inc(weights_in, 16)
            for n in GELU_ROWS:
                sp.dma_start(rows[n][:, :], A[n].partition_broadcast(P)).then_inc(weights_in, 16)
            sp.dma_start(g_raw[:, 0:1], A["g_xattn"].partition_broadcast(P)).then_inc(weights_in, 16)
            sp.dma_start(g_raw[:, 1:2], A["g_ffn"].partition_broadcast(P)).then_inc(weights_in, 16)

        n_loads = 4 + len(GELU_ROWS) + 2

        @block.scalar
        def _(act):
            act.wait_ge(weights_in, 16 * n_loads)
            act.activation(tanh_g[:, :], g_raw[:, :], ACT.Tanh).then_inc(tanh_made, 1)

        @block.vector
        def _(dve):
            dve.memset(running[:, :, :], 0.0)
            dve.memset(neg_half[:, :], -0.5).then_inc(hi_made, 1)
            dve.wait_ge(weights_in, 16 * n_loads)
            for n, (raw, hi, lo) in enumerate(raws):
                dve.tensor_copy(hi, raw).then_inc(hi_made, 1)
            for n, (raw, hi, lo) in enumerate(raws):
                dve.wait_ge(hi_made, n + 2)
                dve.tensor_tensor(lo, raw, hi.bitcast(F32), ALU.subtract).then_inc(lo_made, 1)

        @block.gpsimd
        def _(pool):
            pool.memset(ones_sq[:, :], 1.0).then_inc(ones_made, 1)
            pool.memset(before[:, :], 1.0).then_inc(ones_made, 1)
            pool.wait_ge(ones_made, 2)
            pool.affine_select(out=before[:, :], in_=before[:, :], compare_op=ALU.is_gt, fill=0.0,
                               base=0, pattern=[[1, P]], channel_multiplier=-1)
            pool.iota(experts[:, :], pattern=[[1, NE]], base=0, channel_multiplier=0,
                      allow_small_or_imprecise_dtypes=True).then_inc(iota_made, 1)
            pool.wait_ge(iota_made, 1)
            pool.tensor_scalar(first_row[:, :], experts[:, :], float(CAP), 0.0, ALU.mult, ALU.add)

    work = sb("gelu_parts", [P, 4, 2, S], F32R)
    in_hi, in_lo = (lambda mt: work[:, mt % 4, 0]), (lambda mt: work[:, mt % 4, 1])
    a_hi = sb("g_hi", [P, KD, S], F32R)
    a_lo = sb("g_lo", [P, KD, S], F32R)
    x_tok = sb("gx_tok", [P, QT, D])
    n_tok = sb("gn_tok", [P, QT, D])
    h_tok = sb("gh_tok", [P, QT, D])
    ev = sb("gelu_out", [P, 4, S])
    stats = sb("g_stats", [P, QT, 6])
    mv = sb("g_mv", [P, QT, 2])
    var_eps = sb("g_var_eps", [P, QT])
    rstd = sb("g_rstd", [P, QT])
    sumsq = sb("sumsq", [P, QT])
    logits = sb("logits", [P, QT, NE])
    max8 = sb("max8", [P, QT, 8])
    idx8 = sb("idx8", [P, QT, 8], U32)
    onehot = sb("onehot", [P, 2, QT, NE])
    weighed = sb("weighed", [P, 2, QT, NE])
    place = sb("place", [P, QT, NE])[:, :, :]
    chosen_f = sb("chosen_f", [P, QT, 2])[:, :, :]
    slot_f = sb("slot_f", [P, 2 * QT])[:, :]
    picks = sb("picks", [P, QT, NE], BF16)
    slot_now = sb("slot_now", [P, 2 * QT], U32)
    ps = ctx.enter_context(nc.psum_tensor("ps_g", [P, 8, S], F32))

    scattered = ctx.enter_context(nc.semaphore("scattered"))
    x_in = sem("g_x_in")
    n_in = sem("g_n_in")
    var_made = sem("g_var_made")
    rstd_made = sem("g_rstd_made")
    normed = sem("g_normed")
    affine_mul = sem("g_affine_mul")
    res_made = sem("g_res_made")
    tr_in = sem("g_tr_in")
    a_hi_made = sem("g_a_hi_made")
    a_lo_made = sem("g_a_lo_made")
    o_mm = sem("g_o_mm")
    h_made = sem("g_h_made")
    fi_mm = sem("g_fi_mm")
    gelu_made = sem("g_gelu_made")
    fo_mm = sem("g_fo_mm")
    in_hi_made = sem("g_in_hi_made")
    in_lo_made = sem("g_in_lo_made")
    sq_made = sem("g_sq_made")
    out_made = sem("g_out_made")
    stored = sem("g_stored")
    lg_mm = sem("g_lg_mm")
    picks_made = sem("g_picks_made")
    rank_mm = sem("g_rank_mm")
    slots_made = sem("g_slots_made")
    dve_chain = sem("g_dve_chain")
    with nc.Fori(0, B) as b:
        with nc.Block() as block:

            @block.sync
            def _(sp):
                sp.dma_start(n_tok[:, :, :], scratch["x2"][b]).then_inc(n_in, 16)
                sp.dma_start(x_tok[:, :, :], A["x"][b]).then_inc(x_in, 16)
                sp.wait_ge(out_made, QT)
                sp.dma_start(scratch["res"][b], x_tok[:, :, :]).then_inc(stored, 16)
                sp.wait_ge(stored, 16)

            @block.gpsimd
            def _(pool):
                def root(n):
                    pool.wait_ge(var_made, n + 1)
                    pool.tensor_tensor(rstd[:, :], var_eps[:, :], neg_half[:, :], ALU.pow) \
                        .then_inc(rstd_made, 1)

                def add_beta(n, name):
                    for qt in range(QT):
                        pool.wait_ge(affine_mul, QT * n + qt + 1)
                        pool.tensor_tensor(n_tok[:, qt], h_tok[:, qt], rows[name][:, :], ALU.add) \
                            .then_inc(normed, 1)

                def residual(n, name):
                    pool.wait_ge(tr_in, KD * (n + 1))
                    for qt in range(QT):
                        pool.tensor_tensor(n_tok[:, qt], n_tok[:, qt], rows[name][:, :], ALU.add) \
                            .then_inc(res_made, 1)

                residual(0, "fo_b")
                for mt in range(KF):
                    pool.wait_ge(in_hi_made, mt + 1)
                    pool.tensor_tensor(in_lo(mt), ev[:, mt % NG], in_hi(mt).bitcast(F32),
                                       ALU.subtract).then_inc(in_lo_made, 1)
                root(0)
                add_beta(0, "fo_be")
                root(1)
                root(2)
                pool.wait_ge(slots_made, 1)
                for s in range(2):
                    for qt in range(QT):
                        n = QT * s + qt
                        pool.indirect_dma_start(
                            out=scratch["xs"], in_=n_tok[:, qt], in_offset=None,
                            out_offset=bass.IndirectOffsetOnAxis(ap=slot_now[:, n:n + 1], axis=0)) \
                            .then_inc(scattered, 16)
                pool.wait_ge(scattered, b * (16 * 2 * QT) + 16 * 2 * QT)

            @block.scalar
            def _(act):
                def hi_of_in(n, bank):
                    for mt in range(KD):
                        act.wait_ge(tr_in, KD * n + mt + 1)
                        act.activation(a_hi[:, mt], ps[:, bank + mt], ACT.Copy).then_inc(a_hi_made, 1)

                hi_of_in(0, 6)
                for mt in range(KF):
                    act.wait_ge(fi_mm, mt + 1)
                    if mt >= NG:
                        act.wait_ge(in_lo_made, mt - NG + 1)
                    act.activation(ev[:, mt % NG], ps[:, mt % 4], ACT.Gelu, bias=fi_col(mt)) \
                        .then_inc(gelu_made, 1)
                for qt in range(QT):
                    act.wait_ge(normed, QT + qt + 1)
                    act.activation(ev[:, qt % 4, 0:D], h_tok[:, qt], ACT.Square,
                                   accum_out=sumsq[:, qt:qt + 1]).then_inc(sq_made, 1)
                hi_of_in(1, 2)

            @block.vector
            def _(dve):
                chain = [0]

                def link(ins):
                    chain[0] += 1
                    ins.then_inc(dve_chain, 1)
                    return chain[0]

                def settle():
                    dve.wait_ge(dve_chain, chain[0])

                def statistics(src):
                    for qt in range(QT):
                        link(dve.bn_stats(stats[:, qt], src[:, qt]))
                    settle()
                    for qt in range(QT):
                        link(dve.bn_aggr(mv[:, qt], stats[:, qt]))
                    settle()
                    dve.tensor_scalar(var_eps[:, :], mv[:, :, 1], LN_EPS, None, ALU.add) \
                        .then_inc(var_made, 1)

                def normalise(dst, src, n):
                    dve.wait_ge(rstd_made, n + 1)
                    for qt in range(QT):
                        yield qt, dve.tensor_scalar(dst[:, qt], src[:, qt], mv[:, qt, 0:1],
                                                    rstd[:, qt:qt + 1], ALU.subtract, ALU.mult)

                def lo_of_in(n, bank):
                    for mt in range(KD):
                        dve.wait_ge(a_hi_made, KD * n + mt + 1)
                        dve.tensor_tensor(a_lo[:, mt], ps[:, bank + mt], a_hi[:, mt].bitcast(F32),
                                          ALU.subtract).then_inc(a_lo_made, 1)

                def close(n, gamma):
                    for qt in range(QT):
                        dve.wait_ge(o_mm, QT * n + qt + 1)
                        dve.wait_ge(res_made, QT * n + qt + 1)
                        dve.tensor_tensor(h_tok[:, qt], ps[:, 4 + qt, 0:D], n_tok[:, qt],
                                          ALU.add).then_inc(h_made, 1)
                    dve.wait_ge(h_made, QT * (n + 1))
                    statistics(h_tok)
                    for qt, ins in normalise(h_tok, h_tok, n):
                        link(ins)
                    settle()
                    for qt in range(QT):
                        dve.tensor_tensor(h_tok[:, qt], h_tok[:, qt], rows[gamma][:, :],
                                          ALU.mult).then_inc(affine_mul, 1)

                lo_of_in(0, 6)
                for mt in range(KF):
                    dve.wait_ge(gelu_made, mt + 1)
                    if mt >= 4:
                        dve.wait_ge(fo_mm, mt - 3)
                    dve.tensor_copy(in_hi(mt), ev[:, mt % NG]).then_inc(in_hi_made, 1)
                close(0, "fo_g")
                dve.wait_ge(x_in, 16)
                for qt in range(QT):
                    dve.wait_ge(normed, qt + 1)
                    link(dve.scalar_tensor_tensor(x_tok[:, qt], n_tok[:, qt], tanh_g[:, 0:1],
                                                  x_tok[:, qt], ALU.mult, ALU.add))
                settle()
                statistics(x_tok)
                for qt, ins in normalise(h_tok, x_tok, 1):
                    ins.then_inc(normed, 1)
                dve.wait_ge(normed, 2 * QT)
                for qt in range(QT):
                    dve.scalar_tensor_tensor(x_tok[:, qt], h_tok[:, qt], tanh_g[:, 1:2],
                                             x_tok[:, qt], ALU.mult, ALU.add).then_inc(out_made, 1)
                dve.wait_ge(sq_made, QT)
                dve.tensor_scalar(var_eps[:, :], sumsq[:, :], 1.0 / D, RMS_EPS, ALU.mult,
                                  ALU.add).then_inc(var_made, 1)
                dve.wait_ge(rstd_made, 3)
                for qt in range(QT):
                    dve.scalar_tensor_tensor(n_tok[:, qt], h_tok[:, qt], rstd[:, qt:qt + 1],
                                             rows["rms"][:, :], ALU.mult, ALU.mult) \
                        .then_inc(normed, 1)
                lo_of_in(1, 2)
                dve.wait_ge(lg_mm, 1)
                link(dve.tensor_copy(logits[:, :, :],
                                     ps[:, 0, 0:QT * NE].rearrange("p (q e) -> p q e", q=QT)))
                settle()
                for qt in range(QT):
                    link(dve.max(max8[:, qt], logits[:, qt]))
                settle()
                for qt in range(QT):
                    link(dve.max_index(idx8[:, qt], max8[:, qt], logits[:, qt]))
                settle()
                link(dve.tensor_copy(topv[:, bass.ds(b * QT, QT), :], max8[:, :, 0:2]))
                link(dve.tensor_copy(chosen_f, idx8[:, :, 0:2]))
                link(dve.tensor_copy(running[:, 0], running[:, QT]))
                settle()
                for s in range(2):
                    link(dve.tensor_tensor(
                        onehot[:, s], experts[:, :].unsqueeze(1).to_broadcast([P, QT, NE]),
                        chosen_f[:, :, s].unsqueeze(2).to_broadcast([P, QT, NE]), ALU.is_equal))
                settle()
                dve.tensor_tensor(picks[:, :, :], onehot[:, 0], onehot[:, 1], ALU.add) \
                    .then_inc(picks_made, 1)
                dve.wait_ge(rank_mm, 1)
                for qt in range(QT):
                    link(dve.tensor_tensor(running[:, qt + 1], ps[:, 1, (QT + qt) * NE:(QT + qt + 1) * NE],
                                           running[:, qt], ALU.add))
                    settle()
                link(dve.tensor_tensor(place,
                                       ps[:, 1, 0:QT * NE].rearrange("p (q e) -> p q e", q=QT),
                                       running[:, 0:QT], ALU.add))
                settle()
                link(dve.tensor_tensor(place, place,
                                       first_row[:, :].unsqueeze(1).to_broadcast([P, QT, NE]),
                                       ALU.add))
                settle()
                for s in range(2):
                    link(dve.tensor_tensor(weighed[:, s], onehot[:, s], place, ALU.mult))
                settle()
                link(dve.tensor_reduce(slot_f, weighed[:, :, :, :].rearrange("p s q e -> p (s q) e"),
                                       AX.X, ALU.add))
                settle()
                link(dve.tensor_copy(slots[:, bass.ds(b * 2 * QT, 2 * QT)], slot_f))
                dve.tensor_copy(slot_now[:, :], slot_f).then_inc(slots_made, 1)
                settle()

            @block.tensor
            def _(pe):
                def turn(src, bank, ready, base, done):
                    for mt in range(KD):
                        for qt in range(QT):
                            if mt == 0 and base >= 0:
                                pe.wait_ge(ready, base + qt + 1)
                            ins = pe.transpose(ps[:, bank + mt, qt * P:(qt + 1) * P],
                                               src[:, qt, mt * P:(mt + 1) * P], ident[:, :])
                        ins.then_inc(done, 1)

                def product(out, left, right):
                    terms = [(l_, r_) for ls, rs in zip(left, right)
                             for l_, r_ in split_products(*ls, *rs)]
                    for n, (l_, r_) in enumerate(terms):
                        ins = pe.matmul(out, l_, r_, start=n == 0, stop=n == len(terms) - 1)
                    return ins

                pe.wait_ge(n_in, 16)
                turn(n_tok, 6, n_in, -QT, tr_in)
                pe.wait_ge(a_lo_made, KD)
                def gelu_out(mt):
                    pe.wait_ge(in_lo_made, mt + 1)
                    for qt in range(QT):
                        c = slice(qt * P, (qt + 1) * P)
                        terms = split_products(in_hi(mt)[:, c], in_lo(mt)[:, c], fo_hi[:, mt],
                                               fo_lo[:, mt])
                        for n, (left, right) in enumerate(terms):
                            ins = pe.matmul(ps[:, 4 + qt, 0:D], left, right,
                                            start=mt == 0 and n == 0,
                                            stop=mt == KF - 1 and n == len(terms) - 1)
                        if mt == KF - 1:
                            ins.then_inc(o_mm, 1)
                    if mt < KF - 1:
                        ins.then_inc(fo_mm, 1)

                for mt in range(KF):
                    c = slice(mt * P, (mt + 1) * P)
                    if mt >= 4:
                        pe.wait_ge(gelu_made, mt - 3)
                    product(ps[:, mt % 4], [(fi_hi[:, k, c], fi_lo[:, k, c]) for k in range(KD)],
                            [(a_hi[:, k], a_lo[:, k]) for k in range(KD)]).then_inc(fi_mm, 1)
                    if mt >= 2:
                        gelu_out(mt - 2)
                gelu_out(KF - 2)
                gelu_out(KF - 1)
                turn(n_tok, 2, normed, 2 * QT, tr_in)
                pe.wait_ge(a_lo_made, 2 * KD)
                for qt in range(QT):
                    c = slice(qt * P, (qt + 1) * P)
                    ins = product(ps[:, 0, qt * NE:(qt + 1) * NE],
                                  [(a_hi[:, k, c], a_lo[:, k, c]) for k in range(KD)],
                                  [(gate_hi[:, k], gate_lo[:, k]) for k in range(KD)])
                ins.then_inc(lg_mm, 1)
                pe.wait_ge(picks_made, 1)
                flat = picks[:, :, :].rearrange("p q e -> p (q e)")
                pe.matmul(ps[:, 1, 0:QT * NE], before[:, :], flat, start=True, stop=True)
                pe.matmul(ps[:, 1, QT * NE:2 * QT * NE], ones_sq[:, :], flat, start=True, stop=True) \
                    .then_inc(rank_mm, 1)

        nc.all_engine_barrier(sems_to_clear=range(sem_list[0].num, sem_list[-1].num + 1))




def expert_phase(nc, ctx, A, scratch):
    sb = lambda name, shape, dt=F32: ctx.enter_context(nc.sbuf_tensor(name, shape, dt))
    sem = lambda name: ctx.enter_context(nc.semaphore(name))
    ident, experts, running = A["ident"], A["experts"], A["running"]

    table = sb("table", [P, 2, STEPS], I32)
    counts_i = sb("counts_i", [P, NE], I32)
    zeros = sb("zeros", [P, GT, D])
    ps = ctx.enter_context(nc.psum_tensor("ps_e", [P, 8, 512], F32))

    with nc.sbuf_tensor("steps_f", [P, STEPS], F32) as steps_f, \
            nc.sbuf_tensor("firsts", [P, NE], F32) as firsts, \
            nc.sbuf_tensor("need", [P, NE], F32) as need, \
            nc.sbuf_tensor("upto", [P, 4, NE], F32) as upto, \
            nc.sbuf_tensor("past", [P, NE, STEPS], F32) as past, \
            nc.sbuf_tensor("above", [P, 2 * B * QT, NE], F32) as above, \
            nc.sbuf_tensor("shift", [P, NE], F32) as shift, \
            nc.sbuf_tensor("moved", [P, 2 * B * QT], F32) as moved, \
            nc.sbuf_tensor("found", [P, 6, STEPS], F32) as found, \
            nc.semaphore("iota_s") as iota_s, nc.semaphore("chain") as chain_sem, \
            nc.semaphore("counts_made") as counts_made, nc.semaphore("padded") as padded, \
            nc.Block() as block:
        @block.gpsimd
        def _(pool):
            pool.iota(steps_f[:, :], pattern=[[1, STEPS]], base=0, channel_multiplier=0,
                      allow_small_or_imprecise_dtypes=True).then_inc(iota_s, 1)

        @block.vector
        def _(dve):
            n = [0]

            def step(ins):
                n[0] += 1
                ins.then_inc(chain_sem, 1)
                dve.wait_ge(chain_sem, n[0])

            count = running[:, QT]
            step(dve.tensor_copy(counts_i[:, :], count))
            dve.memset(zeros[:, :, :], 0.0).then_inc(counts_made, 1)
            dve.wait_ge(iota_s, 1)
            over = past[:, :, 0:T // GR + 1]
            j = steps_f[:, 0:T // GR + 1]
            step(dve.tensor_scalar(found[:, 0, 0:T // GR + 1], j, float(GR), None, ALU.mult))
            step(dve.tensor_tensor(over, count.unsqueeze(2).to_broadcast([P, NE, T // GR + 1]),
                                   found[:, 0, 0:T // GR + 1].unsqueeze(1)
                                   .to_broadcast([P, NE, T // GR + 1]), ALU.is_gt))
            step(dve.tensor_reduce(need[:, :], over, AX.X, ALU.add))
            step(dve.tensor_copy(upto[:, 0], need[:, :]))
            for r, reach in enumerate((1, 2, 4)):
                step(dve.tensor_copy(upto[:, r + 1, 0:reach], upto[:, r, 0:reach]))
                step(dve.tensor_tensor(upto[:, r + 1, reach:], upto[:, r, reach:],
                                       upto[:, r, 0:NE - reach], ALU.add))
            step(dve.tensor_tensor(past[:, :, :],
                                   steps_f[:, :].unsqueeze(1).to_broadcast([P, NE, STEPS]),
                                   upto[:, 3].unsqueeze(2).to_broadcast([P, NE, STEPS]), ALU.is_ge))
            by_step = past[:, :, :].rearrange("p e n -> p n e")
            expert, begun, spare, inside, row = (found[:, m] for m in range(5))
            step(dve.tensor_reduce(expert, by_step, AX.X, ALU.add))
            step(dve.tensor_scalar(spare, expert, float(NE), None, ALU.is_ge))
            step(dve.tensor_scalar(expert, expert, float(NE - 1), None, ALU.min))
            step(dve.tensor_tensor(past[:, :, :], past[:, :, :],
                                   need[:, :].unsqueeze(2).to_broadcast([P, NE, STEPS]), ALU.mult))
            step(dve.tensor_reduce(begun, by_step, AX.X, ALU.add))
            step(dve.tensor_tensor(inside, steps_f[:, :], begun, ALU.subtract))
            step(dve.tensor_scalar(found[:, 5], spare, -1.0, 1.0, ALU.mult, ALU.add))
            step(dve.tensor_tensor(inside, inside, found[:, 5], ALU.mult))
            step(dve.tensor_scalar(inside, inside, float(GR), None, ALU.mult))
            step(dve.scalar_tensor_tensor(row, expert, float(CAP), inside, ALU.mult, ALU.add))
            step(dve.tensor_copy(table[:, 0], expert))
            step(dve.tensor_copy(table[:, 1], row))
            slots = A["slots"][:, :]
            n_slots = 2 * B * QT
            step(dve.tensor_tensor(above[:, :, :], slots.unsqueeze(2).to_broadcast([P, n_slots, NE]),
                                   A["first_row"][:, :].unsqueeze(1).to_broadcast([P, n_slots, NE]),
                                   ALU.is_ge))
            step(dve.tensor_scalar(shift[:, 1:NE], need[:, 0:NE - 1], float(GR), float(-CAP),
                                   ALU.mult, ALU.add))
            step(dve.memset(shift[:, 0:1], 0.0))
            step(dve.tensor_tensor(above[:, :, :], above[:, :, :],
                                   shift[:, :].unsqueeze(1).to_broadcast([P, n_slots, NE]), ALU.mult))
            step(dve.tensor_reduce(moved[:, :], above[:, :, :], AX.X, ALU.add))
            step(dve.tensor_tensor(A["picks"][:, :], slots, moved[:, :], ALU.add))

        @block.sync
        def _(sp):
            sp.wait_ge(counts_made, 1)
            for e in range(NE):
                at = sp.value_load(counts_i[0:1, e:e + 1], min_val=0, max_val=T)
                sp.dma_start(scratch["xs"][bass.ds(at + e * CAP, GR), :]
                             .rearrange("(t p) d -> p t d", p=P), zeros[:, :, :]).then_inc(padded, 16)
            sp.wait_ge(padded, 16 * NE)

    w_raw = sb("we_raw", [P, 3, KD * I])
    w_hi = sb("we_hi", [P, 2, 3, KD * I], F32R)
    w_lo = sb("we_lo", [P, 2, 3, KD * I], F32R)
    x_raw = sb("x_raw", [P, 2, GT, D])
    x_hi = sb("x_hi", [P, 2, KD, GR], F32R)
    x_lo = sb("x_lo", [P, 2, KD, GR], F32R)
    silu = sb("silu", [P, 2, GR])
    u_f = sb("u_f", [P, 2, GR])
    u_hi = sb("u_hi", [P, KI, GR], F32R)
    u_lo = sb("u_lo", [P, KI, GR], F32R)
    eo = sb("eo_sb", [P, GT, D])
    raw_in = [sem(f"raw_in{c}") for c in range(3)]
    x_in = [sem("x_in0"), sem("x_in1")]
    whi_made = sem("whi_made")
    wlo_made = sem("wlo_made")
    xt_mm = sem("xt_mm")
    xhi_made = sem("xhi_made")
    xlo_made = sem("xlo_made")
    up_mm = sem("up_mm")
    silu_made = sem("silu_made")
    u_made = sem("u_made")
    uhi_made = sem("uhi_made")
    ulo_made = sem("ulo_made")
    down_kt = sem("down_kt")
    eo_made = sem("eo_made")
    eo_out = sem("eo_out")

    def wait(eng, s, value):
        if not isinstance(value, int) or value > 0:
            eng.wait_ge(s, value)

    def over_steps(eng, body, prologue=None):
        for k in range(2):
            body(0, k, False)
        with eng.Fori(1, STEPS // 2 - 1) as i:
            for k in range(2):
                body(i, k, False)
        for k in range(2):
            body(STEPS // 2 - 1, k, k == 1)

    with nc.Block() as block:
        @block.sync
        def _(sp):
            def body(i, k, last):
                n = i * 2 + k
                e = sp.value_load(table[0:1, 0, bass.ds(n, 1)], min_val=0, max_val=NE - 1)
                r = sp.value_load(table[0:1, 1, bass.ds(n, 1)], min_val=0, max_val=NE * CAP - GR)
                wait(sp, xt_mm, n * 2 - 2)
                sp.dma_start(x_raw[:, k], scratch["xs"][bass.ds(r, GR), :]
                             .rearrange("(t p) d -> p t d", p=P)).then_inc(x_in[k], 16)
                for c in range(3):
                    wait(sp, wlo_made, n * 3 - 2 + c)
                    sp.dma_start(w_raw[:, c], A["experts_w"][bass.ds(e, 1), c]
                                 .rearrange("o p n -> (o p) n")).then_inc(raw_in[c], 16)

            over_steps(sp, body)

        @block.vector
        def _(dve):
            def split(n, k, c):
                wait(dve, raw_in[c], n * 16 + 16)
                if c == 2:
                    wait(dve, down_kt, n * KI - KI)
                dve.tensor_copy(w_hi[:, k, c], w_raw[:, c]).then_inc(whi_made, 1)
                wait(dve, whi_made, n * 3 + c + 1)
                dve.tensor_tensor(w_lo[:, k, c], w_raw[:, c], w_hi[:, k, c].bitcast(F32),
                                  ALU.subtract).then_inc(wlo_made, 1)

            def lo_of_x(n, k, mt):
                wait(dve, xhi_made, n * 2 + mt + 1)
                dve.tensor_tensor(x_lo[:, k, mt], ps[:, 7, 0:GR], x_hi[:, k, mt].bitcast(F32),
                                  ALU.subtract).then_inc(xlo_made, 1)

            lo_of_x(0, 0, 0)
            lo_of_x(0, 0, 1)
            for c in range(3):
                split(0, 0, c)

            def body(i, k, last):
                n = i * 2 + k
                for it in range(KI):
                    slot = (k + it) % 2
                    wait(dve, silu_made, n * KI + it + 1)
                    wait(dve, up_mm, n * (2 * KI) + 2 * it + 2)
                    wait(dve, ulo_made, n * KI + it - 1)
                    dve.tensor_tensor(u_f[:, slot], ps[:, 2 * slot + 1, 0:GR], silu[:, slot],
                                      ALU.mult).then_inc(u_made, 1)
                    if last:
                        continue
                    if it % 2 and it < 6:
                        split(n + 1, 1 - k, it // 2)
                    if it in (3, 5):
                        lo_of_x(n + 1, 1 - k, (it - 3) // 2)

            over_steps(dve, body)

        @block.gpsimd
        def _(pool):
            def body(i, k, last):
                n = i * 2 + k
                for it in range(KI):
                    slot = (k + it) % 2
                    wait(pool, uhi_made, n * KI + it + 1)
                    pool.tensor_tensor(u_lo[:, it], u_f[:, slot], u_hi[:, it].bitcast(F32),
                                       ALU.subtract).then_inc(ulo_made, 1)

            over_steps(pool, body)

        @block.scalar
        def _(act):
            def hi_of_x(n, k, mt):
                wait(act, xt_mm, n * 2 + mt + 1)
                act.activation(x_hi[:, k, mt], ps[:, 7, 0:GR], ACT.Copy).then_inc(xhi_made, 1)

            def hi_of_u(n, k, it):
                wait(act, u_made, n * KI + it + 1)
                wait(act, down_kt, n * KI + it + 1 - KI)
                act.activation(u_hi[:, it], u_f[:, (k + it) % 2], ACT.Copy).then_inc(uhi_made, 1)

            def put_out(n):
                wait(act, down_kt, n * KI + KI)
                wait(act, eo_out, n * 16)
                act.activation(eo[:, :, :], ps[:, 4:4 + GT, 0:D], ACT.Copy).then_inc(eo_made, 1)
                wait(act, eo_made, n + 1)
                act.dma_start(scratch["eo"][bass.ds(n * GR, GR), :].rearrange("(t p) d -> p t d", p=P),
                              eo[:, :, :]).then_inc(eo_out, 16)

            hi_of_x(0, 0, 0)
            hi_of_x(0, 0, 1)

            def body(i, k, last):
                n = i * 2 + k
                for it in range(KI):
                    slot = (k + it) % 2
                    wait(act, up_mm, n * (2 * KI) + 2 * it + 1)
                    wait(act, u_made, n * KI + it - 1)
                    act.activation(silu[:, slot], ps[:, 2 * slot, 0:GR], ACT.Silu) \
                        .then_inc(silu_made, 1)
                    if it:
                        hi_of_u(n, k, it - 1)
                    if it == 1 and not (isinstance(n, int) and n == 0):
                        put_out(n - 1)
                    if it in (3, 5) and not last:
                        hi_of_x(n + 1, 1 - k, (it - 3) // 2)
                hi_of_u(n, k, KI - 1)

            over_steps(act, body)
            put_out(STEPS - 1)
            act.wait_ge(eo_out, 16 * STEPS)

        @block.tensor
        def _(pe):
            def turn_rows(i, n, k, mt):
                if mt == 0:
                    wait(pe, x_in[k], i * 16 + 16)
                wait(pe, xlo_made, n * 2 + mt)
                for t in range(GT):
                    ins = pe.transpose(ps[:, 7, t * P:(t + 1) * P],
                                       x_raw[:, k, t, mt * P:(mt + 1) * P], ident[:, :])
                ins.then_inc(xt_mm, 1)

            def up(n, k, it):
                slot = (k + it) % 2
                wait(pe, u_made, n * KI + it - 1)
                for c in range(2):
                    if it == 0:
                        wait(pe, wlo_made, n * 3 + c + 1)
                    cut = lambda part, kt: part[:, k, c, kt * I + it * P:kt * I + (it + 1) * P]
                    terms = [t for kt in range(KD)
                             for t in split_products(cut(w_hi, kt), cut(w_lo, kt),
                                                     x_hi[:, k, kt], x_lo[:, k, kt])]
                    for m, (left, right) in enumerate(terms):
                        ins = pe.matmul(ps[:, 2 * slot + c, 0:GR], left, right, start=m == 0,
                                        stop=m == len(terms) - 1)
                    ins.then_inc(up_mm, 1)

            def down(n, k, it):
                if it == 0:
                    wait(pe, wlo_made, n * 3 + 3)
                    wait(pe, eo_made, n)
                wait(pe, ulo_made, n * KI + it + 1)
                w2 = slice(it * D, (it + 1) * D)
                for t in range(GT):
                    rows = slice(t * P, (t + 1) * P)
                    terms = split_products(u_hi[:, it, rows], u_lo[:, it, rows],
                                           w_hi[:, k, 2, w2], w_lo[:, k, 2, w2])
                    for m, (left, right) in enumerate(terms):
                        ins = pe.matmul(ps[:, 4 + t, 0:D], left, right, start=it == 0 and m == 0,
                                        stop=it == KI - 1 and m == len(terms) - 1)
                ins.then_inc(down_kt, 1)

            turn_rows(0, 0, 0, 0)
            turn_rows(0, 0, 0, 1)

            def body(i, k, last):
                n = i * 2 + k
                wait(pe, xlo_made, n * 2 + 2)
                for it in range(KI):
                    up(n, k, it)
                    if it >= 2:
                        down(n, k, it - 2)
                    if it in (2, 4) and not last:
                        turn_rows(i + k, n + 1, 1 - k, (it - 2) // 2)
                down(n, k, KI - 2)
                down(n, k, KI - 1)

            over_steps(pe, body)


def combine_phase(nc, ctx, A, scratch, out):
    sb = lambda name, shape, dt=F32: ctx.enter_context(nc.sbuf_tensor(name, shape, dt))
    sem = lambda name: ctx.enter_context(nc.semaphore(name))
    topv, slots, tanh_g = A["topv"], A["picks"], A["tanh_g"]
    share = sb("share", [P, 4, B * QT])
    tmp = sb("share_tmp", [P, 2, B * QT])
    picked = sb("picked", [P, 2, 2, QT, D])
    res = sb("res_sb", [P, 2, QT, D])
    picked_in = [sem("picked_in0"), sem("picked_in1")]
    res_in = [sem("res_in0"), sem("res_in1")]
    gap_made, exp_made, share_made, sum_made, out_sent = (
        sem(n) for n in ("gap_made", "share_exp", "share_made", "sum_made", "out_sent"))

    with nc.Block() as block:
        @block.sync
        def _(sp):
            for b in range(B):
                if b >= 2:
                    sp.wait_ge(out_sent, 16 * (b - 1))
                sp.dma_start(res[:, b % 2], scratch["res"][b]).then_inc(res_in[b % 2], 16)
                if b:
                    sp.wait_ge(sum_made, 2 * QT * b)
                    sp.dma_start(out[b - 1], res[:, (b - 1) % 2]).then_inc(out_sent, 16)
            sp.wait_ge(sum_made, 2 * QT * B)
            sp.dma_start(out[B - 1], res[:, (B - 1) % 2]).then_inc(out_sent, 16)
            sp.wait_ge(out_sent, 16 * B)

        @block.gpsimd
        def _(pool):
            for b in range(B):
                if b >= 2:
                    pool.wait_ge(sum_made, 2 * QT * (b - 1))
                for m in range(2 * QT):
                    n = 2 * QT * b + m
                    pool.indirect_dma_start(
                        out=picked[:, b % 2, m // QT, m % QT], out_offset=None, in_=scratch["eo"],
                        in_offset=bass.IndirectOffsetOnAxis(ap=slots[:, n:n + 1], axis=0)) \
                        .then_inc(picked_in[b % 2], 16)

        @block.scalar
        def _(act):
            act.wait_ge(gap_made, 1)
            act.activation(tmp[:, 1], tmp[:, 0], ACT.Exp).then_inc(exp_made, 1)

        @block.vector
        def _(dve):
            dve.tensor_tensor(tmp[:, 0], topv[:, :, 1], topv[:, :, 0], ALU.subtract) \
                .then_inc(gap_made, 1)
            dve.wait_ge(exp_made, 1)
            dve.tensor_scalar(share[:, 0], tmp[:, 1], 1.0, None, ALU.add).then_inc(share_made, 1)
            dve.wait_ge(share_made, 1)
            dve.reciprocal(share[:, 1], share[:, 0]).then_inc(share_made, 1)
            dve.wait_ge(share_made, 2)
            dve.tensor_scalar(share[:, 2], share[:, 1], tanh_g[:, 1:2], None, ALU.mult) \
                .then_inc(share_made, 1)
            dve.wait_ge(share_made, 3)
            dve.tensor_tensor(share[:, 3], share[:, 2], tmp[:, 1], ALU.mult).then_inc(share_made, 1)
            dve.wait_ge(share_made, 4)
            for b in range(B):
                k = b % 2
                dve.wait_ge(res_in[k], 16 * (b // 2 + 1))
                dve.wait_ge(picked_in[k], 16 * 2 * QT * (b // 2 + 1))
                for s in range(2):
                    if s:
                        dve.wait_ge(sum_made, QT * (2 * b + 1))
                    for qt in range(QT):
                        n = QT * b + qt
                        dve.scalar_tensor_tensor(res[:, k, qt], picked[:, k, s, qt],
                                                 share[:, 2 + s, n:n + 1], res[:, k, qt],
                                                 ALU.mult, ALU.add).then_inc(sum_made, 1)


def build(nc, A, out):
    with ExitStack() as ctx:
        sb = lambda name, shape, dt=F32: ctx.enter_context(nc.sbuf_tensor(name, shape, dt))
        A["ident"] = sb("ident", [P, P])
        A["tanh_g"] = sb("tanh_g", [P, 2])
        A["topv"] = sb("topv", [P, B * QT, 2])
        A["slots"] = sb("slots", [P, B * 2 * QT])
        A["picks"] = sb("picks_at", [P, B * 2 * QT], U32)
        A["experts"] = sb("experts", [P, NE])
        A["first_row"] = sb("first_row", [P, NE])
        A["running"] = sb("running", [P, QT + 1, NE])
        xs = nc.dram_tensor("xs", [NE * CAP, D], F32).ap()
        eo = nc.dram_tensor("eo", [STEPS * GR, D], F32).ap()
        res = nc.dram_tensor("res", [B, P, QT, D], F32).ap()
        x2 = nc.dram_tensor("x2", [B, P, QT, D], F32).ap()
        scratch = {"x2": x2, "xs": xs, "eo": eo, "res": res}
        with nc.semaphore("ident_zero") as ident_zero, nc.Block() as block:
            @block.gpsimd
            def _(pool):
                ident = A["ident"]
                pool.memset(ident[:, :], 0.0).then_inc(ident_zero, 1)
                pool.wait_ge(ident_zero, 1)
                pool.affine_select(out=ident[:, :], in_=ident[:, :], compare_op=ALU.not_equal,
                                   fill=1.0, base=0, pattern=[[-1, P]], channel_multiplier=1)
        with ExitStack() as phase:
            attention_phase(nc, phase, A, scratch)
        with ExitStack() as phase:
            gelu_phase(nc, phase, A, scratch)
        with ExitStack() as phase:
            expert_phase(nc, phase, A, scratch)
        with ExitStack() as phase:
            combine_phase(nc, phase, A, scratch, out)


def kernel(**inputs):
    import numpy as np
    import concourse.bacc as bacc
    from concourse.bass_utils import run_bass_kernel_spmd

    nc = bacc.Bacc("TRN2", target_bir_lowering=False, num_devices=1)
    arrays, A = {}, {}

    def give(name, a):
        a = np.ascontiguousarray(a)
        arrays["in_" + name] = a
        A[name] = nc.dram_tensor("in_" + name, a.shape, mybir.dt.from_np(a.dtype),
                                 kind="ExternalInput").ap()

    def stack(w):
        return w.reshape(-1, P, w.shape[1]).transpose(1, 0, 2)

    X = {k[len("L0_xattn_"):]: np.asarray(v) for k, v in inputs.items() if k.startswith("L0_xattn_")}
    tokens = lambda a: np.asarray(a).reshape(B, QT, P, D).transpose(0, 2, 1, 3)
    give("x", tokens(inputs["x"]))
    give("ctx", tokens(inputs["ctx_1024"]))
    give("mask", np.asarray(inputs["mask_Bx1x1xS2_ff0"]).reshape(B, 1, S))
    give("attn_w", np.stack([stack(X[a + n + "_w"])
                             for a in "cs" for n in "qkvo"], axis=1))
    E1, E2, E3 = (np.asarray(inputs["L0_ffn_w" + n]) for n in "123")
    lay = lambda w: w.reshape(NE, -1, P, w.shape[2]).transpose(0, 2, 1, 3).reshape(NE, P, -1)
    give("experts_w", np.stack([lay(E1.transpose(0, 2, 1)), lay(E3.transpose(0, 2, 1)),
                                lay(E2.transpose(0, 2, 1))], axis=1))
    give("fi_w", stack(X["fi_w"]))
    give("fo_w", stack(X["fo_w"]))
    give("gate_w", stack(np.asarray(inputs["L0_ffn_gate_w"]).T))
    give("cols", np.concatenate([X[a + n + "_b"].reshape(KD, P)
                                 for a in "cs" for n in "kq"]).T)
    give("fi_b", X["fi_b"].reshape(KF, P).T)
    for n in ATTN_ROWS + GELU_ROWS:
        give(n, X[n] if n != "rms" else inputs["L0_ffn_rms_weight"])
    choose = np.zeros((P, 4, 2, 2, P), np.float32)
    choose_mask = np.zeros((P, P), np.float32)
    stack_cols = np.zeros((P, 7), np.float32)
    for half in range(2):
        for place in range(4):
            for d in range(DH):
                feature = 2 * DH * place + DH * half + d
                for what, parts in enumerate(((0, 1, 0), (0, 0, 1))):
                    for t, part in enumerate(parts):
                        choose[feature, place, what, part, 3 * DH * half + DH * t + d] = 1
        stack_cols[3 * DH * half:3 * DH * half + 3 * DH, half] = 1
        stack_cols[ROW_MASK:ROW_MASK + 2, half] = 1
    for t in range(2):
        choose_mask[32 * t, ROW_MASK + t] = 1 / SCALE
        stack_cols[ROW_MASK + t, 6] = 1
        for j in range(G):
            stack_cols[ROW_MAX + G * t + j, 2 + j] = 1
    give("choose", choose)
    give("choose_mask", choose_mask)
    give("stack_cols", stack_cols)
    give("g_xattn", inputs["g_xattn"])
    give("g_ffn", inputs["g_ffn"])
    out = nc.dram_tensor("out", [B, P, QT, D], F32, kind="ExternalOutput").ap()
    build(nc, A, out)
    r = run_bass_kernel_spmd(nc, [arrays], core_ids=[0])
    return r.results[0]["out"].transpose(0, 2, 1, 3).reshape(B, S, D)
```

```python
import concourse.bass as bass
from concourse import mybir
from contextlib import ExitStack

F32 = mybir.dt.float32
F32R = mybir.dt.float32r
BF16 = mybir.dt.bfloat16
U32 = mybir.dt.uint32
I32 = mybir.dt.int32
ALU = mybir.AluOpType
ACT = mybir.ActivationFunctionType
AX = mybir.AxisListType

P = 128
B, S, D = 8, 512, 256
H, DH = 16, 16
F = 1024
I = 896
NE = 8
QT = S // P
KD = D // P
KF = F // P
NP_ = H // 2
G = 4
NG = H // G
HALF = P // 2
SCALE = 1.0 / 4.0
LN_EPS = 1e-5
RMS_EPS = 1e-6
KI = I // P
GT = 3
GR = GT * P
T = B * S
STEPS = (2 * T + NE * (GR - 1)) // GR
STEPS += STEPS % 2
CAP = T + GR
ROW_MASK = 2 * 3 * DH
ROW_MAX = ROW_MASK + 2
SLOTS = NG * 2 * QT
LEAD = 18
ATTN_ROWS = ["cv_b", "co_b", "co_g", "co_be", "sv_b", "so_b", "so_g", "so_be"]
GELU_ROWS = ["fo_b", "fo_g", "fo_be", "rms"]
LN_STEPS = ("stats", "aggr", "var", "root", "normed")
PERIOD_ITEMS = [["stk3"], ["stq3"], [">ctx0"], ["<at3"], ["stk4"], ["stq4"], [">ctx1"],
                ["<tb1", "nm1"], ["stk5"], ["stq5"], ["<o0"], ["<o1", "at0"], ["stk6"],
                ["stq6", ">in0"], [">in1"], ["nm2"], ["stk7", ">k0"], ["stq7", ">q0"], [">k1"],
                ["at1"], [">stk0"], [">stq0"], [">q1"], ["tb0", "nm3"], [">stk1"], [">stq1"],
                [">v0"], ["at2"], [">stk2"], [">stq2"], [">v1"], [">nm0"]]
START_ITEMS = ["ctx0", "ctx1", "in0", "in1", "k0", "q0", "k1", "q1", "v0", "stk0", "stq0", "stk1",
               "stq1", "stk2", "stq2", "v1", "nm0"]
START_MAXIMA = {"stq1": range(0, 8), "v1": range(8, LEAD)}
END_ITEMS = ["at3", "tb1", "o0", "o1"]
LATE_ITEMS = ("ctx", "in", "tb", "k", "q", "nm")
MISC_BANKS = (6, 7)
POOL_LO, DVE_LO = (2, 3, 4, 5), (0, 1, 6, 7)
ROUTE_STEPS = 24


def period_banks(before, after):
    n, slots = 0, []
    for names in PERIOD_ITEMS:
        slots.append([])
        for name in names:
            if name[0] == "<" and not before or name[0] == ">" and not after:
                continue
            if name.startswith(">ctx") and not after[0]:
                continue
            slots[-1].append((name, MISC_BANKS[n % 2]))
            n += 1
    return slots


def start_banks(cross):
    names = START_ITEMS if cross else START_ITEMS[2:]
    return [(name, MISC_BANKS[(n + 1) % 2]) for n, name in enumerate(names)]


def end_banks():
    return [(name, MISC_BANKS[(n + 1) % 2]) for n, name in enumerate(END_ITEMS)]


def positive(count):
    return not isinstance(count, int) or count > 0


def split_products(hi_l, lo_l, hi_r, lo_r):
    return [(hi_l, hi_r), (hi_l, lo_r), (lo_l, hi_r)]




def attention_phase(nc, ctx, A, scratch):
    sb = lambda name, shape, dt=F32: ctx.enter_context(nc.sbuf_tensor(name, shape, dt))
    sem = lambda name: ctx.enter_context(nc.semaphore(name))
    ident = A["ident"]
    w_hi = sb("w_hi", [P, 8, KD, D], F32R)
    w_lo = sb("w_lo", [P, 8, KD, D], F32R)
    rows = {n: sb("row_" + n, [P, D]) for n in ATTN_ROWS}
    cols = sb("cols", [P, 4 * KD])
    col_of = lambda l, what, mt: cols[:, 4 * l + 2 * what + mt:4 * l + 2 * what + mt + 1]
    choose = sb("choose", [P, 4, 2, 2, P], F32R)
    choose_mask = sb("choose_mask", [P, P], F32R)
    stack_cols = sb("stack_cols", [P, 7])
    keep = lambda half: stack_cols[:, half:half + 1]
    k_ones = lambda j: stack_cols[:, 2 + j:3 + j]
    q_ones = stack_cols[:, 6:7]
    K, V, O = 1, 2, 3
    neg_half = sb("neg_half", [P, QT])

    vaug = sb("vaug", [P, 2, QT, H, 2 * DH])
    mask_raw = sb("mask_raw", [HALF, S])
    mask_z = sb("mask_z", [P, S], F32R)
    nz = sb("nz", [P, 2, QT, 32], F32R)

    with nc.sbuf_tensor("w_raw", [P, 8, KD, D], F32) as w_raw, \
            nc.sbuf_tensor("choose_raw", [P, 4, 2, 2, P], F32) as choose_raw, \
            nc.sbuf_tensor("choose_mask_raw", [P, P], F32) as choose_mask_raw, \
            nc.semaphore("weights_in") as weights_in, nc.semaphore("hi_made") as hi_made, \
            nc.semaphore("cleared") as cleared, nc.Block() as block:
        @block.sync
        def _(sp):
            sp.dma_start(w_raw[:, :, :, :], A["attn_w"]).then_inc(weights_in, 16)
            sp.dma_start(cols[:, :], A["cols"]).then_inc(weights_in, 16)
            sp.dma_start(choose_raw[:, :, :, :, :], A["choose"]).then_inc(weights_in, 16)
            sp.dma_start(choose_mask_raw[:, :], A["choose_mask"]).then_inc(weights_in, 16)
            sp.dma_start(stack_cols[:, :], A["stack_cols"]).then_inc(weights_in, 16)
            for n in ATTN_ROWS:
                sp.dma_start(rows[n][:, :], A[n].partition_broadcast(P)).then_inc(weights_in, 16)
            sp.wait_ge(weights_in, 16 * (5 + len(ATTN_ROWS)))

        @block.vector
        def _(dve):
            dve.memset(neg_half[:, :], -0.5)
            dve.memset(mask_z[:, :].bitcast(F32), 0.0)
            dve.memset(mask_raw[:, :], 0.0)
            dve.memset(nz[:, :, :, :].bitcast(F32), 0.0)
            dve.memset(vaug[:, :, :, :, :], 0.0).then_inc(cleared, 1)
            dve.wait_ge(cleared, 1)
            dve.memset(vaug[:, :, :, :, DH:DH + 1], 1.0)
            dve.wait_ge(weights_in, 16 * (5 + len(ATTN_ROWS)))
            dve.tensor_copy(choose[:, :, :, :, :], choose_raw[:, :, :, :, :])
            dve.tensor_copy(choose_mask[:, :], choose_mask_raw[:, :])
            for j in range(8):
                dve.tensor_copy(w_hi[:, j], w_raw[:, j]).then_inc(hi_made, 1)
            for j in range(0, 8, 2):
                dve.wait_ge(hi_made, j + 1)
                dve.tensor_tensor(w_lo[:, j], w_raw[:, j], w_hi[:, j].bitcast(F32), ALU.subtract)

        @block.gpsimd
        def _(pool):
            for j in range(1, 8, 2):
                pool.wait_ge(hi_made, j + 1)
                pool.tensor_tensor(w_lo[:, j], w_raw[:, j], w_hi[:, j].bitcast(F32), ALU.subtract)

    kz = sb("kz", [P, NP_, 2, S], F32R)
    qst = sb("qst", [P, NP_, S], F32R)
    parts = sb("parts", [P, 4, KD, S], F32R)
    k_hi, k_lo, q_hi, q_lo = (parts[:, n] for n in range(4))
    probs = A["spare"]
    a_hi = sb("a_hi", [P, KD, S], F32R)
    a_lo = sb("a_lo", [P, KD, S], F32R)
    ctx_hi = sb("ctx_hi", [P, KD, S], F32R)
    ctx_lo = sb("ctx_lo", [P, KD, S], F32R)
    c_hi = sb("c_hi", [P, KD, S], F32R)
    c_lo = sb("c_lo", [P, KD, S], F32R)
    x_tok = sb("x_tok", [P, QT, D])
    ctx_tok = sb("ctx_tok", [P, QT, D])
    x1_tok = sb("x1_tok", [P, QT, D])
    x1_kept = sb("x1_kept", [P, QT, D])
    resid = sb("resid", [P, 2, QT, D])
    at_tok = sb("at_tok", [P, QT, P])
    sum_tok = sb("sum_tok", [P, QT, D])
    ev = sb("ev", [P, S])
    nraw = sb("nraw", [P, 2, QT, G])
    stats = sb("stats", [P, 2, QT, 6])
    mv = sb("mv", [P, 2, QT, 2])
    var_eps = sb("var_eps", [P, 2, QT])
    rstd = sb("rstd", [P, 2, QT])
    settled = sb("settled", [P, 1])
    rden = sb("rden", [P, QT, G])
    ps = ctx.enter_context(nc.psum_tensor("ps", [P, 8, S], F32))
    SCORE, MAXIMA, OUT, MISC = 0, 3, 5, 6

    x_in, ctx_in, mask_in = sem("x_in"), sem("ctx_in"), sem("mask_in")
    mask_made = sem("mask_made")
    x_stats, x_aggr, x_var, x_root, x_normed = (sem("x_" + n) for n in LN_STEPS)
    kept = sem("kept")
    tr_ctx, ctx_hi_made, ctx_lo_made = sem("tr_ctx"), sem("ctx_hi_made"), sem("ctx_lo_made")
    stored = sem("stored")
    tr_in, in_hi_made, in_lo_made = sem("tr_in"), sem("in_hi_made"), sem("in_lo_made")
    qk_mm, qk_hi_made, qk_lo_made = sem("qk_mm"), sem("qk_hi_made"), sem("qk_lo_made")
    v_mm, v_made = sem("v_mm"), sem("v_made")
    sel_mm = sem("sel_mm")
    kz_made = sem("kz_made")
    qst_made = sem("qst_made")
    max_mm, max_made = sem("max_mm"), sem("max_made")
    nm_hi_made, nm_lo_made, nm_tr = sem("nm_hi_made"), sem("nm_lo_made"), sem("nm_tr")
    nm_even, nm_odd = sem("nm_even"), sem("nm_odd")
    score_mm, exp_made = sem("score_mm"), sem("exp_made")
    pv_mm = sem("pv_mm")
    ev_made, at_tr, rden_made, at_norm = (sem(n) for n in
                                          ("ev_made", "at_tr", "rden_made", "at_norm"))
    tb_mm, c_hi_made, c_lo_made = sem("tb_mm"), sem("c_hi_made"), sem("c_lo_made")
    o_mm, sum_made = sem("o_mm"), sem("sum_made")
    res_made, gain_made, shift_made = sem("res_made"), sem("gain_made"), sem("shift_made")
    t_stats, t_aggr, t_var, t_root, t_normed = (sem("t_" + n) for n in LN_STEPS)

    def run(eng, start, period, end):
        cross, own = True, False
        start(0, cross, 0)
        period(0, 0, (cross, 0), None, (cross, 1))
        period(1, 1, (cross, 1), (cross, 0), (cross, 2))
        period(2, 0, (cross, 2), (cross, 1), (own, 0))
        with eng.Fori(1, B - 2) as i:
            period(i * 2 + 1, 1, (own, i - 1), (cross, i + 1), (cross, i + 2))
            period(i * 2 + 2, 0, (cross, i + 2), (own, i - 1), (own, i))
        period(2 * B - 3, 1, (own, B - 3), (cross, B - 1), (own, B - 2))
        period(2 * B - 2, 0, (own, B - 2), (own, B - 3), (own, B - 1))
        period(2 * B - 1, 1, (own, B - 1), (own, B - 2), None)
        end(2 * B - 1, own, B - 1)

    def unit_of(cross, b):
        if isinstance(b, int) and (cross and b < 2 or not cross and b >= B - 2):
            return b if cross else b + B
        return b * 2 - 2 if cross else b * 2 + 3

    def whose(name, u, now, before, after):
        step = {"<": -1, ">": 1}.get(name[0], 0)
        return (u + step if step else u, *(now, after, before)[step])

    with nc.Block() as block:

        @block.sync
        def _(sp):
            sp.sem_inc(stored, 1)

            def load(u, cross, b):
                if not cross:
                    return
                if not (isinstance(b, int) and b == 0):
                    sp.wait_ge(res_made, unit_of(True, b - 1) + 1)
                sp.dma_start(x_tok[:, :, :], A["x"][b]).then_inc(x_in, 16)
                if positive(b * KD):
                    sp.wait_ge(tr_ctx, b * KD)
                sp.dma_start(ctx_tok[:, :, :], A["ctx"][b]).then_inc(ctx_in, 16)
                for row in (0, 32):
                    if positive(b * 2):
                        sp.wait_ge(mask_made, b * 2)
                    sp.dma_start(mask_raw[row:row + 1, :], A["mask"][b]).then_inc(mask_in, 16)

            def store(u, cross, b):
                if not cross:
                    sp.wait_ge(shift_made, u + 1)
                    sp.dma_start(scratch["x2"][b], sum_tok[:, :, :]).then_inc(stored, 16)

            def period(u, par, now, before, after):
                if after:
                    load(u + 1, *after)
                if before:
                    store(u - 1, *before)

            def end(u, cross, b):
                sp.wait_ge(pv_mm, 2 * B * NG * QT)
                sp.dma_start(A["fi_raw"], A["fi_w"]).then_inc(A["gelu_weights_in"], 16)
                sp.dma_start(A["fo_raw"], A["fo_w"]).then_inc(A["gelu_weights_in"], 16)
                store(u, cross, b)

            run(sp, load, period, end)
            sp.wait_ge(stored, 16 * B + 1)

        @block.gpsimd
        def _(pool):
            def root(n, var, done, count):
                pool.wait_ge(var, count)
                pool.tensor_tensor(rstd[:, n], var_eps[:, n], neg_half[:, :], ALU.pow) \
                    .then_inc(done, 1)

            def row(name):
                return rows[name][:, :].unsqueeze(1).to_broadcast([P, QT, D])

            def split_mask(u, cross, b):
                if not cross:
                    return
                pool.wait_ge(res_made, u + 1)
                pool.wait_ge(mask_made, b * 2 + 1)
                pool.tensor_tensor(mask_z[32:33, :], mask_raw[32:33, :],
                                   mask_z[32:33, :].bitcast(F32), ALU.subtract) \
                    .then_inc(mask_made, 1)
                pool.wait_ge(mask_made, b * 2 + 2)

            def residual(u, cross, b, par):
                pool.wait_ge(tr_in, u * KD + KD)
                if positive(u * 2 - 2):
                    pool.wait_ge(sum_made, u * 2 - 2)
                pool.tensor_tensor(resid[:, par], (x_tok if cross else x1_kept)[:, :, :],
                                   row("co_b" if cross else "so_b"), ALU.add).then_inc(res_made, 1)

            def finish(u, cross, b):
                pool.wait_ge(t_normed, u * QT + QT)
                pool.tensor_tensor(sum_tok[:, :, :], sum_tok[:, :, :], row("co_g" if cross else "so_g"),
                                   ALU.mult).then_inc(gain_made, 1)
                pool.wait_ge(gain_made, u + 1)
                if cross:
                    if positive(b):
                        pool.wait_ge(kept, b)
                    pool.tensor_tensor(x1_tok[:, :, :], sum_tok[:, :, :], row("co_be"), ALU.add) \
                        .then_inc(shift_made, 1)
                else:
                    pool.tensor_tensor(sum_tok[:, :, :], sum_tok[:, :, :], row("so_be"), ALU.add) \
                        .then_inc(shift_made, 1)

            def start(u, cross, b):
                root(0, x_var, x_root, b + 1)
                residual(u, cross, b, u % 2)
                split_mask(u, cross, b)

            def end(u, cross, b):
                root(1, t_var, t_root, u + 1)
                finish(u, cross, b)

            def period(u, par, now, before, after):
                if after and after[0]:
                    root(0, x_var, x_root, after[1] + 1)
                if before:
                    root(1, t_var, t_root, u)
                if after:
                    residual(u + 1, *after, 1 - par)
                    split_mask(u + 1, *after)
                if before:
                    finish(u - 1, *before)

            run(pool, start, period, end)

        @block.scalar
        def _(act):
            def high(dst, done, src_bank, ready, count, bias=None):
                act.wait_ge(ready, count)
                if bias is None:
                    act.activation(dst, ps[:, src_bank], ACT.Copy).then_inc(done, 1)
                else:
                    act.activation(dst, ps[:, src_bank], ACT.Identity, bias=bias).then_inc(done, 1)

            def item(name, bank, u, cross, b):
                kind, n = name[:-1], int(name[-1])
                if kind == "ctx":
                    high(ctx_hi[:, n], ctx_hi_made, bank, tr_ctx, b * KD + n + 1)
                elif kind == "in":
                    high(a_hi[:, n], in_hi_made, bank, tr_in, u * KD + n + 1)
                elif kind == "tb":
                    high(c_hi[:, n], c_hi_made, bank, tb_mm, u * KD + n + 1)
                elif kind in ("k", "q"):
                    what = "kq".index(kind)
                    high((k_hi, q_hi)[what][:, n], qk_hi_made, bank, qk_mm, u * 4 + 2 * n + what + 1,
                         col_of(0 if cross else 1, what, n))
                elif kind == "nm":
                    act.wait_ge(nm_tr, u * NG + n + 1)
                    act.activation(qst[96:P, 2 * n], ps[96:P, bank], ACT.Identity,
                                   bias=q_ones[96:P, :]).then_inc(nm_even, 1)
                elif kind == "stq" and n % 2 == 0:
                    act.wait_ge(sel_mm, u * (2 * NP_) + 2 * n + 2)
                    act.activation(qst[:, n], ps[:, bank], ACT.Identity, bias=q_ones) \
                        .then_inc(qst_made, 1)
                elif kind == "stk":
                    act.wait_ge(sel_mm, u * (2 * NP_) + 2 * n + 1)
                    for half in range(2):
                        act.activation(kz[:, n, half], ps[:, bank], ACT.Identity,
                                       bias=k_ones(2 * (n % 2) + half), scale=keep(half)) \
                            .then_inc(kz_made, 1)

            def split_mask(b):
                act.wait_ge(mask_in, b * 32 + 32)
                if not (isinstance(b, int) and b == 0):
                    act.wait_ge(sel_mm, unit_of(True, b - 1) * (2 * NP_) + 2 * NP_)
                act.activation(mask_z[0:33, :], mask_raw[0:33, :], ACT.Copy).then_inc(mask_made, 1)

            def start(u, cross, b):
                if cross:
                    split_mask(b)
                for name, bank in start_banks(cross):
                    item(name, bank, u, cross, b)

            def outputs(u, g):
                act.wait_ge(pv_mm, u * (NG * QT) + QT * g + QT)
                act.activation(ev[:, :], ps[:, OUT], ACT.Copy).then_inc(ev_made, 1)

            def end(u, cross, b):
                outputs(u, NG - 1)
                for name, bank in end_banks():
                    item(name, bank, u, cross, b)

            def period(u, par, now, before, after):
                banks = period_banks(before, after)
                for s in range(SLOTS):
                    for half in range(2):
                        e = 2 * s + half
                        act.wait_ge(score_mm, u * 64 + e + 1)
                        if positive(u * (NG * QT) + (e - 8) // 4 + 1):
                            act.wait_ge(pv_mm, u * (NG * QT) + (e - 8) // 4 + 1)
                        act.activation(probs[:, e % 8], ps[:, SCORE + e % 3], ACT.Exp,
                                       scale=SCALE).then_inc(exp_made, 1)
                    if s == (18 if now[0] else 4) and after and after[0]:
                        split_mask(after[1])
                    if s % 8 == 1 and (s > 8 or before):
                        outputs(u if s > 8 else u - 1, (s // 8 - 1) % NG)
                    for name, bank in banks[s]:
                        item(name.strip("<>"), bank, *whose(name, u, now, before, after))

            run(act, start, period, end)

        @block.vector
        def _(dve):
            def low(dst, done, bank, high, ready, count, bias=None):
                dve.wait_ge(ready, count)
                if bias is None:
                    dve.tensor_tensor(dst, ps[:, bank], high.bitcast(F32), ALU.subtract) \
                        .then_inc(done, 1)
                else:
                    dve.scalar_tensor_tensor(dst, ps[:, bank], bias, high.bitcast(F32), ALU.add,
                                             ALU.subtract).then_inc(done, 1)

            def item(name, bank, u, cross, b, par):
                kind, n = name[:-1], int(name[-1])
                if kind == "ctx":
                    low(ctx_lo[:, n], ctx_lo_made, bank, ctx_hi[:, n], ctx_hi_made, b * KD + n + 1)
                elif kind == "in":
                    low(a_lo[:, n], in_lo_made, bank, a_hi[:, n], in_hi_made, u * KD + n + 1)
                elif kind == "tb":
                    low(c_lo[:, n], c_lo_made, bank, c_hi[:, n], c_hi_made, u * KD + n + 1)
                elif kind in ("k", "q"):
                    what = "kq".index(kind)
                    low((k_lo, q_lo)[what][:, n], qk_lo_made, bank, (k_hi, q_hi)[what][:, n],
                        qk_hi_made, u * 4 + 2 * n + what + 1, col_of(0 if cross else 1, what, n))
                elif kind == "nm":
                    dve.wait_ge(nm_even, u * NG + n + 1)
                    dve.tensor_scalar(qst[96:P, 2 * n + 1], ps[96:P, bank], q_ones[96:P, :], None,
                                      ALU.add).then_inc(nm_odd, 1)
                elif kind == "stq" and n % 2:
                    dve.wait_ge(sel_mm, u * (2 * NP_) + 2 * n + 2)
                    dve.tensor_scalar(qst[:, n], ps[:, bank], q_ones, None, ALU.add) \
                        .then_inc(qst_made, 1)
                elif kind == "v":
                    dve.wait_ge(v_mm, u * 2 + n + 1)
                    dve.tensor_tensor(
                        vaug[:, par, 2 * n:2 * n + 2, :, 0:DH],
                        ps[:, bank].rearrange("p (t h d) -> p t h d", t=2, d=DH),
                        rows["cv_b" if cross else "sv_b"][:, :].rearrange("p (h d) -> p h d", d=DH)
                        .unsqueeze(1).to_broadcast([P, 2, H, DH]), ALU.add).then_inc(v_made, 1)
                elif kind == "at":
                    dve.wait_ge(at_tr, u * NG + n + 1)
                    src = ps[:, bank].rearrange("p (q j d) -> p q j d", q=QT, j=G)
                    if positive(u * NG + n):
                        dve.wait_ge(at_norm, u * NG + n)
                    dve.reciprocal(rden[:, :, :], src[:, :, :, DH]).then_inc(rden_made, 1)
                    dve.wait_ge(rden_made, u * NG + n + 1)
                    dve.tensor_tensor(
                        at_tok[:, :, G * DH * (n % 2):G * DH * (n % 2 + 1)]
                        .rearrange("p q (j d) -> p q j d", j=G),
                        src[:, :, :, 0:DH], rden[:, :, :].unsqueeze(3).to_broadcast([P, QT, G, DH]),
                        ALU.mult).then_inc(at_norm, 1)
                elif kind == "o":
                    dve.wait_ge(o_mm, u * 2 + n + 1)
                    if n == 0:
                        dve.wait_ge(res_made, u + 1)
                        if positive(u):
                            dve.wait_ge(shift_made, u)
                        if cross and not (isinstance(b, int) and b < 3):
                            dve.wait_ge(stored, b * 16 - 2 * 16 + 1)
                        elif not cross and isinstance(b, int) and b >= B - 2:
                            dve.wait_ge(stored, b * 16 + 1)
                    dve.tensor_tensor(sum_tok[:, 2 * n:2 * n + 2],
                                      ps[:, bank].rearrange("p (t d) -> p t d", t=2),
                                      resid[:, par, 2 * n:2 * n + 2], ALU.add).then_inc(sum_made, 1)

            def moments(n, src, s_stats, s_aggr, s_var, count):
                for qt in range(QT):
                    dve.bn_stats(stats[:, n, qt], src[:, qt]).then_inc(s_stats, 1)
                dve.wait_ge(s_stats, count * QT + QT)
                dve.tensor_copy(settled[:, :], stats[:, n, 0, 0:1])
                for qt in range(QT):
                    dve.bn_aggr(mv[:, n, qt], stats[:, n, qt]).then_inc(s_aggr, 1)
                dve.wait_ge(s_aggr, count * QT + QT)
                dve.tensor_scalar(var_eps[:, n], mv[:, n, :, 1], LN_EPS, None, ALU.add) \
                    .then_inc(s_var, 1)

            def normalise(n, tok, s_root, s_normed, count):
                dve.wait_ge(s_root, count + 1)
                for qt in range(QT):
                    dve.tensor_scalar(tok[:, qt], tok[:, qt], mv[:, n, qt, 0:1],
                                      rstd[:, n, qt:qt + 1], ALU.subtract, ALU.mult) \
                        .then_inc(s_normed, 1)

            def x_moments(b):
                dve.wait_ge(x_in, b * 16 + 16)
                moments(0, x_tok, x_stats, x_aggr, x_var, b)

            def sum_moments(u):
                dve.wait_ge(sum_made, u * 2 + 2)
                moments(1, sum_tok, t_stats, t_aggr, t_var, u)

            def reduce_max(u, m):
                dve.wait_ge(max_mm, u * 64 + m + 1)
                g, j, qt = m // 16, m // 4 % 4, m % 4
                dve.tensor_reduce(nraw[:, g % 2, qt, j:j + 1], ps[:, MAXIMA + m % 2], AX.X, ALU.max,
                                  negate=True).then_inc(max_made, 1)

            def keep_x1(b):
                dve.wait_ge(shift_made, unit_of(True, b) + 1)
                if positive(b):
                    dve.wait_ge(res_made, unit_of(False, b - 1) + 1)
                dve.tensor_copy(x1_kept[:, :, :], x1_tok[:, :, :]).then_inc(kept, 1)

            def split_max(u, g):
                dve.wait_ge(max_made, u * 64 + 16 * g + 16)
                dve.tensor_copy(nz[:, g % 2, :, 2:2 + G], nraw[:, g % 2]).then_inc(nm_hi_made, 1)
                dve.wait_ge(nm_hi_made, u * NG + g + 1)
                dve.tensor_tensor(nz[:, g % 2, :, 2 + G:2 + 2 * G], nraw[:, g % 2],
                                  nz[:, g % 2, :, 2:2 + G].bitcast(F32), ALU.subtract) \
                    .then_inc(nm_lo_made, 1)

            def start(u, cross, b):
                if cross:
                    x_moments(b)
                    normalise(0, x_tok, x_root, x_normed, b)
                for name, bank in start_banks(cross):
                    if name == "nm0":
                        split_max(u, 0)
                    item(name, bank, u, cross, b, u % 2)
                    for m in START_MAXIMA.get(name, ()):
                        reduce_max(u, m)

            def end(u, cross, b):
                for name, bank in end_banks():
                    item(name, bank, u, cross, b, u % 2)
                sum_moments(u)
                normalise(1, sum_tok, t_root, t_normed, u)

            def period(u, par, now, before, after):
                banks = period_banks(before, after)
                late = []
                for s in range(SLOTS):
                    for name, bank in late:
                        item(name.strip("<>"), bank, *whose(name, u, now, before, after),
                             par if name[0] not in "<>" else 1 - par)
                    late = [n for n in banks[s] if n[0].strip("<>")[:-1] in LATE_ITEMS]
                    for m in (2 * s + LEAD, 2 * s + LEAD + 1):
                        if m < 64:
                            reduce_max(u, m)
                        elif after:
                            reduce_max(u + 1, m - 64)
                    if s % 8 == 6:
                        if s < 24:
                            split_max(u, s // 8 + 1)
                        elif after:
                            split_max(u + 1, 0)
                    for name, bank in banks[s]:
                        if (name, bank) not in late:
                            item(name.strip("<>"), bank, *whose(name, u, now, before, after),
                                 par if name[0] not in "<>" else 1 - par)
                    if after and after[0]:
                        if s == 1:
                            x_moments(after[1])
                        if s == 5:
                            normalise(0, x_tok, x_root, x_normed, after[1])
                    if s == 26 and isinstance(u, int) and u == 1:
                        keep_x1(0)
                    if s == 26 and after and not after[0] and not (
                            isinstance(after[1], int) and after[1] == B - 1):
                        keep_x1(after[1] + 1)
                    if before:
                        if s == 13:
                            sum_moments(u - 1)
                        if s == 17:
                            normalise(1, sum_tok, t_root, t_normed, u - 1)
                for name, bank in late:
                    item(name.strip("<>"), bank, *whose(name, u, now, before, after), 1 - par)

            run(dve, start, period, end)

        @block.tensor
        def _(pe):
            taken = {6: [], 7: []}

            def frees(name, u, b=None):
                kind, n = name[:-1], int(name[-1])
                return {"ctx": lambda: [(ctx_lo_made, b * KD + n + 1)],
                        "in": lambda: [(in_lo_made, u * KD + n + 1)],
                        "tb": lambda: [(c_lo_made, u * KD + n + 1)],
                        "k": lambda: [(qk_lo_made, u * 4 + 2 * n + 1)],
                        "q": lambda: [(qk_lo_made, u * 4 + 2 * n + 2)],
                        "v": lambda: [(v_made, u * 2 + n + 1)],
                        "stk": lambda: [(kz_made, u * (2 * NP_) + 2 * n + 2)],
                        "stq": lambda: [(qst_made, u * NP_ + n + 1)],
                        "nm": lambda: [(nm_even, u * NG + n + 1), (nm_odd, u * NG + n + 1)],
                        "at": lambda: [(at_norm, u * NG + n + 1)],
                        "o": lambda: [(sum_made, u * 2 + n + 1)]}[kind]()

            def turn(bank, src, mt):
                for qt in range(QT):
                    ins = pe.transpose(ps[:, bank, qt * P:(qt + 1) * P],
                                       src[:, qt, mt * P:(mt + 1) * P], ident[:, :])
                return ins

            def product(out, left, right):
                terms = [t for ls, rs in zip(left, right) for t in split_products(*ls, *rs)]
                for n, (l_, r_) in enumerate(terms):
                    ins = pe.matmul(out, l_, r_, start=n == 0, stop=n == len(terms) - 1)
                return ins

            def item(name, bank, u, cross, b):
                for s, count in taken[bank]:
                    pe.wait_ge(s, count)
                taken[bank] = frees(name, u, b)
                kind, n = name[:-1], int(name[-1])
                l = 0 if cross else 1
                w = lambda which, k, c: (w_hi[:, 4 * l + which, k, c], w_lo[:, 4 * l + which, k, c])
                key_side = (ctx_hi, ctx_lo) if cross else (a_hi, a_lo)
                if kind == "ctx":
                    pe.wait_ge(ctx_in, b * 16 + 16)
                    turn(bank, ctx_tok, n).then_inc(tr_ctx, 1)
                elif kind == "in":
                    if cross:
                        pe.wait_ge(x_normed, b * QT + QT)
                    else:
                        pe.wait_ge(kept, b + 1)
                    turn(bank, x_tok if cross else x1_kept, n).then_inc(tr_in, 1)
                elif kind in ("k", "q"):
                    side = key_side if kind == "k" else (a_hi, a_lo)
                    if n == 0:
                        pe.wait_ge(in_lo_made, u * KD + KD)
                        if cross:
                            pe.wait_ge(ctx_lo_made, b * KD + KD)
                    c = slice(n * P, (n + 1) * P)
                    product(ps[:, bank], [w("qk".index(kind), k, c) for k in range(KD)],
                            [(side[0][:, k], side[1][:, k]) for k in range(KD)]).then_inc(qk_mm, 1)
                elif kind == "v":
                    for t in range(2):
                        c = slice((2 * n + t) * P, (2 * n + t + 1) * P)
                        ins = product(ps[:, bank, t * D:(t + 1) * D],
                                      [(key_side[0][:, k, c], key_side[1][:, k, c]) for k in range(KD)],
                                      [w(V, k, slice(0, D)) for k in range(KD)])
                    ins.then_inc(v_mm, 1)
                elif kind in ("stk", "stq"):
                    what = "kq".index(kind[2])
                    hi_lo = ((k_hi, k_lo), (q_hi, q_lo))[what]
                    pe.wait_ge(qk_lo_made, u * 4 + 2 * (n // 4) + what + 1)
                    masked = what == 0 and cross
                    if masked:
                        if n == 0:
                            pe.wait_ge(mask_made, b * 2 + 2)
                        pe.matmul(ps[:, bank], choose_mask[:, :], mask_z[:, :], start=True, stop=False)
                    for t in range(2):
                        ins = pe.matmul(ps[:, bank], choose[:, n % 4, what, t], hi_lo[t][:, n // 4],
                                        start=t == 0 and not masked, stop=t == 1)
                    ins.then_inc(sel_mm, 1)
                elif kind == "nm":
                    pe.wait_ge(nm_lo_made, u * NG + n + 1)
                    for qt in range(QT):
                        ins = pe.matmul(ps[96:P, bank, qt * P:(qt + 1) * P],
                                        nz[:, n % 2, qt].bitcast(F32), ident[:, :], start=True,
                                        stop=True, tile_position=(0, 96))
                    ins.then_inc(nm_tr, 1)
                elif kind == "at":
                    pe.wait_ge(ev_made, u * NG + n + 1)
                    for qt in range(QT):
                        ins = pe.transpose(ps[:, bank, qt * P:(qt + 1) * P],
                                           ev[:, qt * P:(qt + 1) * P], ident[:, :])
                    ins.then_inc(at_tr, 1)
                elif kind == "tb":
                    pe.wait_ge(at_norm, u * NG + 2 * n + 2)
                    turn(bank, at_tok, 0).then_inc(tb_mm, 1)
                elif kind == "o":
                    if n == 0:
                        pe.wait_ge(c_lo_made, u * KD + KD)
                    for t in range(2):
                        c = slice((2 * n + t) * P, (2 * n + t + 1) * P)
                        ins = product(ps[:, bank, t * D:(t + 1) * D],
                                      [(c_hi[:, k, c], c_lo[:, k, c]) for k in range(KD)],
                                      [w(O, k, slice(0, D)) for k in range(KD)])
                    ins.then_inc(o_mm, 1)

            def maximum(u, m):
                g, j, qt = m // 16, m // 4 % 4, m % 4
                pair, half = 2 * g + j // 2, j % 2
                if j % 2 == 0 and qt == 0:
                    pe.wait_ge(kz_made, u * (2 * NP_) + 2 * pair + 2)
                    pe.wait_ge(qst_made, u * NP_ + pair + 1)
                if positive(u * 64 + m - 1):
                    pe.wait_ge(max_made, u * 64 + m - 1)
                pe.matmul(ps[:, MAXIMA + m % 2], qst[:, pair, qt * P:(qt + 1) * P],
                          kz[:, pair, half, :], start=True, stop=True).then_inc(max_mm, 1)

            def values(u, g, kt, par):
                pe.wait_ge(exp_made, u * 64 + 16 * g + 4 * kt + 4)
                if kt == 0:
                    if positive(u * NG + g):
                        pe.wait_ge(ev_made, u * NG + g)
                    if g == 0:
                        pe.wait_ge(v_made, u * 2 + 2)
                for j in range(G):
                    ins = pe.matmul(ps[32 * j:32 * j + 32, OUT], vaug[:, par, kt, G * g + j],
                                    probs[:, (4 * kt + j) % 8], start=kt == 0, stop=kt == QT - 1,
                                    tile_position=(0, 32 * j))
                ins.then_inc(pv_mm, 1)

            def start(u, cross, b):
                for name, bank in start_banks(cross):
                    item(name, bank, u, cross, b)
                    for m in START_MAXIMA.get(name, ()):
                        maximum(u, m)

            def end(u, cross, b):
                values(u, NG - 1, QT - 1, u % 2)
                for name, bank in end_banks():
                    item(name, bank, u, cross, b)

            def period(u, par, now, before, after):
                taken[MISC], taken[MISC + 1] = frees("v1", u), frees("nm0", u)
                banks = period_banks(before, after)
                for s in range(SLOTS):
                    g, kt, i = s // 8, s // 2 % 4, s % 2
                    if s % 8 < 2:
                        pe.wait_ge((nm_even, nm_odd)[s % 8], u * NG + g + 1)
                    for half in range(2):
                        e = 2 * s + half
                        if positive(u * 64 + e - 2):
                            pe.wait_ge(exp_made, u * 64 + e - 2)
                        pe.matmul(ps[:, SCORE + e % 3], kz[:, 2 * g + i, half, kt * P:(kt + 1) * P],
                                  qst[:, 2 * g + i, :], start=True, stop=True).then_inc(score_mm, 1)
                    for m in (2 * s + LEAD, 2 * s + LEAD + 1):
                        if m < 64:
                            maximum(u, m)
                        elif after:
                            maximum(u + 1, m - 64)
                    for name, bank in banks[s]:
                        item(name.strip("<>"), bank, *whose(name, u, now, before, after))
                    if s % 2:
                        if s >= 3:
                            values(u, (s - 3) // 8, (s - 3) // 2 % 4, par)
                        elif before:
                            values(u - 1, NG - 1, QT - 1, 1 - par)

            run(pe, start, period, end)


def gelu_phase(nc, ctx, A, scratch):
    sb = lambda name, shape, dt=F32: ctx.enter_context(nc.sbuf_tensor(name, shape, dt))
    sem = lambda name: ctx.enter_context(nc.semaphore(name))
    ident, topv, slots, tanh_g = A["ident"], A["topv"], A["slots"], A["tanh_g"]
    experts, running, first_row = A["experts"], A["running"], A["first_row"]
    fi_hi = sb("fi_hi", [P, KD, F], F32R)
    fi_lo = sb("fi_lo", [P, KD, F], F32R)
    fo_hi = sb("fo_hi", [P, KF, D], F32R)
    fo_lo = sb("fo_lo", [P, KF, D], F32R)
    gate_hi = sb("gate_hi", [P, KD, NE], F32R)
    gate_lo = sb("gate_lo", [P, KD, NE], F32R)
    rows = {n: sb("row_" + n, [P, D]) for n in GELU_ROWS}
    fi_b = sb("fi_b", [P, KF])
    neg_half = sb("neg_half2", [P, QT])
    before = sb("before", [P, P], BF16)
    ones_sq = sb("ones_sq", [P, P], BF16)
    fi_col = lambda mt: fi_b[:, mt:mt + 1]
    fi_raw, fo_raw = A["fi_raw"], A["fo_raw"]
    with nc.sbuf_tensor("gate_raw", [P, KD, NE], F32) as gate_raw, \
            nc.sbuf_tensor("g_raw", [P, 2], F32) as g_raw, \
            nc.semaphore("weights_in") as weights_in, \
            nc.semaphore("hi_made") as hi_made, \
            nc.semaphore("lo_made") as lo_made, \
            nc.semaphore("ones_made") as ones_made, \
            nc.semaphore("iota_made") as iota_made, \
            nc.semaphore("tanh_made") as tanh_made, \
            nc.Block() as block:
        raws = [(fi_raw[:, :, :], fi_hi[:, :, :], fi_lo[:, :, :]),
                (fo_raw[:, :, :], fo_hi[:, :, :], fo_lo[:, :, :]),
                (gate_raw[:, :, :], gate_hi[:, :, :], gate_lo[:, :, :])]

        @block.sync
        def _(sp):
            sp.dma_start(gate_raw[:, :, :], A["gate_w"]).then_inc(weights_in, 16)
            sp.dma_start(fi_b[:, :], A["fi_b"]).then_inc(weights_in, 16)
            for n in GELU_ROWS:
                sp.dma_start(rows[n][:, :], A[n].partition_broadcast(P)).then_inc(weights_in, 16)
            sp.dma_start(g_raw[:, 0:1], A["g_xattn"].partition_broadcast(P)).then_inc(weights_in, 16)
            sp.dma_start(g_raw[:, 1:2], A["g_ffn"].partition_broadcast(P)).then_inc(weights_in, 16)

        n_loads = 2 + len(GELU_ROWS) + 2

        @block.scalar
        def _(act):
            act.wait_ge(weights_in, 16 * n_loads)
            act.activation(tanh_g[:, :], g_raw[:, :], ACT.Tanh).then_inc(tanh_made, 1)

        @block.vector
        def _(dve):
            dve.memset(running[:, :, :], 0.0)
            dve.memset(neg_half[:, :], -0.5).then_inc(hi_made, 1)
            dve.wait_ge(A["gelu_weights_in"], 32)
            dve.wait_ge(weights_in, 16 * n_loads)
            for n, (raw, hi, lo) in enumerate(raws):
                dve.tensor_copy(hi, raw).then_inc(hi_made, 1)
            for n, (raw, hi, lo) in enumerate(raws):
                dve.wait_ge(hi_made, n + 2)
                dve.tensor_tensor(lo, raw, hi.bitcast(F32), ALU.subtract).then_inc(lo_made, 1)

        @block.gpsimd
        def _(pool):
            pool.memset(ones_sq[:, :], 1.0).then_inc(ones_made, 1)
            pool.memset(before[:, :], 1.0).then_inc(ones_made, 1)
            pool.wait_ge(ones_made, 2)
            pool.affine_select(out=before[:, :], in_=before[:, :], compare_op=ALU.is_gt, fill=0.0,
                               base=0, pattern=[[1, P]], channel_multiplier=-1)
            pool.iota(experts[:, :], pattern=[[1, NE]], base=0, channel_multiplier=0,
                      allow_small_or_imprecise_dtypes=True).then_inc(iota_made, 1)
            pool.wait_ge(iota_made, 1)
            pool.tensor_scalar(first_row[:, :], experts[:, :], float(CAP), 0.0, ALU.mult, ALU.add)

    x2_tok = sb("x2_tok", [P, 2, QT, D])
    resid = sb("g_resid", [P, 2, QT, D])
    x_tok = sb("gx_tok", [P, 2, QT, D])
    s_tok = sb("s_tok", [P, QT, D])
    h_tok = sb("gh_tok", [P, QT, D])
    hn_tok = sb("hn_tok", [P, 2, QT, D])
    a_hi = sb("g_hi", [P, 2, KD, S], F32R)
    a_lo = sb("g_lo", [P, 2, KD, S], F32R)
    hn_hi = sb("hn_hi", [P, KD, S], F32R)
    hn_lo = sb("hn_lo", [P, KD, S], F32R)
    gelu_out = sb("gelu_out", [P, 4, S])
    in_hi = sb("gelu_hi", [P, 4, S], F32R)
    in_lo = sb("gelu_lo", [P, 4, S], F32R)
    stats = sb("g_stats", [P, 3, QT, 6])
    mv = sb("g_mv", [P, 3, QT, 2])
    var_eps = sb("g_var_eps", [P, 3, QT])
    rstd = sb("g_rstd", [P, 3, QT])
    mean_sq = sb("mean_sq", [P, QT])
    settled = sb("g_settled", [P, 1])
    idle = sb("idle", [P, 2])
    logits = sb("logits", [P, QT, NE])
    max8 = sb("max8", [P, QT, 8])
    idx8 = sb("idx8", [P, QT, 8], U32)
    onehot = sb("onehot", [P, 2, QT, NE])
    weighed = sb("weighed", [P, 2, QT, NE])
    place = sb("place", [P, QT, NE])
    chosen_f = sb("chosen_f", [P, QT, 2])
    slot_f = sb("slot_f", [P, 2 * QT])
    picks = sb("picks", [P, QT, NE], BF16)
    slot_now = sb("slot_now", [P, 2 * QT], U32)
    ps = ctx.enter_context(nc.psum_tensor("ps_g", [P, 8, S], F32))
    FI, FO, MISC = 0, 2, 6
    BANK = {"hn0": 6, "hn1": 7, "lg": 6, "in0": 7, "rank": 6, "in1": 7}

    x2_in, x_in = [sem("x2_in0"), sem("x2_in1")], [sem("gx_in0"), sem("gx_in1")]
    tr_in, a_hi_made, a_lo_made = sem("g_tr_in"), sem("a_hi_made"), sem("a_lo_made")
    res_made = sem("g_res_made")
    fi_mm, gelu_made, in_hi_made, fo_mm = (sem(n) for n in
                                           ("fi_mm", "gelu_made", "gin_hi_made", "fo_mm"))
    lo_pool, lo_dve = sem("lo_pool"), sem("lo_dve")
    sum_made = sem("g_sum_made")
    s_stats, s_aggr, s_var, s_root, s_normed = (sem("s_" + n) for n in LN_STEPS)
    gained, shifted = sem("gained"), sem("shifted")
    y_made = sem("y_made")
    y_stats, y_aggr, y_var, y_root, h_normed = (sem("y_" + n) for n in LN_STEPS)
    h_stats, h_aggr, sq_made, h_var, h_root = (sem("h_" + n) for n in
                                               ("stats", "aggr", "sq", "var", "root"))
    hn_made, out_made = sem("hn_made"), sem("out_made")
    stored = sem("g_stored")
    tr_hn, hn_hi_made, hn_lo_made = sem("tr_hn"), sem("hn_hi_made"), sem("hn_lo_made")
    lg_mm, picks_made, rank_mm, slots_made = (sem(n) for n in
                                              ("lg_mm", "picks_made", "rank_mm", "slots_made"))
    route = sem("route")
    scattered = sem("scattered")

    def loads(b, k):
        return b * 8 + (16 - 8 * k)

    def run(eng, period):
        period(0, 0, True, False, False, True)
        period(1, 1, True, True, False, True)
        period(2, 0, True, True, True, True)
        with eng.Fori(1, B // 2 - 1) as j:
            for k in (1, 0):
                period(j * 2 + (2 - k), k, True, True, True, True)
        period(B - 1, 1, True, True, True, False)
        period(B, 0, False, True, True, False)
        period(B + 1, 1, False, False, True, False)

    with nc.Block() as block:

        @block.sync
        def _(sp):
            def load_x2(b, k):
                if positive(b - 1):
                    sp.wait_ge(res_made, b - 1)
                sp.dma_start(x2_tok[:, k], scratch["x2"][b]).then_inc(x2_in[k], 16)

            load_x2(0, 0)
            sp.dma_start(x_tok[:, 0], A["x"][0]).then_inc(x_in[0], 16)

            def period(i, k, gelu, first, second, following):
                if following:
                    load_x2(i + 1, 1 - k)
                if first:
                    sp.wait_ge(out_made, i * QT)
                    sp.dma_start(scratch["res"][i - 1], x_tok[:, 1 - k]).then_inc(stored, 16)
                if following:
                    if positive(i * 16):
                        sp.wait_ge(stored, i * 16)
                    sp.dma_start(x_tok[:, 1 - k], A["x"][i + 1]).then_inc(x_in[1 - k], 16)

            run(sp, period)
            sp.wait_ge(stored, 16 * B)

        @block.gpsimd
        def _(pool):
            def root(n, var, done, count):
                pool.wait_ge(var, count)
                pool.tensor_tensor(rstd[:, n], var_eps[:, n], neg_half[:, :], ALU.pow) \
                    .then_inc(done, 1)

            def row(name):
                return rows[name][:, :].unsqueeze(1).to_broadcast([P, QT, D])

            def residual(b, k):
                pool.wait_ge(tr_in, b * KD + KD)
                if positive(b * QT - QT):
                    pool.wait_ge(sum_made, b * QT - QT)
                pool.tensor_tensor(resid[:, k], x2_tok[:, k], row("fo_b"), ALU.add) \
                    .then_inc(res_made, 1)

            def scatter(b, k, s):
                for n in range(QT * s, QT * s + QT):
                    pool.indirect_dma_start(
                        out=scratch["xs"], in_=hn_tok[:, k, n % QT], in_offset=None,
                        out_offset=bass.IndirectOffsetOnAxis(ap=slot_now[:, n:n + 1], axis=0)) \
                        .then_inc(scattered, 16)

            residual(0, 0)

            def period(i, k, gelu, first, second, following):
                for s in range(KF):
                    if s == 2 and first:
                        root(0, s_var, s_root, i)
                    if s == 5 and first:
                        root(1, y_var, y_root, i)
                    if gelu and s in POOL_LO:
                        pool.wait_ge(in_hi_made, i * KF + s + 1)
                        pool.tensor_tensor(in_lo[:, s % 4], gelu_out[:, s % 4], in_hi[:, s % 4].bitcast(F32),
                                           ALU.subtract).then_inc(lo_pool, 1)
                    if s == 5 and following:
                        residual(i + 1, 1 - k)
                    if s == 6 and first:
                        root(2, h_var, h_root, i)
                    if s >= 6 and second:
                        if s == 6:
                            pool.wait_ge(slots_made, i - 1)
                            pool.tensor_tensor(idle[:, k:k + 1], neg_half[:, 0:1], neg_half[:, 0:1],
                                               ALU.mult)
                        scatter(i - 2, k, s - 6)

            run(pool, period)
            pool.wait_ge(scattered, 16 * 2 * QT * B)

        @block.scalar
        def _(act):
            def high(dst, bank, done, ready, count):
                act.wait_ge(ready, count)
                act.activation(dst, ps[:, bank], ACT.Copy).then_inc(done, 1)

            def high_in(b, k, mt):
                high(a_hi[:, k, mt], BANK[f"in{mt}"], a_hi_made, tr_in, b * KD + mt + 1)

            def high_hn(b, mt):
                high(hn_hi[:, mt], BANK[f"hn{mt}"], hn_hi_made, tr_hn, b * KD + mt + 1)

            for mt in range(KD):
                high_in(0, 0, mt)

            def period(i, k, gelu, first, second, following):
                for s in range(KF):
                    if gelu:
                        act.wait_ge(fi_mm, i * KF + s + 1)
                        earlier, done = (s - 4) % KF, i * 4 - (4 if s < 4 else 0)
                        if earlier in POOL_LO and (s >= 4 or positive(i)):
                            act.wait_ge(lo_pool, done + POOL_LO.index(earlier) + 1)
                        if earlier in DVE_LO and (s >= 4 or positive(i)):
                            act.wait_ge(lo_dve, done + DVE_LO.index(earlier) + 1)
                        act.activation(gelu_out[:, s % 4], ps[:, FI + s % 2], ACT.Gelu, bias=fi_col(s)) \
                            .then_inc(gelu_made, 1)
                        act.wait_ge(gelu_made, i * KF + s + 1)
                        if positive(i * KF + s - 3):
                            act.wait_ge(fo_mm, i * KF + s - 3)
                        act.activation(in_hi[:, s % 4], gelu_out[:, s % 4], ACT.Copy) \
                            .then_inc(in_hi_made, 1)
                    if s == 1 and second:
                        for mt in range(KD):
                            high_hn(i - 2, mt)
                    if s in (3, 5) and following:
                        high_in(i + 1, 1 - k, (s - 3) // 2)

            run(act, period)

        @block.vector
        def _(dve):
            def low(dst, high, bank, done, ready, count):
                dve.wait_ge(ready, count)
                dve.tensor_tensor(dst, ps[:, bank], high.bitcast(F32), ALU.subtract).then_inc(done, 1)

            def low_in(b, k, mt):
                low(a_lo[:, k, mt], a_hi[:, k, mt], BANK[f"in{mt}"], a_lo_made, a_hi_made,
                    b * KD + mt + 1)

            def low_hn(b, mt):
                low(hn_lo[:, mt], hn_hi[:, mt], BANK[f"hn{mt}"], hn_lo_made, hn_hi_made,
                    b * KD + mt + 1)

            def moments(n, src, in_stats, in_aggr, count):
                for qt in range(QT):
                    dve.bn_stats(stats[:, n, qt], src[:, qt]).then_inc(in_stats, 1)
                dve.wait_ge(in_stats, count * QT)
                dve.tensor_copy(settled[:, :], stats[:, n, 0, 0:1])
                for qt in range(QT):
                    dve.bn_aggr(mv[:, n, qt], stats[:, n, qt]).then_inc(in_aggr, 1)
                dve.wait_ge(in_aggr, count * QT)

            def variance(n, done):
                dve.tensor_scalar(var_eps[:, n], mv[:, n, :, 1], LN_EPS, None, ALU.add) \
                    .then_inc(done, 1)

            def normalise(n, dst, src, in_root, done, count):
                dve.wait_ge(in_root, count)
                for qt in range(QT):
                    dve.tensor_scalar(dst[:, qt], src[:, qt], mv[:, n, qt, 0:1],
                                      rstd[:, n, qt:qt + 1], ALU.subtract, ALU.mult) \
                        .then_inc(done, 1)

            def route_to_picks(b):
                n = [0]

                def link(ins):
                    n[0] += 1
                    ins.then_inc(route, 1)

                def settle():
                    dve.wait_ge(route, b * ROUTE_STEPS + n[0])

                dve.wait_ge(lg_mm, b + 1)
                link(dve.tensor_copy(logits[:, :, :], ps[:, BANK["lg"], 0:QT * NE]
                                     .rearrange("p (q e) -> p q e", q=QT)))
                settle()
                dve.tensor_copy(settled[:, :], logits[:, 0, 0:1])
                for qt in range(QT):
                    link(dve.max(max8[:, qt], logits[:, qt]))
                settle()
                dve.tensor_copy(settled[:, :], max8[:, 0, 0:1])
                for qt in range(QT):
                    link(dve.max_index(idx8[:, qt], max8[:, qt], logits[:, qt]))
                settle()
                link(dve.tensor_copy(topv[:, bass.ds(b * QT, QT), :], max8[:, :, 0:2]))
                link(dve.tensor_copy(chosen_f[:, :, :], idx8[:, :, 0:2]))
                link(dve.tensor_copy(running[:, 0], running[:, QT]))
                settle()
                for s in range(2):
                    link(dve.tensor_tensor(
                        onehot[:, s], experts[:, :].unsqueeze(1).to_broadcast([P, QT, NE]),
                        chosen_f[:, :, s].unsqueeze(2).to_broadcast([P, QT, NE]), ALU.is_equal))
                settle()
                dve.tensor_tensor(picks[:, :, :], onehot[:, 0], onehot[:, 1], ALU.add) \
                    .then_inc(picks_made, 1)
                return n[0]

            def route_to_slots(b, begun):
                n = [begun]

                def link(ins):
                    n[0] += 1
                    ins.then_inc(route, 1)
                    dve.wait_ge(route, b * ROUTE_STEPS + n[0])

                dve.wait_ge(rank_mm, b + 1)
                ranks = ps[:, BANK["rank"]]
                for qt in range(QT):
                    link(dve.tensor_tensor(running[:, qt + 1], ranks[:, (QT + qt) * NE:(QT + qt + 1) * NE],
                                           running[:, qt], ALU.add))
                link(dve.tensor_tensor(place[:, :, :],
                                       ranks[:, 0:QT * NE].rearrange("p (q e) -> p q e", q=QT),
                                       running[:, 0:QT], ALU.add))
                link(dve.tensor_tensor(place[:, :, :], place[:, :, :],
                                       first_row[:, :].unsqueeze(1).to_broadcast([P, QT, NE]),
                                       ALU.add))
                for s in range(2):
                    link(dve.tensor_tensor(weighed[:, s], onehot[:, s], place[:, :, :], ALU.mult))
                link(dve.tensor_reduce(slot_f[:, :], weighed[:, :, :, :].rearrange("p s q e -> p (s q) e"),
                                       AX.X, ALU.add))
                link(dve.tensor_copy(slots[:, bass.ds(b * 2 * QT, 2 * QT)], slot_f[:, :]))
                if positive(b):
                    dve.wait_ge(scattered, b * (16 * 2 * QT))
                dve.tensor_copy(slot_now[:, :], slot_f[:, :]).then_inc(slots_made, 1)
                assert n[0] == ROUTE_STEPS, n[0]

            for mt in range(KD):
                low_in(0, 0, mt)
            begun = [0]

            def layer_sum(i, k):
                dve.wait_ge(fo_mm, i * KF)
                dve.wait_ge(res_made, i)
                if positive(i * QT - QT):
                    dve.wait_ge(y_made, i * QT - QT)
                for qt in range(QT):
                    dve.tensor_tensor(s_tok[:, qt], ps[:, FO + qt, 0:D], resid[:, k, qt],
                                      ALU.add).then_inc(sum_made, 1)
                dve.wait_ge(sum_made, i * QT)
                moments(0, s_tok, s_stats, s_aggr, i)
                variance(0, s_var)

            def mixer_output(i):
                normalise(0, s_tok, s_tok, s_root, s_normed, i)
                dve.wait_ge(s_normed, i * QT)
                for qt in range(QT):
                    dve.tensor_tensor(s_tok[:, qt], s_tok[:, qt], rows["fo_g"][:, :],
                                      ALU.mult).then_inc(gained, 1)

            def gated_sum(i, k):
                dve.wait_ge(gained, i * QT)
                for qt in range(QT):
                    dve.tensor_tensor(s_tok[:, qt], s_tok[:, qt], rows["fo_be"][:, :],
                                      ALU.add).then_inc(shifted, 1)
                dve.wait_ge(shifted, i * QT)
                dve.wait_ge(x_in[k], loads(i - 1, k))
                for qt in range(QT):
                    dve.scalar_tensor_tensor(x_tok[:, k, qt], s_tok[:, qt], tanh_g[:, 0:1],
                                             x_tok[:, k, qt], ALU.mult, ALU.add) \
                        .then_inc(y_made, 1)
                dve.wait_ge(y_made, i * QT)
                moments(1, x_tok[:, k], y_stats, y_aggr, i)
                variance(1, y_var)

            def hidden(i, k):
                normalise(1, h_tok, x_tok[:, k], y_root, h_normed, i)
                dve.wait_ge(h_normed, i * QT)
                moments(2, h_tok, h_stats, h_aggr, i)
                dve.tensor_tensor(mean_sq[:, :], mv[:, 2, :, 0], mv[:, 2, :, 0], ALU.mult) \
                    .then_inc(sq_made, 1)
                dve.wait_ge(sq_made, i)
                dve.scalar_tensor_tensor(var_eps[:, 2], mean_sq[:, :], RMS_EPS, mv[:, 2, :, 1],
                                         ALU.add, ALU.add).then_inc(h_var, 1)

            def outputs(i, k):
                dve.wait_ge(h_root, i)
                if positive(i - 2):
                    dve.wait_ge(scattered, (i - 2) * (16 * 2 * QT))
                for qt in range(QT):
                    dve.scalar_tensor_tensor(hn_tok[:, k, qt], h_tok[:, qt],
                                             rstd[:, 2, qt:qt + 1], rows["rms"][:, :],
                                             ALU.mult, ALU.mult).then_inc(hn_made, 1)
                for qt in range(QT):
                    dve.scalar_tensor_tensor(x_tok[:, k, qt], h_tok[:, qt], tanh_g[:, 1:2],
                                             x_tok[:, k, qt], ALU.mult, ALU.add) \
                        .then_inc(out_made, 1)

            def low_slice(i, s):
                dve.wait_ge(in_hi_made, i * KF + s + 1)
                dve.tensor_tensor(in_lo[:, s % 4], gelu_out[:, s % 4],
                                  in_hi[:, s % 4].bitcast(F32), ALU.subtract).then_inc(lo_dve, 1)

            def period(i, k, gelu, first, second, following):
                for s in range(KF):
                    if s == 2 and second:
                        for mt in range(KD):
                            low_hn(i - 2, mt)
                    if s in (4, 6) and following:
                        low_in(i + 1, 1 - k, (s - 4) // 2)
                    if s == 5 and second:
                        route_to_slots(i - 2, begun[0])
                    if gelu and s in DVE_LO:
                        low_slice(i, s)
                    if first:
                        if s == 2:
                            layer_sum(i, 1 - k)
                        if s == 3:
                            mixer_output(i)
                        if s == 4:
                            gated_sum(i, 1 - k)
                        if s == 6:
                            hidden(i, 1 - k)
                        if s == 7:
                            outputs(i, 1 - k)
                    if s == 3 and second:
                        begun[0] = route_to_picks(i - 2)

            run(dve, period)

        @block.tensor
        def _(pe):
            def turn(bank, src, mt):
                for qt in range(QT):
                    ins = pe.transpose(ps[:, bank, qt * P:(qt + 1) * P],
                                       src[:, qt, mt * P:(mt + 1) * P], ident[:, :])
                return ins

            def product(out, left, right):
                terms = [t for ls, rs in zip(left, right) for t in split_products(*ls, *rs)]
                for n, (l_, r_) in enumerate(terms):
                    ins = pe.matmul(out, l_, r_, start=n == 0, stop=n == len(terms) - 1)
                return ins

            def turn_in(b, k, mt):
                if mt == 0:
                    pe.wait_ge(x2_in[k], loads(b, k))
                if positive(b * KD + mt):
                    pe.wait_ge(a_lo_made, b * KD + mt)
                turn(BANK[f"in{mt}"], x2_tok[:, k], mt).then_inc(tr_in, 1)

            def turn_hn(b, k, mt):
                if mt == 0:
                    pe.wait_ge(hn_made, b * QT + QT)
                    if positive(b):
                        pe.wait_ge(slots_made, b)
                turn(BANK[f"hn{mt}"], hn_tok[:, k], mt).then_inc(tr_hn, 1)

            def second_product(b, mt):
                if mt in POOL_LO:
                    pe.wait_ge(lo_pool, b * 4 + POOL_LO.index(mt) + 1)
                else:
                    pe.wait_ge(lo_dve, b * 4 + DVE_LO.index(mt) + 1)
                if mt == 0:
                    if positive(b * QT):
                        pe.wait_ge(sum_made, b * QT)
                for qt in range(QT):
                    c = slice(qt * P, (qt + 1) * P)
                    terms = split_products(in_hi[:, mt % 4, c], in_lo[:, mt % 4, c], fo_hi[:, mt],
                                           fo_lo[:, mt])
                    for n, (left, right) in enumerate(terms):
                        ins = pe.matmul(ps[:, FO + qt, 0:D], left, right, start=mt == 0 and n == 0,
                                        stop=mt == KF - 1 and n == len(terms) - 1)
                ins.then_inc(fo_mm, 1)

            for mt in range(KD):
                turn_in(0, 0, mt)

            def period(i, k, gelu, first, second, following):
                for s in range(KF):
                    if gelu:
                        if s == 0:
                            pe.wait_ge(a_lo_made, i * KD + KD)
                        if positive(i * KF + s - 1):
                            pe.wait_ge(gelu_made, i * KF + s - 1)
                        c = slice(s * P, (s + 1) * P)
                        product(ps[:, FI + s % 2], [(fi_hi[:, m, c], fi_lo[:, m, c]) for m in range(KD)],
                                [(a_hi[:, k, m], a_lo[:, k, m]) for m in range(KD)]) \
                            .then_inc(fi_mm, 1)
                    if s < 3 and first:
                        second_product(i - 1, KF - 3 + s)
                    if s >= 3 and gelu:
                        second_product(i, s - 3)
                    if s == 1 and second:
                        for mt in range(KD):
                            turn_hn(i - 2, k, mt)
                    if s == 3 and second:
                        pe.wait_ge(hn_lo_made, (i - 2) * KD + KD)
                        for qt in range(QT):
                            c = slice(qt * P, (qt + 1) * P)
                            ins = product(ps[:, BANK["lg"], qt * NE:(qt + 1) * NE],
                                          [(hn_hi[:, m, c], hn_lo[:, m, c]) for m in range(KD)],
                                          [(gate_hi[:, m], gate_lo[:, m]) for m in range(KD)])
                        ins.then_inc(lg_mm, 1)
                    if s == 3 and following:
                        turn_in(i + 1, 1 - k, 0)
                    if s == 4 and second:
                        pe.wait_ge(picks_made, i - 1)
                        flat = picks[:, :, :].rearrange("p q e -> p (q e)")
                        pe.matmul(ps[:, BANK["rank"], 0:QT * NE], before[:, :], flat, start=True,
                                  stop=True)
                        pe.matmul(ps[:, BANK["rank"], QT * NE:2 * QT * NE], ones_sq[:, :], flat,
                                  start=True, stop=True).then_inc(rank_mm, 1)
                    if s == 5 and following:
                        turn_in(i + 1, 1 - k, 1)

            run(pe, period)


def expert_phase(nc, ctx, A, scratch):
    sb = lambda name, shape, dt=F32: ctx.enter_context(nc.sbuf_tensor(name, shape, dt))
    sem = lambda name: ctx.enter_context(nc.semaphore(name))
    ident, experts, running = A["ident"], A["experts"], A["running"]

    table = sb("table", [P, 2, STEPS], I32)
    w_raw = sb("we_raw", [P, 3, KD * I])
    raw_in = [sem(f"raw_in{c}") for c in range(3)]
    counts_i = sb("counts_i", [P, NE], I32)
    zeros = sb("zeros", [P, GT, D])
    ps = ctx.enter_context(nc.psum_tensor("ps_e", [P, 8, 512], F32))

    with nc.sbuf_tensor("steps_f", [P, STEPS], F32) as steps_f, \
            nc.sbuf_tensor("firsts", [P, NE], F32) as firsts, \
            nc.sbuf_tensor("need", [P, NE], F32) as need, \
            nc.sbuf_tensor("upto", [P, 4, NE], F32) as upto, \
            nc.sbuf_tensor("past", [P, NE, STEPS], F32) as past, \
            nc.sbuf_tensor("above", [P, 2 * B * QT, NE], F32) as above, \
            nc.sbuf_tensor("shift", [P, NE], F32) as shift, \
            nc.sbuf_tensor("moved", [P, 2 * B * QT], F32) as moved, \
            nc.sbuf_tensor("found", [P, 6, STEPS], F32) as found, \
            nc.semaphore("iota_s") as iota_s, nc.semaphore("chain") as chain_sem, \
            nc.semaphore("counts_made") as counts_made, nc.semaphore("table_made") as table_made, \
            nc.semaphore("padded") as padded, \
            nc.Block() as block:
        @block.gpsimd
        def _(pool):
            pool.iota(steps_f[:, :], pattern=[[1, STEPS]], base=0, channel_multiplier=0,
                      allow_small_or_imprecise_dtypes=True).then_inc(iota_s, 1)

        @block.vector
        def _(dve):
            n = [0]

            def step(ins):
                n[0] += 1
                ins.then_inc(chain_sem, 1)
                dve.wait_ge(chain_sem, n[0])

            count = running[:, QT]
            step(dve.tensor_copy(counts_i[:, :], count))
            dve.memset(zeros[:, :, :], 0.0).then_inc(counts_made, 1)
            dve.wait_ge(iota_s, 1)
            over = past[:, :, 0:T // GR + 1]
            j = steps_f[:, 0:T // GR + 1]
            step(dve.tensor_scalar(found[:, 0, 0:T // GR + 1], j, float(GR), None, ALU.mult))
            step(dve.tensor_tensor(over, count.unsqueeze(2).to_broadcast([P, NE, T // GR + 1]),
                                   found[:, 0, 0:T // GR + 1].unsqueeze(1)
                                   .to_broadcast([P, NE, T // GR + 1]), ALU.is_gt))
            step(dve.tensor_reduce(need[:, :], over, AX.X, ALU.add))
            step(dve.tensor_copy(upto[:, 0], need[:, :]))
            for r, reach in enumerate((1, 2, 4)):
                step(dve.tensor_copy(upto[:, r + 1, 0:reach], upto[:, r, 0:reach]))
                step(dve.tensor_tensor(upto[:, r + 1, reach:], upto[:, r, reach:],
                                       upto[:, r, 0:NE - reach], ALU.add))
            step(dve.tensor_tensor(past[:, :, :],
                                   steps_f[:, :].unsqueeze(1).to_broadcast([P, NE, STEPS]),
                                   upto[:, 3].unsqueeze(2).to_broadcast([P, NE, STEPS]), ALU.is_ge))
            by_step = past[:, :, :].rearrange("p e n -> p n e")
            expert, begun, spare, inside, row = (found[:, m] for m in range(5))
            step(dve.tensor_reduce(expert, by_step, AX.X, ALU.add))
            step(dve.tensor_scalar(spare, expert, float(NE), None, ALU.is_ge))
            step(dve.tensor_scalar(expert, expert, float(NE - 1), None, ALU.min))
            step(dve.tensor_tensor(past[:, :, :], past[:, :, :],
                                   need[:, :].unsqueeze(2).to_broadcast([P, NE, STEPS]), ALU.mult))
            step(dve.tensor_reduce(begun, by_step, AX.X, ALU.add))
            step(dve.tensor_tensor(inside, steps_f[:, :], begun, ALU.subtract))
            step(dve.tensor_scalar(found[:, 5], spare, -1.0, 1.0, ALU.mult, ALU.add))
            step(dve.tensor_tensor(inside, inside, found[:, 5], ALU.mult))
            step(dve.tensor_scalar(inside, inside, float(GR), None, ALU.mult))
            step(dve.scalar_tensor_tensor(row, expert, float(CAP), inside, ALU.mult, ALU.add))
            step(dve.tensor_copy(table[:, 1], row))
            dve.tensor_copy(table[:, 0], expert).then_inc(table_made, 1)
            slots = A["slots"][:, :]
            n_slots = 2 * B * QT
            step(dve.tensor_tensor(above[:, :, :], slots.unsqueeze(2).to_broadcast([P, n_slots, NE]),
                                   A["first_row"][:, :].unsqueeze(1).to_broadcast([P, n_slots, NE]),
                                   ALU.is_ge))
            step(dve.tensor_scalar(shift[:, 1:NE], need[:, 0:NE - 1], float(GR), float(-CAP),
                                   ALU.mult, ALU.add))
            step(dve.memset(shift[:, 0:1], 0.0))
            step(dve.tensor_tensor(above[:, :, :], above[:, :, :],
                                   shift[:, :].unsqueeze(1).to_broadcast([P, n_slots, NE]), ALU.mult))
            step(dve.tensor_reduce(moved[:, :], above[:, :, :], AX.X, ALU.add))
            step(dve.tensor_tensor(A["picks"][:, :], slots, moved[:, :], ALU.add))

        @block.sync
        def _(sp):
            sp.wait_ge(counts_made, 1)
            for e in range(NE):
                at = sp.value_load(counts_i[0:1, e:e + 1], min_val=0, max_val=T)
                sp.dma_start(scratch["xs"][bass.ds(at + e * CAP, GR), :]
                             .rearrange("(t p) d -> p t d", p=P), zeros[:, :, :]).then_inc(padded, 16)
            sp.wait_ge(table_made, 1)
            first = sp.value_load(table[0:1, 0, 0:1], min_val=0, max_val=NE - 1)
            for c in range(3):
                sp.dma_start(w_raw[:, c], A["experts_w"][bass.ds(first, 1), c]
                             .rearrange("o p n -> (o p) n")).then_inc(raw_in[c], 16)
            sp.wait_ge(padded, 16 * NE)

    w_hi = sb("we_hi", [P, 2, 3, KD * I], F32R)
    w_lo = sb("we_lo", [P, 2, 3, KD * I], F32R)
    x_raw = sb("x_raw", [P, 2, GT, D])
    x_hi = sb("x_hi", [P, 2, KD, GR], F32R)
    x_lo = sb("x_lo", [P, 2, KD, GR], F32R)
    silu = sb("silu", [P, 2, GR])
    u_f = sb("u_f", [P, 2, GR])
    u_hi = sb("u_hi", [P, KI, GR], F32R)
    u_lo = sb("u_lo", [P, KI, GR], F32R)
    eo = sb("eo_sb", [P, GT, D])
    x_in = [sem("x_in0"), sem("x_in1")]
    whi_made = sem("whi_made")
    wlo_made = sem("wlo_made")
    xt_mm = sem("xt_mm")
    xhi_made = sem("xhi_made")
    xlo_made = sem("xlo_made")
    up_mm = sem("up_mm")
    silu_made = sem("silu_made")
    u_made = sem("u_made")
    uhi_made = sem("uhi_made")
    ulo_made = sem("ulo_made")
    down_kt = sem("down_kt")
    eo_made = sem("eo_made")
    eo_out = sem("eo_out")

    def over_steps(eng, body, prologue=None):
        for k in range(2):
            body(0, k, False)
        with eng.Fori(1, STEPS // 2 - 1) as i:
            for k in range(2):
                body(i, k, False)
        for k in range(2):
            body(STEPS // 2 - 1, k, k == 1)

    with nc.Block() as block:
        @block.sync
        def _(sp):
            def body(i, k, last):
                n = i * 2 + k
                e = sp.value_load(table[0:1, 0, bass.ds(n, 1)], min_val=0, max_val=NE - 1)
                r = sp.value_load(table[0:1, 1, bass.ds(n, 1)], min_val=0, max_val=NE * CAP - GR)
                if positive(n * 2 - 2):
                    sp.wait_ge(xt_mm, n * 2 - 2)
                sp.dma_start(x_raw[:, k], scratch["xs"][bass.ds(r, GR), :]
                             .rearrange("(t p) d -> p t d", p=P)).then_inc(x_in[k], 16)
                for c in range(3):
                    if isinstance(n, int) and n == 0:
                        continue
                    if positive(n * 3 - 2 + c):
                        sp.wait_ge(wlo_made, n * 3 - 2 + c)
                    sp.dma_start(w_raw[:, c], A["experts_w"][bass.ds(e, 1), c]
                                 .rearrange("o p n -> (o p) n")).then_inc(raw_in[c], 16)

            over_steps(sp, body)

        @block.vector
        def _(dve):
            def hi_of_w(n, k, c):
                dve.wait_ge(raw_in[c], n * 16 + 16)
                if c == 2 and positive(n * KI - KI):
                    dve.wait_ge(down_kt, n * KI - KI)
                dve.tensor_copy(w_hi[:, k, c], w_raw[:, c]).then_inc(whi_made, 1)

            def lo_of_w(n, k, c):
                dve.wait_ge(whi_made, n * 3 + c + 1)
                dve.tensor_tensor(w_lo[:, k, c], w_raw[:, c], w_hi[:, k, c].bitcast(F32),
                                  ALU.subtract).then_inc(wlo_made, 1)

            def lo_of_x(n, k, mt):
                dve.wait_ge(xhi_made, n * 2 + mt + 1)
                dve.tensor_tensor(x_lo[:, k, mt], ps[:, 7, 0:GR], x_hi[:, k, mt].bitcast(F32),
                                  ALU.subtract).then_inc(xlo_made, 1)

            lo_of_x(0, 0, 0)
            lo_of_x(0, 0, 1)
            for c in range(3):
                hi_of_w(0, 0, c)
                lo_of_w(0, 0, c)

            def body(i, k, last):
                n = i * 2 + k
                for it in range(KI):
                    slot = (k + it) % 2
                    dve.wait_ge(silu_made, n * KI + it + 1)
                    dve.wait_ge(up_mm, n * (2 * KI) + 2 * it + 2)
                    if positive(n * KI + it - 1):
                        dve.wait_ge(ulo_made, n * KI + it - 1)
                    dve.tensor_tensor(u_f[:, slot], ps[:, 2 * slot + 1, 0:GR], silu[:, slot],
                                      ALU.mult).then_inc(u_made, 1)
                    if last:
                        continue
                    if it < 6:
                        (hi_of_w, lo_of_w)[it % 2](n + 1, 1 - k, it // 2)
                    if it in (4, 6):
                        lo_of_x(n + 1, 1 - k, (it - 4) // 2)

            over_steps(dve, body)

        @block.gpsimd
        def _(pool):
            def body(i, k, last):
                n = i * 2 + k
                for it in range(KI):
                    slot = (k + it) % 2
                    pool.wait_ge(uhi_made, n * KI + it + 1)
                    pool.tensor_tensor(u_lo[:, it], u_f[:, slot], u_hi[:, it].bitcast(F32),
                                       ALU.subtract).then_inc(ulo_made, 1)

            over_steps(pool, body)

        @block.scalar
        def _(act):
            def hi_of_x(n, k, mt):
                act.wait_ge(xt_mm, n * 2 + mt + 1)
                act.activation(x_hi[:, k, mt], ps[:, 7, 0:GR], ACT.Copy).then_inc(xhi_made, 1)

            def hi_of_u(n, k, it):
                act.wait_ge(u_made, n * KI + it + 1)
                if positive(n * KI + it + 1 - KI):
                    act.wait_ge(down_kt, n * KI + it + 1 - KI)
                act.activation(u_hi[:, it], u_f[:, (k + it) % 2], ACT.Copy).then_inc(uhi_made, 1)

            def put_out(n):
                act.wait_ge(down_kt, n * KI + KI)
                if positive(n * 16):
                    act.wait_ge(eo_out, n * 16)
                act.activation(eo[:, :, :], ps[:, 4:4 + GT, 0:D], ACT.Copy).then_inc(eo_made, 1)
                act.wait_ge(eo_made, n + 1)
                act.dma_start(scratch["eo"][bass.ds(n * GR, GR), :].rearrange("(t p) d -> p t d", p=P),
                              eo[:, :, :]).then_inc(eo_out, 16)

            hi_of_x(0, 0, 0)
            hi_of_x(0, 0, 1)

            def body(i, k, last):
                n = i * 2 + k
                for it in range(KI):
                    slot = (k + it) % 2
                    act.wait_ge(up_mm, n * (2 * KI) + 2 * it + 1)
                    if positive(n * KI + it - 1):
                        act.wait_ge(u_made, n * KI + it - 1)
                    act.activation(silu[:, slot], ps[:, 2 * slot, 0:GR], ACT.Silu) \
                        .then_inc(silu_made, 1)
                    if it:
                        hi_of_u(n, k, it - 1)
                    if it == 2 and not (isinstance(n, int) and n == 0):
                        put_out(n - 1)
                    if it in (3, 6) and not last:
                        hi_of_x(n + 1, 1 - k, it // 6)
                hi_of_u(n, k, KI - 1)

            over_steps(act, body)
            put_out(STEPS - 1)
            act.wait_ge(eo_out, 16 * STEPS)

        @block.tensor
        def _(pe):
            def turn_rows(i, n, k, mt):
                if mt == 0:
                    pe.wait_ge(x_in[k], i * 16 + 16)
                if positive(n * 2 + mt):
                    pe.wait_ge(xlo_made, n * 2 + mt)
                for t in range(GT):
                    ins = pe.transpose(ps[:, 7, t * P:(t + 1) * P],
                                       x_raw[:, k, t, mt * P:(mt + 1) * P], ident[:, :])
                ins.then_inc(xt_mm, 1)

            def up(n, k, it):
                slot = (k + it) % 2
                if positive(n * KI + it - 1):
                    pe.wait_ge(u_made, n * KI + it - 1)
                for c in range(2):
                    if it == 0:
                        pe.wait_ge(wlo_made, n * 3 + c + 1)
                    cut = lambda part, kt: part[:, k, c, kt * I + it * P:kt * I + (it + 1) * P]
                    terms = [t for kt in range(KD)
                             for t in split_products(cut(w_hi, kt), cut(w_lo, kt),
                                                     x_hi[:, k, kt], x_lo[:, k, kt])]
                    for m, (left, right) in enumerate(terms):
                        ins = pe.matmul(ps[:, 2 * slot + c, 0:GR], left, right, start=m == 0,
                                        stop=m == len(terms) - 1)
                    ins.then_inc(up_mm, 1)

            def down(n, k, it):
                if it == 0:
                    pe.wait_ge(wlo_made, n * 3 + 3)
                    if positive(n):
                        pe.wait_ge(eo_made, n)
                pe.wait_ge(ulo_made, n * KI + it + 1)
                w2 = slice(it * D, (it + 1) * D)
                for t in range(GT):
                    rows = slice(t * P, (t + 1) * P)
                    terms = split_products(u_hi[:, it, rows], u_lo[:, it, rows],
                                           w_hi[:, k, 2, w2], w_lo[:, k, 2, w2])
                    for m, (left, right) in enumerate(terms):
                        ins = pe.matmul(ps[:, 4 + t, 0:D], left, right, start=it == 0 and m == 0,
                                        stop=it == KI - 1 and m == len(terms) - 1)
                ins.then_inc(down_kt, 1)

            turn_rows(0, 0, 0, 0)
            turn_rows(0, 0, 0, 1)

            def body(i, k, last):
                n = i * 2 + k
                pe.wait_ge(xlo_made, n * 2 + 2)
                for it in range(KI):
                    up(n, k, it)
                    if it >= 3:
                        down(n, k, it - 3)
                    elif it < 2 and not (isinstance(n, int) and n == 0):
                        down(n - 1, 1 - k, KI - 2 + it)
                    if it in (2, 5) and not last:
                        turn_rows(i + k, n + 1, 1 - k, it // 5)
                down(n, k, KI - 3)

            over_steps(pe, body)
            for it in (KI - 2, KI - 1):
                down(STEPS - 1, (STEPS - 1) % 2, it)


def combine_phase(nc, ctx, A, scratch, out):
    sb = lambda name, shape, dt=F32: ctx.enter_context(nc.sbuf_tensor(name, shape, dt))
    sem = lambda name: ctx.enter_context(nc.semaphore(name))
    topv, slots, tanh_g = A["topv"], A["picks"], A["tanh_g"]
    share = sb("share", [P, 4, B * QT])
    tmp = sb("share_tmp", [P, 2, B * QT])
    picked = sb("picked", [P, 2, 2, QT, D])
    res = sb("res_sb", [P, 2, QT, D])
    picked_in = [sem("picked_in0"), sem("picked_in1")]
    res_in = [sem("res_in0"), sem("res_in1")]
    gap_made, exp_made, share_made, sum_made, out_sent = (
        sem(n) for n in ("gap_made", "share_exp", "share_made", "sum_made", "out_sent"))

    with nc.Block() as block:
        @block.sync
        def _(sp):
            for b in range(B):
                if b >= 2:
                    sp.wait_ge(out_sent, 16 * (b - 1))
                sp.dma_start(res[:, b % 2], scratch["res"][b]).then_inc(res_in[b % 2], 16)
                if b:
                    sp.wait_ge(sum_made, 2 * QT * b)
                    sp.dma_start(out[b - 1], res[:, (b - 1) % 2]).then_inc(out_sent, 16)
            sp.wait_ge(sum_made, 2 * QT * B)
            sp.dma_start(out[B - 1], res[:, (B - 1) % 2]).then_inc(out_sent, 16)
            sp.wait_ge(out_sent, 16 * B)

        @block.gpsimd
        def _(pool):
            for b in range(B):
                if b >= 2:
                    pool.wait_ge(sum_made, 2 * QT * (b - 1))
                for m in range(2 * QT):
                    n = 2 * QT * b + m
                    pool.indirect_dma_start(
                        out=picked[:, b % 2, m // QT, m % QT], out_offset=None, in_=scratch["eo"],
                        in_offset=bass.IndirectOffsetOnAxis(ap=slots[:, n:n + 1], axis=0)) \
                        .then_inc(picked_in[b % 2], 16)

        @block.scalar
        def _(act):
            act.wait_ge(gap_made, 1)
            act.activation(tmp[:, 1], tmp[:, 0], ACT.Exp).then_inc(exp_made, 1)

        @block.vector
        def _(dve):
            dve.tensor_tensor(tmp[:, 0], topv[:, :, 1], topv[:, :, 0], ALU.subtract) \
                .then_inc(gap_made, 1)
            dve.wait_ge(exp_made, 1)
            dve.tensor_scalar(share[:, 0], tmp[:, 1], 1.0, None, ALU.add).then_inc(share_made, 1)
            dve.wait_ge(share_made, 1)
            dve.reciprocal(share[:, 1], share[:, 0]).then_inc(share_made, 1)
            dve.wait_ge(share_made, 2)
            dve.tensor_scalar(share[:, 2], share[:, 1], tanh_g[:, 1:2], None, ALU.mult) \
                .then_inc(share_made, 1)
            dve.wait_ge(share_made, 3)
            dve.tensor_tensor(share[:, 3], share[:, 2], tmp[:, 1], ALU.mult).then_inc(share_made, 1)
            dve.wait_ge(share_made, 4)
            for b in range(B):
                k = b % 2
                dve.wait_ge(res_in[k], 16 * (b // 2 + 1))
                dve.wait_ge(picked_in[k], 16 * 2 * QT * (b // 2 + 1))
                for s in range(2):
                    if s:
                        dve.wait_ge(sum_made, QT * (2 * b + 1))
                    for qt in range(QT):
                        n = QT * b + qt
                        dve.scalar_tensor_tensor(res[:, k, qt], picked[:, k, s, qt],
                                                 share[:, 2 + s, n:n + 1], res[:, k, qt],
                                                 ALU.mult, ALU.add).then_inc(sum_made, 1)


def build(nc, A, out):
    with ExitStack() as ctx:
        sb = lambda name, shape, dt=F32: ctx.enter_context(nc.sbuf_tensor(name, shape, dt))
        A["ident"] = sb("ident", [P, P])
        A["spare"] = sb("spare", [P, 8, S])
        A["fi_raw"] = A["spare"][:, 0:4].rearrange("p (k a) n -> p k (a n)", k=KD)
        A["fo_raw"] = A["spare"][:, 4:8].rearrange("p k (a n) -> p (k a) n", n=D)
        A["gelu_weights_in"] = ctx.enter_context(nc.semaphore("gelu_weights_in"))
        A["tanh_g"] = sb("tanh_g", [P, 2])
        A["topv"] = sb("topv", [P, B * QT, 2])
        A["slots"] = sb("slots", [P, B * 2 * QT])
        A["picks"] = sb("picks_at", [P, B * 2 * QT], U32)
        A["experts"] = sb("experts", [P, NE])
        A["first_row"] = sb("first_row", [P, NE])
        A["running"] = sb("running", [P, QT + 1, NE])
        xs = nc.dram_tensor("xs", [NE * CAP, D], F32).ap()
        eo = nc.dram_tensor("eo", [STEPS * GR, D], F32).ap()
        res = nc.dram_tensor("res", [B, P, QT, D], F32).ap()
        x2 = nc.dram_tensor("x2", [B, P, QT, D], F32).ap()
        scratch = {"x2": x2, "xs": xs, "eo": eo, "res": res}
        with nc.semaphore("ident_zero") as ident_zero, nc.Block() as block:
            @block.gpsimd
            def _(pool):
                ident = A["ident"]
                pool.memset(ident[:, :], 0.0).then_inc(ident_zero, 1)
                pool.wait_ge(ident_zero, 1)
                pool.affine_select(out=ident[:, :], in_=ident[:, :], compare_op=ALU.not_equal,
                                   fill=1.0, base=0, pattern=[[-1, P]], channel_multiplier=1)
        with ExitStack() as phase:
            attention_phase(nc, phase, A, scratch)
        with ExitStack() as phase:
            gelu_phase(nc, phase, A, scratch)
        with ExitStack() as phase:
            expert_phase(nc, phase, A, scratch)
        with ExitStack() as phase:
            combine_phase(nc, phase, A, scratch, out)


def kernel(**inputs):
    import numpy as np
    import concourse.bacc as bacc
    from concourse.bass_utils import run_bass_kernel_spmd

    nc = bacc.Bacc("TRN2", target_bir_lowering=False, num_devices=1)
    arrays, A = {}, {}

    def give(name, a):
        a = np.ascontiguousarray(a)
        arrays["in_" + name] = a
        A[name] = nc.dram_tensor("in_" + name, a.shape, mybir.dt.from_np(a.dtype),
                                 kind="ExternalInput").ap()

    def stack(w):
        return w.reshape(-1, P, w.shape[1]).transpose(1, 0, 2)

    X = {k[len("L0_xattn_"):]: np.asarray(v) for k, v in inputs.items() if k.startswith("L0_xattn_")}
    tokens = lambda a: np.asarray(a).reshape(B, QT, P, D).transpose(0, 2, 1, 3)
    give("x", tokens(inputs["x"]))
    give("ctx", tokens(inputs["ctx_1024"]))
    give("mask", np.asarray(inputs["mask_Bx1x1xS2_ff0"]).reshape(B, 1, S))
    give("attn_w", np.stack([stack(X[a + n + "_w"])
                             for a in "cs" for n in "qkvo"], axis=1))
    E1, E2, E3 = (np.asarray(inputs["L0_ffn_w" + n]) for n in "123")
    lay = lambda w: w.reshape(NE, -1, P, w.shape[2]).transpose(0, 2, 1, 3).reshape(NE, P, -1)
    give("experts_w", np.stack([lay(E1.transpose(0, 2, 1)), lay(E3.transpose(0, 2, 1)),
                                lay(E2.transpose(0, 2, 1))], axis=1))
    give("fi_w", stack(X["fi_w"]))
    give("fo_w", stack(X["fo_w"]))
    give("gate_w", stack(np.asarray(inputs["L0_ffn_gate_w"]).T))
    give("cols", np.concatenate([X[a + n + "_b"].reshape(KD, P)
                                 for a in "cs" for n in "kq"]).T)
    give("fi_b", X["fi_b"].reshape(KF, P).T)
    for n in ATTN_ROWS + GELU_ROWS:
        give(n, X[n] if n != "rms" else inputs["L0_ffn_rms_weight"])
    choose = np.zeros((P, 4, 2, 2, P), np.float32)
    choose_mask = np.zeros((P, P), np.float32)
    stack_cols = np.zeros((P, 7), np.float32)
    for half in range(2):
        for place in range(4):
            for d in range(DH):
                feature = 2 * DH * place + DH * half + d
                for what, parts in enumerate(((0, 1, 0), (0, 0, 1))):
                    for t, part in enumerate(parts):
                        choose[feature, place, what, part, 3 * DH * half + DH * t + d] = 1
        stack_cols[3 * DH * half:3 * DH * half + 3 * DH, half] = 1
        stack_cols[ROW_MASK:ROW_MASK + 2, half] = 1
    for t in range(2):
        choose_mask[32 * t, ROW_MASK + t] = 1 / SCALE
        stack_cols[ROW_MASK + t, 6] = 1
        for j in range(G):
            stack_cols[ROW_MAX + G * t + j, 2 + j] = 1
    give("choose", choose)
    give("choose_mask", choose_mask)
    give("stack_cols", stack_cols)
    give("g_xattn", inputs["g_xattn"])
    give("g_ffn", inputs["g_ffn"])
    out = nc.dram_tensor("out", [B, P, QT, D], F32, kind="ExternalOutput").ap()
    build(nc, A, out)
    r = run_bass_kernel_spmd(nc, [arrays], core_ids=[0])
    return r.results[0]["out"].transpose(0, 2, 1, 3).reshape(B, S, D)
```
